# Optimizing a Trainium2 kernel written in Bass

```python
import numpy as np
import jax
import jax.numpy as jnp

def _softmax(x, axis=-1):
    return jax.nn.softmax(x, axis=axis)

def _gelu(x):
    return jax.nn.gelu(x, approximate=True)

def _silu(x):
    return jax.nn.silu(x)

def _sigmoid(x):
    return jax.nn.sigmoid(x)

def _layernorm(x, axis=-1, eps=1e-05):
    m = jnp.mean(x, axis=axis, keepdims=True)
    v = jnp.var(x, axis=axis, keepdims=True)
    return (x - m) / jnp.sqrt(v + eps)

def _scatter_add(tgt, idx, src, axis=0):
    return tgt.at[idx].add(src)

def _segment_sum(src, seg, n):
    return jax.ops.segment_sum(src, seg, n)
kernel_name = 'mk_hybrid_d1_jaxref_r8_d2a28d'

def setup_inputs(seed: int=0):
    np.random.seed(seed)
    _w = jnp.asarray

    def _L0_attn_a_setup():
        import jax, jax.numpy as jnp
        import numpy as np
        B, T, D, H = (2, 256, 128, 16)
        key = jax.random.key(seed)
        ks = jax.random.split(key, 5)
        s = 0.02
        return {'x': jax.random.normal(ks[0], (B, T, D), dtype=jnp.float32), 'W_qkv': jax.random.normal(ks[1], (3 * D, D), dtype=jnp.float32) * s, 'b_qkv': jnp.zeros((3 * D,), dtype=jnp.float32), 'W_out': jax.random.normal(ks[2], (D, D), dtype=jnp.float32) * s, 'b_out': jnp.zeros((D,), dtype=jnp.float32)}
    _L0_attn_a_in = _L0_attn_a_setup()

    def _L0_attn_b_setup():
        import jax, jax.numpy as jnp
        import numpy as np
        import math
        B, S, D = (4, 256, 128)
        H = 16
        HD = D // H
        R = 128
        P = 2 * R
        key = jax.random.key(seed)
        ks = jax.random.split(key, 6)
        x = jax.random.normal(ks[0], (B, S, D), dtype=jnp.float32)
        s = 0.02
        Wk = jax.random.normal(ks[1], (D, D), dtype=jnp.float32) * s
        Wq = jax.random.normal(ks[2], (D, D), dtype=jnp.float32) * s
        Wv = jax.random.normal(ks[3], (D, D), dtype=jnp.float32) * s
        Wp = jax.random.normal(ks[4], (D, D), dtype=jnp.float32) * s
        pos_emb_k = jax.random.normal(ks[5], (P, HD), dtype=jnp.float32) * 0.02
        return {'x': x, 'Wq': Wq, 'Wk': Wk, 'Wv': Wv, 'Wp': Wp, 'pos_emb_k': pos_emb_k}
    _L0_attn_b_in = _L0_attn_b_setup()

    def _L0_ffn_setup():
        import jax, jax.numpy as jnp
        import numpy as np
        E = 32
        H = 128
        I = 64
        G = 8
        TKG = 4
        TOPK = 8
        NSH = 2
        SCALE = 2.5
        key = jax.random.key(seed)
        ks = jax.random.split(key, 10)
        s = 0.02
        return {'hidden_states': jax.random.normal(ks[0], (2, 128, H), jnp.float32), 'gate_w': jax.random.normal(ks[1], (E, H), jnp.float32) * s, 'gate_bias': jax.random.normal(ks[2], (E,), jnp.float32) * s, 'w_gate': jax.random.normal(ks[3], (E, I, H), jnp.float32) * s, 'w_up': jax.random.normal(ks[4], (E, I, H), jnp.float32) * s, 'w_down': jax.random.normal(ks[5], (E, H, I), jnp.float32) * s, 'sh_gate': jax.random.normal(ks[6], (I * NSH, H), jnp.float32) * s, 'sh_up': jax.random.normal(ks[7], (I * NSH, H), jnp.float32) * s, 'sh_down': jax.random.normal(ks[8], (H, I * NSH), jnp.float32) * s}
    _L0_ffn_in = _L0_ffn_setup()
    _d = {'L0_attn_a_x': _L0_attn_a_in['x'], 'L0_attn_a_W_qkv': _L0_attn_a_in['W_qkv'], 'L0_attn_a_b_qkv': _L0_attn_a_in['b_qkv'], 'L0_attn_a_W_out': _L0_attn_a_in['W_out'], 'L0_attn_a_b_out': _L0_attn_a_in['b_out'], 'L0_attn_b_Wq': _L0_attn_b_in['Wq'], 'L0_attn_b_Wk': _L0_attn_b_in['Wk'], 'L0_attn_b_Wv': _L0_attn_b_in['Wv'], 'L0_attn_b_Wp': _L0_attn_b_in['Wp'], 'L0_attn_b_pos_emb_k': _L0_attn_b_in['pos_emb_k'], 'L0_ffn_gate_w': _L0_ffn_in['gate_w'], 'L0_ffn_gate_bias': _L0_ffn_in['gate_bias'], 'L0_ffn_w_gate': _L0_ffn_in['w_gate'], 'L0_ffn_w_up': _L0_ffn_in['w_up'], 'L0_ffn_w_down': _L0_ffn_in['w_down'], 'L0_ffn_sh_gate': _L0_ffn_in['sh_gate'], 'L0_ffn_sh_up': _L0_ffn_in['sh_up'], 'L0_ffn_sh_down': _L0_ffn_in['sh_down']}
    _x0 = _d['L0_attn_a_x']
    _d['L0_attn_a_x'] = jax.random.normal(jax.random.fold_in(jax.random.key(seed), 1), (32, 256, 128), dtype=_x0.dtype)
    del _x0
    return _d

def reference(L0_attn_a_x, L0_attn_a_W_qkv, L0_attn_a_b_qkv, L0_attn_a_W_out, L0_attn_a_b_out, L0_attn_b_Wq, L0_attn_b_Wk, L0_attn_b_Wv, L0_attn_b_Wp, L0_attn_b_pos_emb_k, L0_ffn_gate_w, L0_ffn_gate_bias, L0_ffn_w_gate, L0_ffn_w_up, L0_ffn_w_down, L0_ffn_sh_gate, L0_ffn_sh_up, L0_ffn_sh_down):

    def _L0_attn_a_ref(x, W_qkv, b_qkv, W_out, b_out):
        import jax, jax.numpy as jnp
        import numpy as np
        B, T, D, H = (2, 256, 128, 16)
        Bx, Tx, Dx = x.shape
        Hh = H
        hd = Dx // Hh
        topk = max(1, int(Tx * 0.3))
        scale = Dx ** (-0.5)
        qkv = x @ W_qkv.T + b_qkv
        qkv = qkv.reshape(Bx, Tx, 3, Hh, hd)
        q = jnp.transpose(qkv[:, :, 0], (0, 2, 1, 3))
        k = jnp.transpose(qkv[:, :, 1], (0, 2, 1, 3))
        v = jnp.transpose(qkv[:, :, 2], (0, 2, 1, 3))
        scores = jnp.einsum('bhid,bhjd->bhij', q, k) * scale
        topk_scores, indices = jax.lax.top_k(scores, topk)
        bi = jnp.arange(Bx)[:, None, None, None]
        hi = jnp.arange(Hh)[None, :, None, None]
        ti = jnp.arange(Tx)[None, None, :, None]
        masked = jnp.full_like(scores, -jnp.inf)
        masked = masked.at[bi, hi, ti, indices].set(topk_scores)
        attn = jax.nn.softmax(masked, axis=-1)
        out = jnp.einsum('bhij,bhjd->bhid', attn, v)
        out = jnp.transpose(out, (0, 2, 1, 3)).reshape(Bx, Tx, Dx)
        return out @ W_out.T + b_out

    def _L0_attn_b_ref(x, Wq, Wk, Wv, Wp, pos_emb_k):
        import jax, jax.numpy as jnp
        import numpy as np
        import math
        B, S, D = (4, 256, 128)
        H = 16
        HD = D // H
        R = 128
        P = 2 * R
        batch, ctx, emb = x.shape

        def heads(w):
            return (x @ w.T).reshape(batch, ctx, H, HD).transpose(0, 2, 1, 3)
        q, k, v = (heads(Wq), heads(Wk), heads(Wv))
        att_rel_pos = jnp.einsum('bhsd,pd->bhsp', q, pos_emb_k)
        i = jnp.arange(ctx)
        att_idxs = jnp.clip(i[None, :] - i[:, None], -R, R - 1) % P
        att_pos = jnp.take_along_axis(att_rel_pos, att_idxs[None, None, :, :].astype(jnp.int32), axis=3)
        attn_val = jnp.einsum('bhsd,bhtd->bhst', q, k) + att_pos
        attn_scale = 1.0 / math.sqrt(HD)
        att = jax.nn.softmax((attn_val + att_pos) * attn_scale, axis=-1)
        y = jnp.einsum('bhst,bhtd->bhsd', att, v)
        y = y.transpose(0, 2, 1, 3).reshape(batch, ctx, emb)
        return y @ Wp.T

    def _L0_ffn_ref(hidden_states, gate_w, gate_bias, w_gate, w_up, w_down, sh_gate, sh_up, sh_down):
        import jax, jax.numpy as jnp
        import numpy as np
        E = 32
        H = 128
        I = 64
        G = 8
        TKG = 4
        TOPK = 8
        NSH = 2
        SCALE = 2.5
        B, S, Hd = hidden_states.shape
        h = hidden_states.reshape(-1, Hd)
        logits = h.astype(jnp.float32) @ gate_w.T
        scores = jax.nn.sigmoid(logits)
        sc = scores + gate_bias
        grp = sc.reshape(-1, G, E // G)
        group_scores = jax.lax.top_k(grp, 2)[0].sum(-1)
        gidx = jax.lax.top_k(group_scores, TKG)[1]
        gmask = jnp.sum(jax.nn.one_hot(gidx, G, dtype=sc.dtype), axis=1)
        smask = jnp.repeat(gmask, E // G, axis=1)
        masked = jnp.where(smask > 0, sc, jnp.zeros_like(sc))
        tki = jax.lax.top_k(masked, TOPK)[1]
        tkw = jnp.take_along_axis(scores, tki, axis=1)
        tkw = tkw / (tkw.sum(-1, keepdims=True) + 1e-20)
        tkw = tkw * SCALE
        combine = (jax.nn.one_hot(tki, E, dtype=tkw.dtype) * tkw[..., None]).sum(1)
        g = jax.nn.silu(jnp.einsum('th,eih->tei', h, w_gate))
        u = jnp.einsum('th,eih->tei', h, w_up)
        routed = jnp.einsum('tei,ehi->th', g * u * combine[:, :, None], w_down)
        sg = jax.nn.silu(h @ sh_gate.T)
        shared = sg * (h @ sh_up.T) @ sh_down.T
        return (routed + shared).reshape(B, S, Hd)
    x = L0_attn_a_x
    x = x + _L0_attn_a_ref(_layernorm(x, axis=-1), L0_attn_a_W_qkv, L0_attn_a_b_qkv, L0_attn_a_W_out, L0_attn_a_b_out)
    x = x + _L0_ffn_ref(_layernorm(x, axis=-1), L0_ffn_gate_w, L0_ffn_gate_bias, L0_ffn_w_gate, L0_ffn_w_up, L0_ffn_w_down, L0_ffn_sh_gate, L0_ffn_sh_up, L0_ffn_sh_down)
    x = x + _L0_attn_b_ref(_layernorm(x, axis=-1), L0_attn_b_Wq, L0_attn_b_Wk, L0_attn_b_Wv, L0_attn_b_Wp, L0_attn_b_pos_emb_k)
    x = x + _L0_ffn_ref(_layernorm(x, axis=-1), L0_ffn_gate_w, L0_ffn_gate_bias, L0_ffn_w_gate, L0_ffn_w_up, L0_ffn_w_down, L0_ffn_sh_gate, L0_ffn_sh_up, L0_ffn_sh_down)
    return x

_drawn_inputs = setup_inputs


def setup_inputs(seed=0):
    import zlib

    import numpy as np

    out = dict(_drawn_inputs(seed))
    spreads = {'L0_attn_a_b_qkv': (0.0, 0.367), 'L0_attn_a_b_out': (0.0, 0.1)}
    factors = {'L0_attn_a_W_qkv': 7.171,
     'L0_attn_b_Wq': 8.0,
     'L0_attn_b_Wk': 8.0,
     'L0_attn_b_Wv': 8.0,
     'L0_attn_b_Wp': 8.0,
     'L0_attn_b_pos_emb_k': 8.0,
     'L0_ffn_gate_w': 8.0,
     'L0_ffn_gate_bias': 8.0,
     'L0_ffn_w_gate': 7.807,
     'L0_ffn_w_up': 7.763,
     'L0_ffn_w_down': 7.771,
     'L0_ffn_sh_gate': 4.937,
     'L0_ffn_sh_up': 4.869,
     'L0_ffn_sh_down': 4.911}
    for name, (base, spread) in spreads.items():
        noise = np.random.default_rng([zlib.crc32(name.encode()), seed]).standard_normal(out[name].shape)
        drawn = base * np.exp(spread * noise) if base else spread * noise
        out[name] = jnp.asarray(drawn.astype(out[name].dtype))
    for name, factor in factors.items():
        out[name] = (out[name] * factor).astype(out[name].dtype)
    return out
```

```python
import concourse.bass as bass
from concourse import mybir
from contextlib import ExitStack

BATCH, T, D = 32, 256, 128
P = 128
HALVES = T // P
H = 16
HD = D // H
TOPK = int(T * 0.3)
NE, NI = 32, 64
EB = NE * NI // P
NBLK = EB + 1
NG, GSZ = 8, NE // 8
REL = 128
PAD32 = 32
CH = H // 4
J = 16
A = T // J
HG = 8
VW = HD + 1
EPS = 1e-5
SCALE_A = float(D) ** -0.5
SCALE_B = float(HD) ** -0.5
ROUTED_SCALE = 2.5
GONE = -3.0e38
GONE_BELOW = -2.9e38


class Own:

    def __init__(self, eng, sem):
        self.eng, self.sem, self.n = eng, sem, 0

    def mark(self, ins):
        ins.then_inc(self.sem, 1)
        self.n += 1
        return self.n

    def need(self, n):
        self.eng.wait_ge(self.sem, n)

    def link(self, ins):
        self.need(self.mark(ins))

    def end(self):
        self.need(self.n)
        self.eng.sem_clear(self.sem)
        self.n = 0


def build(nc, x, W_qkv, b_qkv, W_out, b_out, Wq, Wk, Wv, Wp, pos, gate_w, gate_bias,
          w_gate, w_up, w_down, sh_gate, sh_up, sh_down, out):
    f32 = mybir.dt.float32
    ALU = mybir.AluOpType
    ACT = mybir.ActivationFunctionType
    AX = mybir.AxisListType.X
    ctx = ExitStack()
    with ctx:
        def sb(name, shape, dt=f32):
            return ctx.enter_context(nc.sbuf_tensor(name, shape, dt))

        def sem(name):
            return ctx.enter_context(nc.semaphore(name))

        bank = [ctx.enter_context(nc.psum_tensor(f"bank{i}", [P, 512], f32)) for i in range(8)]
        misc = bank[6:8]

        xres = sb("xres", [P, BATCH * HALVES, D])
        ident = sb("ident", [P, P])
        ones1 = sb("ones1", [1, P])
        wqkT = sb("wqkT", [P, 2, CH, P])
        bqk = sb("bqk", [P, 2, CH])
        wvT = sb("wvT", [P, D])
        bv = sb("bv", [1, D])
        woT = sb("woT", [P, D])
        bo = sb("bo", [1, D])
        wqT = sb("wqT", [P, D])
        wkT = sb("wkT", [P, D])
        wvbT = sb("wvbT", [P, D])
        wpT = sb("wpT", [P, D])
        wqrep = sb("wqrep", [P, H, P])
        px = sb("px", [P, T + (A - 1) * J])
        mask_h16 = sb("mask_h16", [P, H])
        mask_h8 = sb("mask_h8", [P, HG])
        gwT = sb("gwT", [P, NE])
        gbias = sb("gbias", [P, NE])
        wgT = sb("wgT", [P, NBLK, P])
        wuT = sb("wuT", [P, NBLK, P])
        wdT = sb("wdT", [P, NBLK, P])
        sel = sb("sel", [NE, EB, P])
        half_pow = sb("half_pow", [P, HALVES])
        eps_t = sb("eps_t", [P, HALVES])

        stats = sb("stats", [P, HALVES, 6])
        mv = sb("mv", [P, HALVES, 2])
        vareps = sb("vareps", [P, HALVES])
        rstd = sb("rstd", [P, HALVES])
        xn = sb("xn", [P, HALVES, D])
        xT = sb("xT", [P, T])
        q4 = sb("q4", [P, CH, T])
        k4 = sb("k4", [P, CH, T])
        vaug = sb("vaug", [P, HALVES, H, VW])
        mx = sb("mx", [P, HALVES, 8])
        mlast = sb("mlast", [P, HALVES, 8])
        nb = sb("nb", [P, 2, HALVES])
        work = sb("work", [P, HALVES, T])
        ex = sb("ex", [P, 2, HALVES, T])
        prob = sb("prob", [P, 2, HALVES, T])
        pT = sb("pT", [P, 2, HALVES, T])
        rinv = sb("rinv", [P, HALVES * H])
        onrm = sb("onrm", [P, HALVES, D])
        oT = sb("oT", [P, T])
        stage = sb("stage", [P, 3, EB, P])

        def transposes_of_weights():
            jobs = []
            for k in range(EB):
                jobs.append((stage[:, 0, k, :], wgT[:, k, :]))
                jobs.append((stage[:, 1, k, :], wuT[:, k, :]))
                jobs.append((stage[:, 2, k, :], wdT[:, k, :]))
            return jobs

        nat = sb("nat", [P, 11, P])
        gnat = sb("gnat", [NE, D])
        pnat = sb("pnat", [P, 2, HD])
        pext = sb("pext", [HD, 2 * T + J])

        s_ones = sem("s_ones")
        s_const = sem("s_const")
        s_w = sem("s_w")
        s_x = sem("s_x")
        s_tr = sem("s_tr")
        s_trc = sem("s_trc")
        s_rep = sem("s_rep")
        s_pext = sem("s_pext")
        s_px = sem("s_px")
        s_setv = sem("s_setv")

        b_cgd = b_qkv.rearrange("(w c g d) -> w g d c", w=3, c=CH, g=4)
        x_dram = x.rearrange("b (h p) d -> p (b h) d", p=P)
        out_dram = out.rearrange("b (h p) d -> p (b h) d", p=P)

        NWT = 3 * EB + 11
        with nc.Block() as block:
            @block.sync
            def _(sp):
                sp.wait_ge(s_setv, 1)
                for i, w in enumerate((W_qkv[0:P, :], W_qkv[P:2 * P, :], W_qkv[2 * P:3 * P, :], W_out,
                                       Wq, Wk, Wv, Wp, sh_gate, sh_up, sh_down)):
                    sp.dma_start(nat[:, i, :], w).then_inc(s_w, 16)
                sp.dma_start(gnat[:, :], gate_w).then_inc(s_w, 16)
                sp.dma_start(pnat[:, :, :], pos.rearrange("(k p) d -> p k d", p=P)).then_inc(s_w, 16)
                sp.dma_start(bv[:, :], b_qkv[2 * D:3 * D].rearrange("(a n) -> a n", a=1)).then_inc(s_w, 16)
                sp.dma_start(bo[:, :], b_out.rearrange("(a n) -> a n", a=1)).then_inc(s_w, 16)
                sp.dma_start(gbias[:, :], gate_bias.rearrange("(a n) -> a n", a=1).to_broadcast([P, NE])).then_inc(s_w, 16)
                for w in range(2):
                    for g in range(4):
                        sp.dma_start(bqk[PAD32 * g:PAD32 * g + HD, w, :], b_cgd[w, g],
                                     allow_slow_non_contiguous=True).then_inc(s_w, 16)
                sp.dma_start(stage[:, 0], w_gate.rearrange("e i h -> (e i) h").rearrange("(k p) h -> p k h", p=P)).then_inc(s_w, 16)
                sp.dma_start(stage[:, 1], w_up.rearrange("e i h -> (e i) h").rearrange("(k p) h -> p k h", p=P)).then_inc(s_w, 16)
                sp.dma_start(stage[:, 2].rearrange("h k (e i) -> h (k e) i", e=2), w_down.rearrange("e h i -> h e i")).then_inc(s_w, 16)
                for c in range(4):
                    n = BATCH * HALVES // 4
                    sp.dma_start(xres[:, c * n:(c + 1) * n, :], x_dram[:, c * n:(c + 1) * n, :]).then_inc(s_x, 16)
                sp.wait_ge(s_pext, 1)
                for j in range(J):
                    sp.dma_start(px[HD * j:HD * j + HD, :], pext[:, J - 1 - j:J - 1 - j + T + (A - 1) * J]).then_inc(s_px, 16)
                sp.wait_ge(s_px, 16 * J)
                sp.wait_ge(s_x, 16 * 4)

            @block.gpsimd
            def _(pool):
                one = [
                    pool.memset(ident[:, :], 0.0), pool.memset(mask_h16[:, :], 1.0),
                    pool.memset(sel[:, :, :], 1.0), pool.memset(half_pow[:, :], -0.5), pool.memset(eps_t[:, :], EPS),
                    pool.memset(ones1[:, :], 1.0),
                ]
                one[-1].then_inc(s_ones, 1)
                pool.wait_ge(s_ones, 1)
                pool.affine_select(out=ident[:, :], in_=ident[:, :], compare_op=ALU.not_equal, fill=1.0, base=0,
                                   pattern=[[-1, P]], channel_multiplier=1)
                pool.affine_select(out=mask_h16[:, :], in_=mask_h16[:, :], compare_op=ALU.is_ge, fill=0.0, base=0,
                                   pattern=[[-HD, H]], channel_multiplier=1)
                pool.affine_select(out=sel[:, :, :], in_=sel[:, :, :], compare_op=ALU.is_equal, fill=0.0, base=0,
                                   pattern=[[-2, EB], [-1, 2], [0, NI]], channel_multiplier=1).then_inc(s_ones, 1)
                pool.wait_ge(s_ones, 2)
                pool.affine_select(out=mask_h16[:, :], in_=mask_h16[:, :], compare_op=ALU.is_ge, fill=0.0, base=HD - 1,
                                   pattern=[[HD, H]], channel_multiplier=-1).then_inc(s_const, 1)

            @block.tensor
            def _(pe):
                pe.wait_ge(s_const, 1)
                pe.wait_ge(s_w, 16 * 27)
                jobs = ([nat[:, i, :] for i in range(11)]
                        + [stage[:, w, k, :] for w in range(3) for k in range(EB)])
                for n, src in enumerate(jobs):
                    if n % 4 == 0 and n >= 16:
                        pe.wait_ge(s_trc, n // 4 - 3)
                    last = nc.tensor.transpose(bank[(n // 4) % 4][:, (n % 4) * P:(n % 4 + 1) * P], src, ident[:, :])
                    if n % 4 == 3 or n == len(jobs) - 1:
                        last.then_inc(s_tr, 1)
                nc.tensor.transpose(bank[4][:, 0:NE], gnat[:, :], ident[0:NE, 0:NE])
                for k in range(2):
                    last = nc.tensor.transpose(bank[4][0:HD, 64 + k * P:64 + (k + 1) * P], pnat[:, k, :], ident[:, :])
                last.then_inc(s_tr, 1)

            @block.vector
            def _(dve):
                own = Own(dve, sem("set_own"))
                nc.vector.memset(bqk[:, :, :], 0.0).then_inc(s_setv, 1)
                nc.vector.memset(vaug[:, :, :, :], 1.0)
                own.link(nc.vector.memset(wqkT[:, :, :, :], 0.0))
                dst = []
                NJ = 11 + 3 * EB
                flat = [wgT, wuT, wdT]

                def put(n, src):
                    if n < 2:
                        o = wqkT[:, n, :, :].rearrange("p c (g e) -> p (c g) e", g=4)[:, :, 0:HD]
                        return nc.vector.tensor_copy(o, src.rearrange("p (h d) -> p h d", d=HD))
                    o = {2: wvT[:, :], 3: woT[:, :], 4: wqT[:, :], 5: wkT[:, :], 6: wvbT[:, :], 7: wpT[:, :],
                         8: wgT[:, EB, :], 9: wuT[:, EB, :], 10: wdT[:, EB, :]}.get(n)
                    if o is None:
                        o = flat[(n - 11) // EB][:, (n - 11) % EB, :]
                    return nc.vector.tensor_copy(o, src)

                for n in range(NJ):
                    if n % 4 == 0:
                        dve.wait_ge(s_tr, n // 4 + 1)
                    last = put(n, bank[(n // 4) % 4][:, (n % 4) * P:(n % 4 + 1) * P])
                    if n % 4 == 3 or n == NJ - 1:
                        last.then_inc(s_trc, 1)
                dve.wait_ge(s_tr, (NJ + 3) // 4 + 1)
                nc.vector.tensor_copy(gwT[:, :], bank[4][:, 0:NE])
                mid = T - J + (J - 1) - REL
                own.mark(nc.vector.tensor_scalar(pext[:, mid:mid + REL], bank[4][0:HD, 64 + P:64 + 2 * P], 2.0, None, ALU.mult))
                own.link(nc.vector.tensor_scalar(pext[:, mid + REL:mid + 2 * REL], bank[4][0:HD, 64:64 + P], 2.0, None, ALU.mult))
                nc.vector.tensor_copy(pext[:, 0:mid], pext[:, mid:mid + 1].to_broadcast([HD, mid]))
                tail = 2 * T + J - mid - 2 * REL
                nc.vector.tensor_copy(pext[:, mid + 2 * REL:], pext[:, mid + 2 * REL - 1:mid + 2 * REL].to_broadcast([HD, tail])).then_inc(s_pext, 1)
                dve.wait_ge(s_const, 1)
                nc.vector.tensor_tensor(mask_h8[:, :], mask_h16[:, 0:HG], mask_h16[:, HG:H], ALU.add)
                dve.wait_ge(s_trc, (NJ + 3) // 4)
                nc.vector.tensor_copy(wqrep[:, :, :].rearrange("p h (j d) -> p h j d", d=HD),
                                      wqT[:, :].rearrange("p (h d) -> p h d", d=HD).unsqueeze(2).to_broadcast([P, H, J, HD]))

        def norm_dve(dve, own, b, s):
            rows = xres[:, bass.ds(b * HALVES, HALVES), :]
            for h in range(HALVES):
                n = own.mark(nc.vector.bn_stats(stats[:, h, :], xres[:, bass.ds(b * HALVES + h, 1), :].rearrange("p a d -> p (a d)")))
            own.need(n)
            for h in range(HALVES):
                n = nc.vector.bn_aggr(mv[:, h, :], stats[:, h, :])
            n.then_inc(s["mv"], 1)
            dve.wait_ge(s["rstd"], b + 1)
            for h in range(HALVES):
                n = nc.vector.tensor_scalar(xn[:, h, :], xres[:, bass.ds(b * HALVES + h, 1), :].rearrange("p a d -> p (a d)"),
                                            mv[:, h, 0:1], rstd[:, h:h + 1], ALU.subtract, ALU.mult)
            n.then_inc(s["xn"], 1)

        def norm_pool(pool, own, b, s):
            pool.wait_ge(s["mv"], b + 1)
            own.link(pool.tensor_tensor(vareps[:, :], mv[:, :, 1], eps_t[:, :], ALU.add))
            pool.tensor_tensor(rstd[:, :], vareps[:, :], half_pow[:, :], ALU.pow).then_inc(s["rstd"], 1)
            own.end()

        def sems(tag, names):
            return {n: sem(f"{tag}_{n}") for n in names.split()}

        s = sems("a", "mv rstd xn xt misc yused scores gate gate2 nmax sact p pused pt pv oready on y ex own pown")
        S = bank[0:3]
        PT = bank[3:5]
        O = bank[5]
        o_all = O[:, 0:HALVES * H * VW].rearrange("p (n w) -> p n w", w=VW)

        def mcol(n):
            return misc[n % 2]

        with nc.Block() as block:
            @block.gpsimd
            def _(pool):
                own = Own(pool, s["pown"])
                with pool.Fori(0, BATCH) as b:
                    norm_pool(pool, own, b, s)

            @block.tensor
            def _(pe):
                pe.sem_inc(s["pv"], 2)
                pe.sem_inc(s["pused"], 2)
                with pe.Fori(0, BATCH) as b:
                    MISC = 7
                    pe.wait_ge(s["xn"], b + 1)
                    for h in range(HALVES):
                        last = nc.tensor.transpose(mcol(0)[:, h * P:(h + 1) * P], xn[:, h, :], ident[:, :])
                    last.then_inc(s["xt"], 1)
                    pe.wait_ge(s["yused"], b + 1)
                    pe.wait_ge(s["misc"], MISC * b + 1)
                    for m in range(1, 5):
                        if m >= 2:
                            pe.wait_ge(s["misc"], MISC * b + m - 1)
                        for i in range(2):
                            last = nc.tensor.matmul(mcol(m)[:, i * T:(i + 1) * T], wqkT[:, (m - 1) // 2, 2 * ((m - 1) % 2) + i, :],
                                                    xT[:, :], start=True, stop=True)
                        last.then_inc(s["xt"], 1)
                    pe.wait_ge(s["misc"], MISC * b + 4)
                    for h in range(HALVES):
                        nc.tensor.matmul(mcol(5)[:, h * P:(h + 1) * P], xT[:, h * P:(h + 1) * P], wvT[:, :], start=True, stop=False)
                        last = nc.tensor.matmul(mcol(5)[:, h * P:(h + 1) * P], ones1[:, :], bv[:, :], start=False, stop=True)
                    last.then_inc(s["xt"], 1)
                    pe.wait_ge(s["misc"], MISC * b + 5)

                    def scores(h):
                        pe.wait_ge(s["sact"], H * b + h + 1)
                        r = slice(PAD32 * (h % 4), PAD32 * (h % 4) + HD)
                        for i in range(HALVES):
                            last = nc.tensor.matmul(S[h % 3][:, i * T:(i + 1) * T], q4[r, h // 4, i * P:(i + 1) * P],
                                                    k4[r, h // 4, :], start=True, stop=True)
                        last.then_inc(s["scores"], 1)

                    def weigh(h):
                        pe.wait_ge(s["pt"], H * b + h + 1)
                        for i in range(HALVES):
                            for t in range(HALVES):
                                o = (i * H + h) * VW
                                last = nc.tensor.matmul(O[:, o:o + VW], pT[:, h % 2, t, i * P:(i + 1) * P], vaug[:, t, h, :],
                                                        start=(t == 0), stop=(t == HALVES - 1))
                        last.then_inc(s["pv"], 1)

                    for h in range(3):
                        scores(h)
                    for h in range(H):
                        pe.wait_ge(s["p"], H * b + h + 1)
                        for i in range(HALVES):
                            for t in range(HALVES):
                                last = nc.tensor.transpose(PT[h % 2][:, t * T + i * P:t * T + (i + 1) * P],
                                                           prob[:, h % 2, i, t * P:(t + 1) * P], ident[:, :])
                        last.then_inc(s["pused"], 1)
                        if h + 3 < H:
                            scores(h + 3)
                        if h == 0:
                            pe.wait_ge(s["misc"], MISC * b + 6)
                        if h >= 1:
                            weigh(h - 1)
                    weigh(H - 1)
                    pe.wait_ge(s["on"], b + 1)
                    for i in range(HALVES):
                        last = nc.tensor.transpose(mcol(6)[:, i * P:(i + 1) * P], onrm[:, i, :], ident[:, :])
                    last.then_inc(s["xt"], 1)
                    pe.wait_ge(s["misc"], MISC * b + 7)
                    for i in range(HALVES):
                        nc.tensor.matmul(mcol(7)[:, i * P:(i + 1) * P], oT[:, i * P:(i + 1) * P], woT[:, :], start=True, stop=False)
                        last = nc.tensor.matmul(mcol(7)[:, i * P:(i + 1) * P], ones1[:, :], bo[:, :], start=False, stop=True)
                    last.then_inc(s["y"], 1)

            @block.scalar
            def _(act):
                act.sem_inc(s["sact"], 3)
                with act.Fori(0, BATCH) as b:
                    act.wait_ge(s["xt"], 7 * b + 1)
                    nc.scalar.copy(xT[:, :], mcol(0)[:, 0:T]).then_inc(s["misc"], 1)
                    for m in range(1, 5):
                        act.wait_ge(s["xt"], 7 * b + m + 1)
                        dst = (q4, k4)[(m - 1) // 2]
                        for i in range(2):
                            c = 2 * ((m - 1) % 2) + i
                            last = nc.scalar.activation(dst[:, c, :], mcol(m)[:, i * T:(i + 1) * T], ACT.Identity,
                                                        bias=bqk[:, (m - 1) // 2, c:c + 1])
                        last.then_inc(s["misc"], 1)
                    act.wait_ge(s["xt"], 7 * b + 6)
                    nc.scalar.copy(vaug[:, :, :, 0:HD].rearrange("p t h d -> p (t h) d"),
                                   mcol(5)[:, 0:T].rearrange("p (n d) -> p n d", d=HD)).then_inc(s["misc"], 1)

                    def copy_pt(h):
                        act.wait_ge(s["pused"], H * b + h + 3)
                        act.wait_ge(s["pv"], H * b + h + 1)
                        nc.scalar.copy(pT[:, h % 2, :, :].rearrange("p t i -> p (t i)"), PT[h % 2][:, :]).then_inc(s["pt"], 1)

                    for h in range(H):
                        act.wait_ge(s["nmax"], H * b + h + 1)
                        for i in range(HALVES):
                            last = nc.scalar.activation(ex[:, h % 2, i, :], S[h % 3][:, i * T:(i + 1) * T], ACT.Exp,
                                                        bias=nb[:, h % 2, i:i + 1], scale=SCALE_A)
                        last.then_inc(s["sact"], 1)
                        if h >= 1:
                            copy_pt(h - 1)
                    copy_pt(H - 1)
                    act.wait_ge(s["xt"], 7 * b + 7)
                    nc.scalar.copy(oT[:, :], mcol(6)[:, 0:T]).then_inc(s["misc"], 1)

            @block.vector
            def _(dve):
                own = Own(dve, s["own"])
                dve.sem_inc(s["yused"], 1)
                with dve.Fori(0, BATCH) as b:
                    norm_dve(dve, own, b, s)
                    for h in range(H):
                        dve.wait_ge(s["scores"], H * b + h + 1)
                        dve.sem_inc(s["gate"], 1)
                        sc = [S[h % 3][:, i * T:(i + 1) * T] for i in range(HALVES)]
                        full, rest = TOPK // 8, TOPK % 8
                        for i in range(HALVES):
                            n = own.mark(nc.vector.max(mx[:, i, :], sc[i]))
                        own.need(n)
                        for r in range(full):
                            for i in range(HALVES):
                                if r:
                                    own.need(n - 1 + i)
                                m = own.mark(nc.vector.match_replace(work[:, i, :], mx[:, i, :], work[:, i, :] if r else sc[i], GONE))
                            n = m
                            if r == 0:
                                own.need(n)
                                nc.vector.tensor_scalar(nb[:, h % 2, :], mx[:, :, 0], -SCALE_A, None, ALU.mult).then_inc(s["nmax"], 1)
                                dve.wait_ge(s["nmax"], H * b + h + 1)
                                dve.sem_inc(s["gate"], 1)
                            for i in range(HALVES):
                                if r:
                                    own.need(n - 1 + i)
                                dst = mx if r < full - 1 else mlast
                                k = own.mark(nc.vector.max(dst[:, i, :], work[:, i, :]))
                            n = k
                        own.need(n)
                        own.link(nc.vector.memset(mlast[:, :, rest:8], GONE))
                        for i in range(HALVES):
                            n = own.mark(nc.vector.match_replace(work[:, i, :], mlast[:, i, :], work[:, i, :], GONE))
                        own.need(n)
                        dve.wait_ge(s["sact"], H * b + h + 4)
                        dve.wait_ge(s["pused"], H * b + h + 1)
                        last = nc.vector.scalar_tensor_tensor(prob[:, h % 2, :, :], work[:, :, :], GONE_BELOW, ex[:, h % 2, :, :],
                                                              ALU.is_le, ALU.mult)
                        last.then_inc(s["p"], 1)
                    dve.wait_ge(s["pv"], H * b + H + 2)
                    own.link(nc.vector.reciprocal(rinv[:, :], o_all[:, :, HD]))
                    nc.vector.tensor_tensor(onrm[:, :, :].rearrange("p i (h d) -> p (i h) d", d=HD), o_all[:, :, 0:HD],
                                            rinv[:, :].unsqueeze(2).to_broadcast([P, HALVES * H, HD]), ALU.mult).then_inc(s["on"], 1)
                    dve.wait_ge(s["y"], b + 1)
                    rows = xres[:, bass.ds(b * HALVES, HALVES), :]
                    nc.vector.tensor_tensor(rows, rows, mcol(7)[:, 0:T].rearrange("p (i d) -> p i d", i=HALVES), ALU.add).then_inc(s["yused"], 1)
                    dve.wait_ge(s["yused"], b + 2)
                    dve.sem_inc(s["gate2"], 1)
                    own.end()

        hid = sb("hid", [P, 2, T])
        th = sb("th", [P, 2, T])
        g_s = sb("g_s", [P, 2, T])
        g_m = sb("g_m", [P, 2, T])
        sg = sb("sg", [P, HALVES, NE])
        sc_ = sb("sc_", [P, HALVES, NE])
        hi = sb("hi", [P, HALVES * NG, 2])
        lo = sb("lo", [P, HALVES * NG, 2])
        m1 = sb("m1", [P, HALVES * NG])
        m2 = sb("m2", [P, HALVES * NG])
        m3 = sb("m3", [P, HALVES * NG])
        gsc = sb("gsc", [P, HALVES, 2 * NG])
        g8 = sb("g8", [P, HALVES, 8])
        gr = sb("gr", [P, HALVES, 2 * NG])
        gm = sb("gm", [P, HALVES, NG])
        comb = sb("comb", [P, HALVES, NE])
        wsum = sb("wsum", [P, HALVES])
        combT = sb("combT", [NE, T])

        def experts(tag):
            s = sems(tag, "mv rstd xn tr cp lg th gs gate comb gu hid yused own pown gfree gate2")
            GU = bank[0:3]
            CB = [bank[3], bank[7]]
            Y = bank[4:6]
            with nc.Block() as block:
                @block.gpsimd
                def _(pool):
                    own = Own(pool, s["pown"])
                    with pool.Fori(0, BATCH) as b:
                        norm_pool(pool, own, b, s)

                @block.tensor
                def _(pe):
                    with pe.Fori(0, BATCH) as b:
                        pe.wait_ge(s["xn"], b + 1)
                        for h in range(HALVES):
                            last = nc.tensor.transpose(misc[0][:, h * P:(h + 1) * P], xn[:, h, :], ident[:, :])
                        last.then_inc(s["tr"], 1)
                        pe.wait_ge(s["cp"], 2 * b + 1)
                        for h in range(HALVES):
                            last = nc.tensor.matmul(misc[0][:, h * NE:(h + 1) * NE], xT[:, h * P:(h + 1) * P], gwT[:, :], start=True, stop=True)
                        last.then_inc(s["tr"], 1)

                        def up(e):
                            pe.wait_ge(s["gfree"], NBLK * b + e + 1)
                            g = GU[e % 3]
                            nc.tensor.matmul(g[:, 0:T], wgT[:, e, :], xT[:, :], start=True, stop=True)
                            last = nc.tensor.matmul(g[:, T:2 * T], wuT[:, e, :], xT[:, :], start=True, stop=True)
                            last.then_inc(s["gu"], 1)

                        def spread(e):
                            c = CB[e % 2][:, 0:T]
                            if e < EB:
                                nc.tensor.matmul(c, sel[:, e, :], combT[:, :], start=True, stop=True).then_inc(s["gate"], 1)

                        def down(e):
                            pe.wait_ge(s["hid"], NBLK * b + e + 1)
                            for h in range(HALVES):
                                last = nc.tensor.matmul(Y[h][:, 0:D], hid[:, e % 2, h * P:(h + 1) * P], wdT[:, e, :],
                                                        start=(e == 0), stop=(e == NBLK - 1))
                            last.then_inc(s["lg"], 1)

                        up(0)
                        up(1)
                        pe.wait_ge(s["comb"], b + 1)
                        for h in range(HALVES):
                            last = nc.tensor.transpose(misc[0][0:NE, h * P:(h + 1) * P], comb[:, h, :], ident[:, :])
                        last.then_inc(s["tr"], 1)
                        pe.wait_ge(s["cp"], 2 * b + 2)
                        pe.wait_ge(s["yused"], b + 1)
                        spread(0)
                        spread(1)
                        for e in range(NBLK):
                            if e + 2 < NBLK:
                                up(e + 2)
                            down(e)
                            if e + 2 < NBLK:
                                spread(e + 2)

                @block.scalar
                def _(act):
                    with act.Fori(0, BATCH) as b:
                        act.wait_ge(s["tr"], 3 * b + 1)
                        nc.scalar.copy(xT[:, :], misc[0][:, 0:T]).then_inc(s["cp"], 1)
                        act.wait_ge(s["tr"], 3 * b + 2)
                        nc.scalar.activation(sg[:, :, :].rearrange("p h e -> p (h e)"), misc[0][:, 0:HALVES * NE], ACT.Tanh, scale=0.5).then_inc(s["gs"], 1)

                        def tanh(e):
                            act.wait_ge(s["gu"], NBLK * b + e + 1)
                            act.wait_ge(s["gfree"], NBLK * b + e + 2)
                            nc.scalar.activation(th[:, e % 2, :], GU[e % 3][:, 0:T], ACT.Tanh, scale=0.5).then_inc(s["th"], 1)

                        tanh(0)
                        act.wait_ge(s["tr"], 3 * b + 3)
                        nc.scalar.copy(combT[:, :], misc[0][0:NE, 0:T]).then_inc(s["cp"], 1)
                        for e in range(1, NBLK):
                            tanh(e)

                @block.vector
                def _(dve):
                    own = Own(dve, s["own"])
                    dve.sem_inc(s["yused"], 1)
                    dve.sem_inc(s["gfree"], 3)
                    nc.vector.memset(gsc[:, :, :], GONE)
                    with dve.Fori(0, BATCH) as b:
                        V = nc.vector
                        norm_dve(dve, own, b, s)
                        dve.wait_ge(s["gs"], b + 1)
                        own.link(V.tensor_scalar(sg[:, :, :], sg[:, :, :], 0.5, 0.5, ALU.mult, ALU.add))
                        own.link(V.tensor_tensor(sc_[:, :, :], sg[:, :, :], gbias[:, :].unsqueeze(1).to_broadcast([P, HALVES, NE]), ALU.add))
                        q = sc_[:, :, :].rearrange("p h (g k two) -> p (h g) k two", k=2, two=2)
                        V.tensor_tensor(hi[:, :, :], q[:, :, :, 0], q[:, :, :, 1], ALU.max)
                        own.link(V.tensor_tensor(lo[:, :, :], q[:, :, :, 0], q[:, :, :, 1], ALU.min))
                        V.tensor_tensor(m1[:, :], hi[:, :, 0], hi[:, :, 1], ALU.max)
                        V.tensor_tensor(m2[:, :], hi[:, :, 0], hi[:, :, 1], ALU.min)
                        own.link(V.tensor_tensor(m3[:, :], lo[:, :, 0], lo[:, :, 1], ALU.max))
                        own.link(V.tensor_tensor(m2[:, :], m2[:, :], m3[:, :], ALU.max))
                        own.link(V.tensor_tensor(gsc[:, :, 0:NG], m1[:, :].rearrange("p (h g) -> p h g", h=HALVES),
                                                 m2[:, :].rearrange("p (h g) -> p h g", h=HALVES), ALU.add))
                        for h in range(HALVES):
                            n = own.mark(V.max(g8[:, h, :], gsc[:, h, :]))
                        own.need(n)
                        own.link(V.memset(g8[:, :, 4:8], GONE))
                        for h in range(HALVES):
                            n = own.mark(V.match_replace(gr[:, h, :], g8[:, h, :], gsc[:, h, :], GONE))
                        own.need(n)
                        own.link(V.tensor_scalar(gm[:, :, :], gr[:, :, 0:NG], GONE_BELOW, None, ALU.is_le))
                        own.link(V.tensor_tensor(sc_[:, :, :].rearrange("p h (g k) -> p h g k", k=GSZ), sc_[:, :, :].rearrange("p h (g k) -> p h g k", k=GSZ),
                                                 gm[:, :, :].unsqueeze(3).to_broadcast([P, HALVES, NG, GSZ]), ALU.mult))
                        own.link(V.tensor_scalar(sc_[:, :, :], sc_[:, :, :], 0.0, None, ALU.add))
                        for h in range(HALVES):
                            n = own.mark(V.max(g8[:, h, :], sc_[:, h, :]))
                        own.need(n)
                        for h in range(HALVES):
                            n = own.mark(V.match_replace(comb[:, h, :], g8[:, h, :], sc_[:, h, :], GONE))
                        own.need(n)
                        for h in range(HALVES):
                            n = own.mark(V.scalar_tensor_tensor(comb[:, h, :], comb[:, h, :], GONE_BELOW, sg[:, h, :], ALU.is_le, ALU.mult,
                                                                accum_out=wsum[:, h:h + 1]))
                        own.need(n)
                        own.link(V.tensor_scalar(wsum[:, :], wsum[:, :], 1e-20, None, ALU.add))
                        own.link(V.reciprocal(wsum[:, :], wsum[:, :]))
                        for h in range(HALVES):
                            n = V.tensor_scalar(comb[:, h, :], comb[:, h, :], wsum[:, h:h + 1], 0.5 * ROUTED_SCALE, ALU.mult, ALU.mult)
                        n.then_inc(s["comb"], 1)
                        for e in range(NBLK):
                            g = GU[e % 3]
                            dve.wait_ge(s["th"], NBLK * b + e + 1)
                            own.link(V.scalar_tensor_tensor(g_s[:, e % 2, :], th[:, e % 2, :], 1.0, g[:, 0:T], ALU.add, ALU.mult))
                            if e < EB:
                                V.tensor_tensor(g_m[:, e % 2, :], g_s[:, e % 2, :], g[:, T:2 * T], ALU.mult).then_inc(s["gfree"], 1)
                                dve.wait_ge(s["gfree"], NBLK * b + e + 4)
                                dve.wait_ge(s["gate"], EB * b + e + 1)
                                if e >= 2:
                                    dve.wait_ge(s["lg"], NBLK * b + e - 1)
                                V.tensor_tensor(hid[:, e % 2, :], g_m[:, e % 2, :], CB[e % 2][:, 0:T], ALU.mult).then_inc(s["hid"], 1)
                            else:
                                dve.wait_ge(s["lg"], NBLK * b + e - 1)
                                V.scalar_tensor_tensor(hid[:, e % 2, :], g_s[:, e % 2, :], 0.5, g[:, T:2 * T], ALU.mult, ALU.mult).then_inc(s["hid"], 1)
                                dve.wait_ge(s["hid"], NBLK * b + NBLK)
                                dve.sem_inc(s["gfree"], 1)
                        dve.wait_ge(s["lg"], NBLK * b + NBLK)
                        for h in range(HALVES):
                            rows = xres[:, bass.ds(b * HALVES + h, 1), :].rearrange("p a d -> p (a d)")
                            n = V.tensor_tensor(rows, rows, Y[h][:, 0:D], ALU.add)
                        n.then_inc(s["yused"], 1)
                        dve.wait_ge(s["yused"], b + 2)
                        dve.sem_inc(s["gate2"], 1)
                        own.end()

        experts("f1")

        q1 = sb("q1", [P, A, HG, J])
        q2 = sb("q2", [P, A, H, J])
        qTb = sb("qTb", [P, T])
        kTb = sb("kTb", [P, T])
        pTb = sb("pTb", [P, 2, HALVES, HG, P])
        mxb = sb("mxb", [P, 2, HALVES])
        s = sems("b", "mv rstd xn tr cp yused q1 rep q2 scores nmax sdve sact pused pt pv on y own pown gate2")
        PAIRS = H
        with nc.Block() as block:
            @block.gpsimd
            def _(pool):
                own = Own(pool, s["pown"])
                with pool.Fori(0, BATCH) as b:
                    norm_pool(pool, own, b, s)

            @block.tensor
            def _(pe):
                pe.sem_inc(s["pv"], 2)
                pe.sem_inc(s["pused"], 2)
                with pe.Fori(0, BATCH) as b:
                    pe.wait_ge(s["xn"], b + 1)
                    for h in range(HALVES):
                        last = nc.tensor.transpose(misc[0][:, h * P:(h + 1) * P], xn[:, h, :], ident[:, :])
                    last.then_inc(s["tr"], 1)
                    pe.wait_ge(s["yused"], b + 1)
                    pe.wait_ge(s["cp"], 4 * b + 1)
                    nc.tensor.matmul(misc[1][:, 0:T], wqT[:, :], xT[:, :], start=True, stop=True)
                    nc.tensor.matmul(misc[1][:, T:2 * T], wkT[:, :], xT[:, :], start=True, stop=True).then_inc(s["tr"], 1)
                    for h in range(HALVES):
                        last = nc.tensor.matmul(misc[0][:, h * P:(h + 1) * P], xT[:, h * P:(h + 1) * P], wvbT[:, :], start=True, stop=True)
                    last.then_inc(s["tr"], 1)
                    for r in range(H // 2):
                        if r >= 2:
                            pe.wait_ge(s["q2"], H // 2 * b + r - 1)
                        for i in range(2):
                            last = nc.tensor.matmul(PT[r % 2][:, i * T:(i + 1) * T], wqrep[:, 2 * r + i, :], xT[:, :], start=True, stop=True)
                        last.then_inc(s["rep"], 1)
                    pe.wait_ge(s["q2"], H // 2 * b + H // 2)
                    pe.wait_ge(s["q1"], b + 1)
                    pe.wait_ge(s["cp"], 4 * b + 3)

                    def scores(u):
                        pe.wait_ge(s["sdve"], PAIRS * b + u + 1)
                        pe.wait_ge(s["sact"], PAIRS * b + u + 1)
                        hg = u // 8
                        for i in range(2):
                            a = 8 * ((u // 4) % 2) + 2 * (u % 4) + i
                            o = S[u % 3][:, i * T:(i + 1) * T]
                            r = slice(64 * hg, 64 * hg + 64)
                            nc.tensor.matmul(o, q1[r, a, :, :], kTb[r, :], start=True, stop=False)
                            last = nc.tensor.matmul(o, q2[:, a, hg * HG:(hg + 1) * HG, :], px[:, (A - 1 - a) * J:(A - 1 - a) * J + T],
                                                    start=False, stop=True)
                        last.then_inc(s["scores"], 1)

                    def weigh(g):
                        pe.wait_ge(s["pt"], PAIRS * b + 4 * g + 4)
                        hg, i = g // 2, g % 2
                        for h in range(HG):
                            for t in range(HALVES):
                                o = (i * H + hg * HG + h) * VW
                                last = nc.tensor.matmul(O[:, o:o + VW], pTb[:, g % 2, t, h, :], vaug[:, t, hg * HG + h, :],
                                                        start=(t == 0), stop=(t == HALVES - 1))
                        last.then_inc(s["pv"], 1)

                    for u in range(3):
                        scores(u)
                    for u in range(PAIRS):
                        pe.wait_ge(s["sact"], PAIRS * b + u + 4)
                        if u >= 2:
                            pe.wait_ge(s["pt"], PAIRS * b + u - 1)
                        for t in range(HALVES):
                            for i in range(2):
                                o = PT[u % 2][:, t * T:(t + 1) * T].rearrange("p (h i j) -> p h i j", h=HG, i=2)[:, :, i, :]
                                last = nc.tensor.transpose(o,
                                                           prob[:, u % 2, i, t * P:(t + 1) * P], ident[:, :])
                        last.then_inc(s["pused"], 1)
                        if u + 3 < PAIRS:
                            scores(u + 3)
                        if u % 4 == 1 and u > 4:
                            weigh(u // 4 - 1)
                    weigh(3)
                    pe.wait_ge(s["on"], b + 1)
                    for i in range(HALVES):
                        last = nc.tensor.transpose(misc[0][:, i * P:(i + 1) * P], onrm[:, i, :], ident[:, :])
                    last.then_inc(s["tr"], 1)
                    pe.wait_ge(s["cp"], 4 * b + 4)
                    for i in range(HALVES):
                        last = nc.tensor.matmul(misc[1][:, i * P:(i + 1) * P], oT[:, i * P:(i + 1) * P], wpT[:, :], start=True, stop=True)
                    last.then_inc(s["y"], 1)

            @block.scalar
            def _(act):
                act.sem_inc(s["sact"], 3)
                with act.Fori(0, BATCH) as b:
                    act.wait_ge(s["tr"], 4 * b + 1)
                    nc.scalar.copy(xT[:, :], misc[0][:, 0:T]).then_inc(s["cp"], 1)
                    act.wait_ge(s["tr"], 4 * b + 2)
                    nc.scalar.copy(qTb[:, :], misc[1][:, 0:T])
                    nc.scalar.copy(kTb[:, :], misc[1][:, T:2 * T]).then_inc(s["cp"], 1)
                    act.wait_ge(s["tr"], 4 * b + 3)
                    nc.scalar.copy(vaug[:, :, :, 0:HD].rearrange("p t h d -> p (t h) d"),
                                   misc[0][:, 0:T].rearrange("p (n d) -> p n d", d=HD)).then_inc(s["cp"], 1)
                    for u in range(PAIRS):
                        act.wait_ge(s["nmax"], PAIRS * b + u + 1)
                        act.wait_ge(s["pused"], PAIRS * b + u + 1)
                        for i in range(2):
                            last = nc.scalar.activation(prob[:, u % 2, i, :], S[u % 3][:, i * T:(i + 1) * T], ACT.Exp,
                                                        bias=nb[:, u % 2, i:i + 1], scale=SCALE_B)
                        last.then_inc(s["sact"], 1)
                    act.wait_ge(s["tr"], 4 * b + 4)
                    nc.scalar.copy(oT[:, :], misc[0][:, 0:T]).then_inc(s["cp"], 1)

            @block.vector
            def _(dve):
                own = Own(dve, s["own"])
                V = nc.vector
                dve.sem_inc(s["yused"], 1)
                dve.sem_inc(s["sdve"], 3)
                with dve.Fori(0, BATCH) as b:
                    norm_dve(dve, own, b, s)
                    for r in range(H // 2):
                        dve.wait_ge(s["rep"], H // 2 * b + r + 1)
                        V.tensor_tensor(q2[:, :, 2 * r:2 * r + 2, :].rearrange("p a h j -> p h a j"),
                                        PT[r % 2][:, :].rearrange("p (h a j) -> p h a j", h=2, a=A),
                                        mask_h16[:, :].unsqueeze(1).unsqueeze(1).to_broadcast([P, 2, A, J]), ALU.mult).then_inc(s["q2"], 1)
                    dve.wait_ge(s["cp"], 4 * b + 2)
                    V.tensor_tensor(q1[:, :, :, :], qTb[:, :].rearrange("p (a j) -> p a j", j=J).unsqueeze(2).to_broadcast([P, A, HG, J]),
                                    mask_h8[:, :].unsqueeze(1).unsqueeze(3).to_broadcast([P, A, HG, J]), ALU.mult).then_inc(s["q1"], 1)

                    def copy_pt(u):
                        dve.wait_ge(s["pused"], PAIRS * b + u + 3)
                        if u % 4 == 0:
                            dve.wait_ge(s["pv"], 4 * b + u // 4 + 1)
                        V.tensor_copy(pTb[:, (u // 4) % 2, :, :, 2 * J * (u % 4):2 * J * (u % 4 + 1)],
                                      PT[u % 2][:, :].rearrange("p (t h r) -> p t h r", t=2, h=HG)).then_inc(s["pt"], 1)

                    for u in range(PAIRS):
                        dve.wait_ge(s["scores"], PAIRS * b + u + 1)
                        V.tensor_reduce(mxb[:, u % 2, :], S[u % 3][:, :].rearrange("p (i t) -> p i t", i=2), AX, ALU.max).then_inc(s["sdve"], 1)
                        dve.wait_ge(s["sdve"], PAIRS * b + u + 4)
                        V.tensor_scalar(nb[:, u % 2, :], mxb[:, u % 2, :], -SCALE_B, None, ALU.mult).then_inc(s["nmax"], 1)
                        if u >= 1:
                            copy_pt(u - 1)
                    copy_pt(PAIRS - 1)
                    dve.wait_ge(s["pv"], 4 * b + 6)
                    own.link(V.reciprocal(rinv[:, :], o_all[:, :, HD]))
                    V.tensor_tensor(onrm[:, :, :].rearrange("p i (h d) -> p (i h) d", d=HD), o_all[:, :, 0:HD],
                                    rinv[:, :].unsqueeze(2).to_broadcast([P, HALVES * H, HD]), ALU.mult).then_inc(s["on"], 1)
                    dve.wait_ge(s["y"], b + 1)
                    rows = xres[:, bass.ds(b * HALVES, HALVES), :]
                    V.tensor_tensor(rows, rows, misc[1][:, 0:T].rearrange("p (i d) -> p i d", i=HALVES), ALU.add).then_inc(s["yused"], 1)
                    dve.wait_ge(s["yused"], b + 2)
                    dve.sem_inc(s["gate2"], 1)
                    own.end()

        experts("f2")

        s_out = sem("s_out")
        with nc.Block() as block:
            @block.sync
            def _(sp):
                for c in range(4):
                    n = BATCH * HALVES // 4
                    sp.dma_start(out_dram[:, c * n:(c + 1) * n, :], xres[:, c * n:(c + 1) * n, :]).then_inc(s_out, 16)
                sp.wait_ge(s_out, 16 * 4)


_INS = ['L0_attn_a_x', 'L0_attn_a_W_qkv', 'L0_attn_a_b_qkv', 'L0_attn_a_W_out', 'L0_attn_a_b_out',
        'L0_attn_b_Wq', 'L0_attn_b_Wk', 'L0_attn_b_Wv', 'L0_attn_b_Wp', 'L0_attn_b_pos_emb_k',
        'L0_ffn_gate_w', 'L0_ffn_gate_bias', 'L0_ffn_w_gate', 'L0_ffn_w_up', 'L0_ffn_w_down',
        'L0_ffn_sh_gate', 'L0_ffn_sh_up', 'L0_ffn_sh_down']


def kernel(**inputs):
    import numpy as _np
    import concourse.bacc as _bacc
    from concourse import mybir as _mybir
    from concourse.bass_utils import run_bass_kernel_spmd as _run

    nc = _bacc.Bacc("TRN2", target_bir_lowering=False, num_devices=1)
    arrays, args = {}, []
    for name in _INS:
        a = _np.ascontiguousarray(inputs[name])
        arrays[f"in_{name}_dram"] = a
        args.append(nc.dram_tensor(f"in_{name}_dram", a.shape, _mybir.dt.from_np(a.dtype), kind="ExternalInput").ap())
    args.append(nc.dram_tensor("out_0_dram", (BATCH, T, D), _mybir.dt.float32, kind="ExternalOutput").ap())
    build(nc, *args)
    r = _run(nc, [arrays], core_ids=[0])
    return r.results[0]["out_0_dram"]
```

```python
import concourse.bass as bass
from concourse import mybir
from contextlib import ExitStack

BATCH, T, D = 32, 256, 128
P = 128
HALVES = T // P
H = 16
HD = D // H
TOPK = int(T * 0.3)
NE, NI = 32, 64
EB = NE * NI // P
NBLK = EB + 1
NG, GSZ = 8, NE // 8
REL = 128
PAD32 = 32
CH = H // 4
J = 16
A = T // J
HG = 8
VW = HD + 1
EPS = 1e-5
SCALE_A = float(D) ** -0.5
SCALE_B = float(HD) ** -0.5
ROUTED_SCALE = 2.5
GONE = -3.0e38
GONE_BELOW = -2.9e38


class Own:

    def __init__(self, eng, sem):
        self.eng, self.sem, self.n = eng, sem, 0

    def mark(self, ins):
        ins.then_inc(self.sem, 1)
        self.n += 1
        return self.n

    def need(self, n):
        self.eng.wait_ge(self.sem, n)

    def link(self, ins):
        self.need(self.mark(ins))

    def end(self):
        if self.n == 0:
            return
        self.need(self.n)
        self.eng.sem_clear(self.sem)
        self.n = 0


def build(nc, x, W_qkv, b_qkv, W_out, b_out, Wq, Wk, Wv, Wp, pos, gate_w, gate_bias,
          w_gate, w_up, w_down, sh_gate, sh_up, sh_down, out):
    f32 = mybir.dt.float32
    ALU = mybir.AluOpType
    ACT = mybir.ActivationFunctionType
    AX = mybir.AxisListType.X
    ctx = ExitStack()
    with ctx:
        def sb(name, shape, dt=f32):
            return ctx.enter_context(nc.sbuf_tensor(name, shape, dt))

        def sem(name):
            return ctx.enter_context(nc.semaphore(name))

        bank = [ctx.enter_context(nc.psum_tensor(f"bank{i}", [P, 512], f32)) for i in range(8)]
        misc = bank[6:8]

        xres = sb("xres", [P, BATCH * HALVES, D])
        ident = sb("ident", [P, P])
        ones1 = sb("ones1", [1, P])
        wqkT = sb("wqkT", [P, 2, CH, P])
        bqk = sb("bqk", [P, 2, CH])
        wvT = sb("wvT", [P, D])
        bv = sb("bv", [1, D])
        woT = sb("woT", [P, D])
        bo = sb("bo", [1, D])
        wqT = sb("wqT", [P, D])
        wqT_a = sb("wqT_a", [P, D])
        wkT_a = sb("wkT_a", [P, D])
        wkT = sb("wkT", [P, D])
        wvbT = sb("wvbT", [P, D])
        wpT = sb("wpT", [P, D])
        px = sb("px", [P, T + (A - 1) * J])
        mask_h16 = sb("mask_h16", [P, H])
        mask_h8 = sb("mask_h8", [P, HG])
        gwT = sb("gwT", [P, NE])
        gbias = sb("gbias", [P, NE])
        wgT = sb("wgT", [P, NBLK, P])
        wuT = sb("wuT", [P, NBLK, P])
        wdT = sb("wdT", [P, NBLK, P])
        sel = sb("sel", [NE, EB, P])
        half_pow = sb("half_pow", [P, HALVES])
        eps_t = sb("eps_t", [P, HALVES])

        stats = sb("stats", [P, HALVES, 6])
        mv = sb("mv", [P, HALVES, 2])
        vareps = sb("vareps", [P, HALVES])
        rstd = sb("rstd", [P, HALVES])
        xn = sb("xn", [P, HALVES, D])
        xT = sb("xT", [P, T])
        mx = sb("mx", [P, HALVES, 8])
        mlast = sb("mlast", [P, HALVES, 8])
        nb = sb("nb", [P, 2, HALVES])
        work = sb("work", [P, HALVES, T])
        prob = sb("prob", [P, 2, HALVES, T])
        pT = sb("pT", [P, 2, HALVES, T])
        rinv = sb("rinv", [P, HALVES * H])
        onrm = sb("onrm", [P, HALVES, D])
        oT = sb("oT", [P, T])
        sctx = ctx.enter_context(ExitStack())

        def sb_setup(name, shape):
            return sctx.enter_context(nc.sbuf_tensor(name, shape, f32))

        stage = sb_setup("stage", [P, 3, EB, P])

        def transposes_of_weights():
            jobs = []
            for k in range(EB):
                jobs.append((stage[:, 0, k, :], wgT[:, k, :]))
                jobs.append((stage[:, 1, k, :], wuT[:, k, :]))
                jobs.append((stage[:, 2, k, :], wdT[:, k, :]))
            return jobs

        nat = sb_setup("nat", [P, 11, P])
        gnat = sb_setup("gnat", [NE, D])
        pnat = sb_setup("pnat", [P, 2, HD])
        pext = sb_setup("pext", [HD, 2 * T + J])

        s_ones = sem("s_ones")
        s_const = sem("s_const")
        s_w = sem("s_w")
        s_x = sem("s_x")
        s_tr = sem("s_tr")
        s_trc = sem("s_trc")
        s_rep = sem("s_rep")
        s_pext = sem("s_pext")
        s_px = sem("s_px")
        s_setv = sem("s_setv")

        b_cgd = b_qkv.rearrange("(w c g d) -> w g d c", w=3, c=CH, g=4)
        x_dram = x.rearrange("b (h p) d -> p (b h) d", p=P)
        out_dram = out.rearrange("b (h p) d -> p (b h) d", p=P)

        NWT = 3 * EB + 11
        with nc.Block() as block:
            @block.sync
            def _(sp):
                sp.wait_ge(s_setv, 1)
                for i, w in enumerate((W_qkv[0:P, :], W_qkv[P:2 * P, :], W_qkv[2 * P:3 * P, :], W_out,
                                       Wq, Wk, Wv, Wp, sh_gate, sh_up, sh_down)):
                    sp.dma_start(nat[:, i, :], w).then_inc(s_w, 16)
                sp.dma_start(gnat[:, :], gate_w).then_inc(s_w, 16)
                sp.dma_start(pnat[:, :, :], pos.rearrange("(k p) d -> p k d", p=P)).then_inc(s_w, 16)
                sp.dma_start(bv[:, :], b_qkv[2 * D:3 * D].rearrange("(a n) -> a n", a=1)).then_inc(s_w, 16)
                sp.dma_start(bo[:, :], b_out.rearrange("(a n) -> a n", a=1)).then_inc(s_w, 16)
                sp.dma_start(gbias[:, :], gate_bias.rearrange("(a n) -> a n", a=1).to_broadcast([P, NE])).then_inc(s_w, 16)
                for w in range(2):
                    for g in range(4):
                        sp.dma_start(bqk[PAD32 * g:PAD32 * g + HD, w, :], b_cgd[w, g],
                                     allow_slow_non_contiguous=True).then_inc(s_w, 16)
                sp.dma_start(stage[:, 0], w_gate.rearrange("e i h -> (e i) h").rearrange("(k p) h -> p k h", p=P)).then_inc(s_w, 16)
                sp.dma_start(stage[:, 1], w_up.rearrange("e i h -> (e i) h").rearrange("(k p) h -> p k h", p=P)).then_inc(s_w, 16)
                sp.dma_start(stage[:, 2].rearrange("h k (e i) -> h (k e) i", e=2), w_down.rearrange("e h i -> h e i")).then_inc(s_w, 16)
                for c in range(4):
                    n = BATCH * HALVES // 4
                    sp.dma_start(xres[:, c * n:(c + 1) * n, :], x_dram[:, c * n:(c + 1) * n, :]).then_inc(s_x, 16)
                sp.wait_ge(s_pext, 1)
                for j in range(J):
                    sp.dma_start(px[HD * j:HD * j + HD, :], pext[:, J - 1 - j:J - 1 - j + T + (A - 1) * J]).then_inc(s_px, 16)
                sp.wait_ge(s_px, 16 * J)
                sp.wait_ge(s_x, 16 * 4)

            @block.gpsimd
            def _(pool):
                one = [
                    pool.memset(ident[:, :], 0.0), pool.memset(mask_h16[:, :], 1.0),
                    pool.memset(sel[:, :, :], 1.0), pool.memset(half_pow[:, :], -0.5), pool.memset(eps_t[:, :], EPS),
                    pool.memset(ones1[:, :], 1.0),
                ]
                one[-1].then_inc(s_ones, 1)
                pool.wait_ge(s_ones, 1)
                pool.affine_select(out=ident[:, :], in_=ident[:, :], compare_op=ALU.not_equal, fill=1.0, base=0,
                                   pattern=[[-1, P]], channel_multiplier=1)
                pool.affine_select(out=mask_h16[:, :], in_=mask_h16[:, :], compare_op=ALU.is_ge, fill=0.0, base=0,
                                   pattern=[[-HD, H]], channel_multiplier=1)
                pool.affine_select(out=sel[:, :, :], in_=sel[:, :, :], compare_op=ALU.is_equal, fill=0.0, base=0,
                                   pattern=[[-2, EB], [-1, 2], [0, NI]], channel_multiplier=1).then_inc(s_ones, 1)
                pool.wait_ge(s_ones, 2)
                pool.affine_select(out=mask_h16[:, :], in_=mask_h16[:, :], compare_op=ALU.is_ge, fill=0.0, base=HD - 1,
                                   pattern=[[HD, H]], channel_multiplier=-1).then_inc(s_const, 1)

            @block.tensor
            def _(pe):
                pe.wait_ge(s_const, 1)
                pe.wait_ge(s_w, 16 * 27)
                jobs = ([nat[:, i, :] for i in range(11)]
                        + [stage[:, w, k, :] for w in range(3) for k in range(EB)])
                for n, src in enumerate(jobs):
                    if n % 4 == 0 and n >= 16:
                        pe.wait_ge(s_trc, n // 4 - 3)
                    last = nc.tensor.transpose(bank[(n // 4) % 4][:, (n % 4) * P:(n % 4 + 1) * P], src, ident[:, :])
                    if n % 4 == 3 or n == len(jobs) - 1:
                        last.then_inc(s_tr, 1)
                nc.tensor.transpose(bank[4][:, 0:NE], gnat[:, :], ident[0:NE, 0:NE])
                for k in range(2):
                    last = nc.tensor.transpose(bank[4][0:HD, 64 + k * P:64 + (k + 1) * P], pnat[:, k, :], ident[:, :])
                last.then_inc(s_tr, 1)

            @block.vector
            def _(dve):
                own = Own(dve, sem("set_own"))
                nc.vector.memset(bqk[:, :, :], 0.0).then_inc(s_setv, 1)
                own.link(nc.vector.memset(wqkT[:, :, :, :], 0.0))
                dst = []
                NJ = 11 + 3 * EB
                flat = [wgT, wuT, wdT]

                def put(n, src):
                    if n < 2:
                        nc.vector.tensor_copy((wqT_a, wkT_a)[n][:, :], src)
                        o = wqkT[:, n, :, :].rearrange("p c (g e) -> p (c g) e", g=4)[:, :, 0:HD]
                        return nc.vector.tensor_copy(o, src.rearrange("p (h d) -> p h d", d=HD))
                    o = {2: wvT[:, :], 3: woT[:, :], 4: wqT[:, :], 5: wkT[:, :], 6: wvbT[:, :], 7: wpT[:, :],
                         8: wgT[:, EB, :], 9: wuT[:, EB, :], 10: wdT[:, EB, :]}.get(n)
                    if o is None:
                        o = flat[(n - 11) // EB][:, (n - 11) % EB, :]
                    return nc.vector.tensor_copy(o, src)

                for n in range(NJ):
                    if n % 4 == 0:
                        dve.wait_ge(s_tr, n // 4 + 1)
                    last = put(n, bank[(n // 4) % 4][:, (n % 4) * P:(n % 4 + 1) * P])
                    if n % 4 == 3 or n == NJ - 1:
                        last.then_inc(s_trc, 1)
                dve.wait_ge(s_tr, (NJ + 3) // 4 + 1)
                nc.vector.tensor_copy(gwT[:, :], bank[4][:, 0:NE])
                mid = T - J + (J - 1) - REL
                own.mark(nc.vector.tensor_scalar(pext[:, mid:mid + REL], bank[4][0:HD, 64 + P:64 + 2 * P], 2.0, None, ALU.mult))
                own.link(nc.vector.tensor_scalar(pext[:, mid + REL:mid + 2 * REL], bank[4][0:HD, 64:64 + P], 2.0, None, ALU.mult))
                nc.vector.tensor_copy(pext[:, 0:mid], pext[:, mid:mid + 1].to_broadcast([HD, mid]))
                tail = 2 * T + J - mid - 2 * REL
                nc.vector.tensor_copy(pext[:, mid + 2 * REL:], pext[:, mid + 2 * REL - 1:mid + 2 * REL].to_broadcast([HD, tail])).then_inc(s_pext, 1)
                dve.wait_ge(s_const, 1)
                nc.vector.tensor_tensor(mask_h8[:, :], mask_h16[:, 0:HG], mask_h16[:, HG:H], ALU.add)
                dve.wait_ge(s_trc, (NJ + 3) // 4)

        def norm_dve(dve, own, b, s):
            rows = xres[:, bass.ds(b * HALVES, HALVES), :]
            for h in range(HALVES):
                n = own.mark(nc.vector.bn_stats(stats[:, h, :], xres[:, bass.ds(b * HALVES + h, 1), :].rearrange("p a d -> p (a d)")))
            own.need(n)
            for h in range(HALVES):
                n = nc.vector.bn_aggr(mv[:, h, :], stats[:, h, :])
            n.then_inc(s["mv"], 1)
            dve.wait_ge(s["rstd"], b + 1)
            for h in range(HALVES):
                n = nc.vector.tensor_scalar(xn[:, h, :], xres[:, bass.ds(b * HALVES + h, 1), :].rearrange("p a d -> p (a d)"),
                                            mv[:, h, 0:1], rstd[:, h:h + 1], ALU.subtract, ALU.mult)
            n.then_inc(s["xn"], 1)

        def norm_pool(pool, own, b, s):
            pool.wait_ge(s["mv"], b + 1)
            own.link(pool.tensor_tensor(vareps[:, :], mv[:, :, 1], eps_t[:, :], ALU.add))
            pool.tensor_tensor(rstd[:, :], vareps[:, :], half_pow[:, :], ALU.pow).then_inc(s["rstd"], 1)
            own.end()

        def sems(tag, names):
            return {n: sem(f"{tag}_{n}") for n in names.split()}

        sctx.close()

        GT = 16
        GROUPS = BATCH * 2
        NB4 = 4
        TARGET = TOPK - 8
        Z0, DENS = 0.626, 0.328
        GAIN = (0.7, 0.5)
        actx = ctx.enter_context(ExitStack())

        def ab(name, shape, dt=f32):
            return actx.enter_context(nc.sbuf_tensor(name, shape, dt))

        q4 = ab("q4", [P, 2, CH, T])
        k4 = ab("k4", [P, 2, CH, T])
        vaug4 = ab("vaug4", [P, 2, HALVES, H, PAD32])
        SS = ab("SS", [P, NB4, GT, T])
        xTc = ab("xTc", [P, T])
        xsum = ab("xsum", [P, 2])
        ktok = ab("ktok", [P, HALVES, D])
        qtok = ab("qtok", [P, HALVES, D])
        qnat = ab("qnat", [P, T])
        gram = ab("gram", [P, D])
        prod = ab("prod", [P, HALVES * H, HD])
        sig = ab("sig", [P, 2, H, HALVES])
        var = ab("var", [P, HALVES * H])
        kap = ab("kap", [P, 2, H, HALVES])
        nt0 = ab("nt0", [P, 2, H, HALVES])
        mxs = ab("mxs", [P, NB4, GT])
        nbs = ab("nbs", [P, NB4, GT])
        acc = ab("acc", [P, 3, NB4, GT])
        nt = ab("nt", [P, 2, GT])
        tmp = ab("tmp", [P, GT])
        hi_t = ab("hi_t", [P, 2, GT])
        kk = ab("kk", [P, 2, GT])
        osum = ab("osum", [P, 2, T])
        rinv8 = ab("rinv8", [P, HALVES, 8])
        zt = ab("zt", [P, 2, T])
        L = ab("L", [P, GT, 16])
        iota = ab("iota", [P, GT, 15])
        oh = ab("oh", [P, GT, 15])
        pick = ab("pick", [P, GT, 15])
        cur = ab("cur", [P, GT])
        nxt = ab("nxt", [P, GT])
        mid = ab("mid", [P, NB4, GT])
        fine = ab("fine", [P, NB4, GT])
        fail = ab("fail", [P, GT])
        flags = ab("flags", [1, GT + 1], mybir.dt.int32)
        junk = ab("junk", [P, 2, T], mybir.dt.bfloat16)
        ring = ab("ring", [P, 4, HALVES, T])
        bnat = ab("bnat", [P, 1])
        bq = ab("bq", [1, D])
        ones128 = ab("ones128", [P, 1])
        half_p = ab("half_p", [P, HALVES * H])
        mask_bd = ab("mask_bd", [P, H, HD])

        s = sems("a", "mv rstd xn m0 m0c m1 m1c var sig scores evac signs u0 u1 u2 thr failed flag okay "
                      "exp p pused pt pv on own aown pown slow oc gate ini inid")
        S = bank[0:3]
        PT = bank[3:5]
        O = bank[5]
        o_all = O[:, 0:HALVES * H * VW].rearrange("p (n w) -> p n w", w=VW)

        def runs(t, lag=0, n=GROUPS):
            return not isinstance(t, int) or 0 <= t - lag < n

        def wait(eng, sm, v):
            if not (isinstance(v, int) and v <= 0):
                eng.wait_ge(sm, v)

        M0, M1 = misc
        USES = ({"v": 0, "xT": -1, "oT": 2, "q0": -1, "q1": -1, "k0": -1, "k1": -1, "qn": -1},
                {"n0": 2, "y": 2, "f0": 1, "n1": 1, "f1": 1, "ktok": -1, "qtok": -1, "gram": -1, "mom": -1})

        def before(m, b, what):
            order = USES[m]
            first = sum(lag == -1 for lag in order.values())
            if not isinstance(b, int):
                return b * len(order) + first - sum(max(lag, 0) for lag in order.values()) + list(order).index(what)
            n = first
            for c in range(b + 1):
                for o, lag in order.items():
                    if c == b and o == what:
                        return n
                    n += 0 <= c - lag < BATCH

        SIGNS = {"c1": 0, "c2": 0, "c3": 0}

        def signs(t, what, tiles=GT):
            if not isinstance(t, int):
                return (t * len(SIGNS) + list(SIGNS).index(what)) * GT + tiles
            n = 0
            for c in range(t + 1):
                for o, lag in SIGNS.items():
                    if c == t and o == what:
                        return n + tiles
                    n += GT * (0 <= c - lag < GROUPS)

        def m0_before(b, what):
            return before(0, b, what)

        def m1_before(b, what):
            return before(1, b, what)

        BODY = (1, BATCH // 2 - 1)

        def schedule(eng, step):
            step(-1, -1, 3)
            for u in range(4):
                step(u, 0, u)
            with eng.Fori(*BODY) as i:
                for u in range(4):
                    step(i * 4 + u, i * 2 + u // 2, u)
            for i in (BODY[1], BODY[1] + 1):
                for u in range(4):
                    if 4 * i + u <= GROUPS + 2:
                        step(4 * i + u, 2 * i + u // 2, u)

        with nc.Block() as block:
            @block.gpsimd
            def _(pool):
                own = Own(pool, s["pown"])
                pool.memset(half_p[:, :], 0.5)
                pool.memset(ones128[:, :], 1.0)
                pool.memset(mask_bd[:, :, :], 1.0).then_inc(s["ini"], 1)
                pool.wait_ge(s["ini"], 1)
                pool.affine_select(out=mask_bd[:, :, :], in_=mask_bd[:, :, :], compare_op=ALU.is_ge, fill=0.0, base=0,
                                   pattern=[[-HD, H], [0, HD]], channel_multiplier=1).then_inc(s["ini"], 1)
                pool.iota(iota[:, :, :], [[0, GT], [1, 15]], base=1, channel_multiplier=0,
                          allow_small_or_imprecise_dtypes=True)
                pool.wait_ge(s["ini"], 2)
                pool.affine_select(out=mask_bd[:, :, :], in_=mask_bd[:, :, :], compare_op=ALU.is_ge, fill=0.0, base=HD - 1,
                                   pattern=[[HD, H], [0, HD]], channel_multiplier=-1).then_inc(s["ini"], 1)

                def front(b):
                    pool.wait_ge(s["mv"], b + 1)
                    own.link(pool.tensor_tensor(vareps[:, :], mv[:, :, 1], eps_t[:, :], ALU.add))
                    pool.tensor_tensor(rstd[:, :], vareps[:, :], half_pow[:, :], ALU.pow).then_inc(s["rstd"], 1)

                def spread(b, par):
                    pool.wait_ge(s["var"], b + 1)
                    pool.tensor_tensor(sig[:, par, :, :].rearrange("p h i -> p i h"), var[:, :].rearrange("p (i h) -> p i h", i=HALVES),
                                       half_p[:, :].rearrange("p (i h) -> p i h", i=HALVES), ALU.pow).then_inc(s["sig"], 1)

                front(0)
                spread(0, 0)
                own.end()

                def pair(i):
                    for v in range(2):
                        if runs(2 * i + v, -1, BATCH):
                            front(2 * i + v + 1)
                            spread(2 * i + v + 1, (v + 1) % 2)
                    own.end()

                pair(0)
                with pool.Fori(*BODY) as i:
                    pair(i)
                pair(BODY[1])

            @block.sync
            def _(sp):
                sp.dma_start(bnat[:, :], b_qkv[0:D].rearrange("(n a) -> n a", a=1), allow_slow_non_contiguous=True).then_inc(s["inid"], 16)
                sp.dma_start(bq[:, :], b_qkv[0:D].rearrange("(a n) -> a n", a=1)).then_inc(s["inid"], 16)
                sp.wait_ge(s["inid"], 32)

            @block.tensor
            def _(pe):
                pe.wait_ge(s["ini"], 3)
                pe.wait_ge(s["inid"], 32)

                def use0(n):
                    wait(pe, s["m0c"], n)

                def use1(n):
                    wait(pe, s["m1c"], n)

                def turn_x(b, n):
                    pe.wait_ge(s["xn"], b + 1)
                    use0(n)
                    for h in range(HALVES):
                        last = nc.tensor.transpose(M0[:, h * P:(h + 1) * P], xn[:, h, :], ident[:, :])
                    last.then_inc(s["m0"], 1)

                def project(m, n):
                    use0(n)
                    for j in range(2):
                        last = nc.tensor.matmul(M0[:, j * T:(j + 1) * T], wqkT[:, m // 2, 2 * (m % 2) + j, :],
                                                (xT if m < 2 else xTc)[:, :], start=True, stop=True)
                    last.then_inc(s["m0"], 1)

                def values(n):
                    use0(n)
                    for h in range(HALVES):
                        nc.tensor.matmul(M0[:, h * P:(h + 1) * P], xT[:, h * P:(h + 1) * P], wvT[:, :], start=True, stop=False)
                        last = nc.tensor.matmul(M0[:, h * P:(h + 1) * P], ones1[:, :], bv[:, :], start=False, stop=True)
                    last.then_inc(s["m0"], 1)

                def queries(n):
                    use0(n)
                    nc.tensor.matmul(M0[:, 0:T], wqT_a[:, :], xT[:, :], start=True, stop=True).then_inc(s["m0"], 1)

                def k_rows(n):
                    use1(n)
                    for h in range(HALVES):
                        last = nc.tensor.matmul(M1[:, h * P:(h + 1) * P], xTc[:, h * P:(h + 1) * P], wkT_a[:, :], start=True, stop=True)
                    last.then_inc(s["m1"], 1)

                def q_rows(n):
                    use1(n)
                    for h in range(HALVES):
                        nc.tensor.matmul(M1[:, h * P:(h + 1) * P], xT[:, h * P:(h + 1) * P], wqT_a[:, :], start=True, stop=False)
                        last = nc.tensor.matmul(M1[:, h * P:(h + 1) * P], ones1[:, :], bq[:, :], start=False, stop=True)
                    last.then_inc(s["m1"], 1)

                def moments(n):
                    use1(n)
                    for h in range(HALVES):
                        last = nc.tensor.matmul(M1[:, 0:P], ktok[:, h, :], ktok[:, h, :], start=(h == 0), stop=(h == HALVES - 1))
                    last.then_inc(s["m1"], 1)

                def spreads(n):
                    use1(n)
                    for h in range(HALVES):
                        last = nc.tensor.matmul(M1[:, h * P:(h + 1) * P], qnat[:, h * P:(h + 1) * P], gram[:, :], start=True, stop=True)
                    last.then_inc(s["m1"], 1)

                turn_x(0, 0)
                for m in range(4):
                    project(m, m + 1)
                queries(5)
                wait(pe, s["m0c"], 6)
                for n, f in enumerate((k_rows, q_rows, moments, spreads)):
                    f(n)

                def step(t, b, u):
                    par, even = u // 2 % 2, u % 2 == 0
                    bb = t // 2 if isinstance(t, int) else b
                    front = not isinstance(bb, int) or 0 <= bb < BATCH - 1

                    def scores(h):
                        if not runs(t, -1):
                            return
                        g = 8 * ((u + 1) % 2) + h
                        p1 = (u + 1) // 2 % 2
                        wait(pe, s["evac"], GT * (t + 1) + (-2, 0)[h] if h < 2 else GT * (t + 1) + 2 * h - 4)
                        r = slice(PAD32 * (g % 4), PAD32 * (g % 4) + HD)
                        for i in range(HALVES):
                            last = nc.tensor.matmul(S[h % 3][:, i * T:(i + 1) * T], q4[r, p1, g // 4, i * P:(i + 1) * P],
                                                    k4[r, p1, g // 4, :], start=True, stop=True)
                        last.then_inc(s["scores"], 1)

                    if not even and front:
                        wait(pe, s["m0c"], m0_before(bb, "k1") + 1)
                    for h in range(3):
                        scores(h)
                    if runs(t, 3):
                        wait(pe, s["oc"], t - 2)
                        use1(m1_before(bb, "n0" if even else "n1"))
                        for i in range(HALVES):
                            for c in range(2):
                                last = nc.tensor.transpose(M1[:, (i * 2 + c) * P:(i * 2 + c + 1) * P], osum[:, c, i * P:(i + 1) * P], ident[:, :])
                        last.then_inc(s["m1"], 1)
                    if even and runs(bb, 0, BATCH):
                        values(m0_before(bb, "v"))
                    if even and front:
                        turn_x(bb + 1, m0_before(bb, "xT"))
                    tail = runs(bb, 2, BATCH)
                    if even and tail:
                        pe.wait_ge(s["on"], t - 2)
                        use0(m0_before(bb, "oT"))
                        for i in range(HALVES):
                            last = nc.tensor.transpose(M0[:, i * P:(i + 1) * P], onrm[:, i, :], ident[:, :])
                        last.then_inc(s["m0"], 1)
                    scores(3)
                    scores(4)
                    if even and tail:
                        wait(pe, s["m0c"], m0_before(bb, "oT") + 1)
                        use1(m1_before(bb, "y"))
                        for i in range(HALVES):
                            nc.tensor.matmul(M1[:, i * P:(i + 1) * P], oT[:, i * P:(i + 1) * P], woT[:, :], start=True, stop=False)
                            last = nc.tensor.matmul(M1[:, i * P:(i + 1) * P], ones1[:, :], bo[:, :], start=False, stop=True)
                        last.then_inc(s["m1"], 1)
                    scores(5)
                    if runs(t, 2):
                        wait(pe, s["failed"], t - 1)
                        use1(m1_before(bb, "f0" if even else "f1"))
                        nc.tensor.matmul(M1[0:1, 0:GT], ones128[:, :], fail[:, :], start=True, stop=True).then_inc(s["m1"], 1)
                    scores(6)
                    scores(7)

                    def weigh(h):
                        g = 8 * (u % 2) + h
                        wait(pe, s["pt"], 8 * (t - 2) + h + 1)
                        if h == 0:
                            wait(pe, s["oc"], t - 2)
                        for k in range(HALVES):
                            last = nc.tensor.matmul(O[PAD32 * (h % 4):PAD32 * (h % 4 + 1), (h // 4) * T:(h // 4 + 1) * T],
                                                    vaug4[:, (u // 2 + 1) % 2, k, g, :], pT[:, h % 2, k, :],
                                                    start=(k == 0), stop=(k == HALVES - 1), tile_position=(0, PAD32 * (h % 4)))
                        last.then_inc(s["pv"], 1)

                    for h in range(8):
                        if runs(t, 2):
                            wait(pe, s["p"], 8 * (t - 2) + h + 1)
                            for i in range(HALVES):
                                for k in range(HALVES):
                                    last = nc.tensor.transpose(PT[h % 2][:, k * T + i * P:k * T + (i + 1) * P],
                                                               prob[:, h % 2, i, k * P:(k + 1) * P], ident[:, :])
                            last.then_inc(s["pused"], 1)
                            if h >= 1:
                                weigh(h - 1)
                        if front and even and h < 5:
                            n = m0_before(bb, ("q0", "q1", "k0", "k1", "qn")[h])
                            if h < 4:
                                project(h, n)
                            else:
                                queries(n)
                        if front and not even and h < 4:
                            if h == 0:
                                wait(pe, s["m0c"], m0_before(bb, "qn") + 1)
                            (k_rows, q_rows, moments, spreads)[h](m1_before(bb, ("ktok", "qtok", "gram", "mom")[h]))
                    if runs(t, 2):
                        weigh(7)

                schedule(pe, step)

            @block.scalar
            def _(act):
                own = Own(act, s["aown"])
                act.wait_ge(s["inid"], 32)

                def take_x(n):
                    wait(act, s["m0"], n + 1)
                    own.link(nc.scalar.activation(xT[:, :], M0[:, 0:T], ACT.Copy, accum_out=xsum[:, 0:1]))
                    own.link(nc.scalar.mul(xsum[:, 1:2], xsum[:, 0:1], -1.0 / T))
                    nc.scalar.activation(xTc[:, :], xT[:, :], ACT.Identity, bias=xsum[:, 1:2]).then_inc(s["m0c"], 1)

                def take_q(m, par, n):
                    wait(act, s["m0"], n + 1)
                    for j in range(2):
                        c = 2 * (m % 2) + j
                        if m < 2:
                            last = nc.scalar.activation(q4[:, par, c, :], M0[:, j * T:(j + 1) * T], ACT.Identity, bias=bqk[:, 0, c:c + 1])
                    if m >= 2:
                        last = nc.scalar.copy(k4[:, par, 2 * (m % 2):2 * (m % 2) + 2, :].rearrange("p c t -> p (c t)"), M0[:, :])
                    last.then_inc(s["m0c"], 1)

                def take_v(slot, n):
                    wait(act, s["m0"], n + 1)
                    nc.scalar.copy(vaug4[:, slot, :, :, 0:HD].rearrange("p t h d -> p (t h) d"),
                                   M0[:, 0:T].rearrange("p (n d) -> p n d", d=HD)).then_inc(s["m0c"], 1)

                def take_qn(n):
                    wait(act, s["m0"], n + 1)
                    nc.scalar.activation(qnat[:, :], M0[:, 0:T], ACT.Identity, bias=bnat[:, 0:1]).then_inc(s["m0c"], 1)

                take_x(0)
                for m in range(4):
                    take_q(m, 0, m + 1)
                take_qn(5)
                own.end()

                def step(t, b, u):
                    par, even = u // 2 % 2, u % 2 == 0
                    bb = t // 2 if isinstance(t, int) else b
                    front = not isinstance(bb, int) or 0 <= bb < BATCH - 1

                    def count(tt, k, uu, bias, ready, done, part=range(GT)):
                        if part[0] == 0:
                            wait(act, s[ready], tt + 1)
                        for c in part:
                            wait(act, s["signs"], signs(t, done, c) - 1)
                            nc.scalar.activation(junk[:, c % 2, :], SS[:, uu % 4, c, :], ACT.Sign, bias=bias(c),
                                                 accum_out=acc[:, k, uu % 4, c:c + 1]).then_inc(s["signs"], 1)

                    if runs(t, 3):
                        wait(act, s["pv"], 8 * (t - 2))
                        nc.scalar.copy(osum[:, :, :].rearrange("p c i -> p (c i)"), O[:, :]).then_inc(s["oc"], 1)
                    if even and runs(bb, 0, BATCH):
                        take_v(par, m0_before(bb, "v"))
                    if front and even:
                        take_x(m0_before(bb, "xT"))
                    if even and runs(bb, 2, BATCH):
                        wait(act, s["m0"], m0_before(bb, "oT") + 1)
                        nc.scalar.copy(oT[:, :], M0[:, 0:T]).then_inc(s["m0c"], 1)
                    if runs(t):
                        wait(act, s["evac"], GT * t + GT)
                        count(t, 0, u, lambda c: nt0[:, par, 8 * (u % 2) + c // 2, c % 2:c % 2 + 1], "u0", "c1")

                    def copy_pt(h):
                        wait(act, s["pused"], 8 * (t - 2) + h + 1)
                        wait(act, s["pv"], 8 * (t - 2) + h - 1)
                        nc.scalar.copy(pT[:, h % 2, :, :].rearrange("p t i -> p (t i)"), PT[h % 2][:, :]).then_inc(s["pt"], 1)

                    for h in range(8):
                        if runs(t, 2):
                            if h == 0:
                                wait(act, s["okay"], t - 1)
                            wait(act, s["p"], 8 * (t - 2) + h - 3)
                            for i in range(HALVES):
                                c = 2 * h + i
                                last = nc.scalar.activation(ring[:, h % 4, i, :], SS[:, (u + 2) % 4, c, :], ACT.Exp,
                                                            bias=nbs[:, (u + 2) % 4, c:c + 1], scale=SCALE_A)
                            last.then_inc(s["exp"], 1)
                            if h >= 1:
                                copy_pt(h - 1)
                        if front and even and h < 5:
                            n = m0_before(bb, ("q0", "q1", "k0", "k1", "qn")[h])
                            if h < 4:
                                take_q(h, (par + 1) % 2, n)
                            else:
                                take_qn(n)
                        if runs(t):
                            count(t, 1, u, lambda c: nt[:, 0, c:c + 1], "u1", "c2", range(2 * h, 2 * h + 2))
                    if runs(t, 2):
                        copy_pt(7)
                    if runs(t):
                        count(t, 2, u, lambda c: nt[:, 1, c:c + 1], "u2", "c3")
                    if u == 3:
                        own.end()

                schedule(act, step)

            @block.vector
            def _(dve):
                own = Own(dve, s["own"])
                V = nc.vector
                va = vaug4[:, :, :, :, :].rearrange("p a t h w -> p (a t h) w")
                own.link(V.memset(va, 0.0))
                own.link(V.memset(va[:, :, HD:VW], 1.0))
                dve.wait_ge(s["ini"], 3)

                def statistics(b):
                    for h in range(HALVES):
                        n = own.mark(V.bn_stats(stats[:, h, :], xrow(b, h)))
                    own.need(n)
                    for h in range(HALVES):
                        n = V.bn_aggr(mv[:, h, :], stats[:, h, :])
                    n.then_inc(s["mv"], 1)

                def xrow(b, h):
                    if isinstance(b, int):
                        return xres[:, b * HALVES + h, :]
                    return xres[:, bass.ds(b * HALVES + h, 1), :].rearrange("p a d -> p (a d)")

                def normed(b):
                    dve.wait_ge(s["rstd"], b + 1)
                    for h in range(HALVES):
                        n = V.tensor_scalar(xn[:, h, :], xrow(b, h), mv[:, h, 0:1], rstd[:, h:h + 1], ALU.subtract, ALU.mult)
                    n.then_inc(s["xn"], 1)

                def take_k(n):
                    wait(dve, s["m1"], n + 1)
                    V.tensor_copy(ktok[:, :, :].rearrange("p i d -> p (i d)"), M1[:, 0:T]).then_inc(s["m1c"], 1)

                def take_qr(n):
                    wait(dve, s["m1"], n + 1)
                    V.tensor_copy(qtok[:, :, :].rearrange("p i d -> p (i d)"), M1[:, 0:T]).then_inc(s["m1c"], 1)

                def take_g(n):
                    wait(dve, s["m1"], n + 1)
                    V.tensor_tensor(gram[:, :], M1[:, 0:P], mask_bd[:, :, :].rearrange("p h d -> p (h d)"), ALU.mult).then_inc(s["m1c"], 1)

                def take_mom(b, n):
                    wait(dve, s["m1"], n + 1)
                    wait(dve, s["m1c"], n - 1)
                    V.tensor_tensor(prod[:, :, :].rearrange("p n d -> p (n d)"), M1[:, 0:T], qtok[:, :, :].rearrange("p i d -> p (i d)"),
                                    ALU.mult).then_inc(s["m1c"], 1)
                    wait(dve, s["m1c"], n + 1)
                    own.link(V.tensor_reduce(var[:, :], prod[:, :, :], AX, ALU.add))
                    V.tensor_scalar(var[:, :], var[:, :], 0.0, None, ALU.max).then_inc(s["var"], 1)

                def guess(b, par):
                    dve.wait_ge(s["sig"], b + 1)
                    V.tensor_scalar(kap[:, par, :, :], sig[:, par, :, :], 1.0 / (T ** 0.5 * T * DENS), None, ALU.mult)
                    own.link(V.tensor_scalar(nt0[:, par, :, :], sig[:, par, :, :], -Z0 / T ** 0.5, None, ALU.mult))
                    dve.sem_inc(s["u0"], 2)

                statistics(0)
                normed(0)
                for n, f in enumerate((take_k, take_qr, take_g)):
                    f(n)
                take_mom(0, 3)
                guess(0, 0)
                own.end()

                def step(t, b, u):
                    par, even = u // 2 % 2, u % 2 == 0
                    bb = t // 2 if isinstance(t, int) else b
                    front = not isinstance(bb, int) or 0 <= bb < BATCH - 1
                    tail = runs(bb, 2, BATCH)
                    z1 = (u + 3) % 4
                    z2 = (u + 2) % 4

                    def evac(h):
                        if not runs(t, -1):
                            return
                        wait(dve, s["scores"], 8 * (t + 1) + h + 1)
                        for i in range(HALVES):
                            c = 2 * h + i
                            V.tensor_scalar(SS[:, (u + 1) % 4, c, :], S[h % 3][:, i * T:(i + 1) * T], 1.0, -3.0e38, ALU.mult, ALU.max,
                                            accum_out=mxs[:, (u + 1) % 4, c:c + 1]).then_inc(s["evac"], 1)
                        if h == 7:
                            wait(dve, s["evac"], GT * (t + 1) + GT)
                            own.mark(V.tensor_scalar(nbs[:, (u + 1) % 4, :], mxs[:, (u + 1) % 4, :], -SCALE_A, None, ALU.mult))

                    def judge():
                        V.tensor_scalar(fail[:, :], fine[:, z2, :], -1.0, 1.0, ALU.mult, ALU.add).then_inc(s["failed"], 1)

                    def largest(p):
                        if not runs(t, 1):
                            return
                        for i in range(2):
                            c = 2 * p + i
                            n = own.mark(V.scalar_tensor_tensor(zt[:, i, :], SS[:, z1, c, :], hi_t[:, 0, c:c + 1], SS[:, z1, c, :],
                                                                ALU.is_le, ALU.mult))
                        for i in range(2):
                            own.need(n - 1 + i)
                            m = own.mark(V.max(L[:, 2 * p + i, 0:8], zt[:, i, :]))
                        for i in range(2):
                            own.need(m - 1 + i)
                            n = own.mark(V.match_replace(zt[:, i, :], L[:, 2 * p + i, 0:8], zt[:, i, :], GONE))
                        for i in range(2):
                            own.need(n - 1 + i)
                            m = own.mark(V.max(L[:, 2 * p + i, 8:16], zt[:, i, :]))
                        if p < 7:
                            own.need(m)

                    def move(k, done, prev, out):
                        if runs(t):
                            wait(dve, s["signs"], signs(t, ("c1", "c2")[k]))
                            kp = kap[:, par, 8 * (u % 2):8 * (u % 2) + 8, :].rearrange("p h i -> p (h i)")
                            own.link(V.tensor_scalar(tmp[:, :], acc[:, k, u, :], float(T - 2 * TARGET), -0.5 * GAIN[k], ALU.add, ALU.mult))
                            own.link(V.tensor_tensor(tmp[:, :], tmp[:, :], kp, ALU.mult))
                            V.tensor_tensor(out, prev, tmp[:, :], ALU.add).then_inc(s[done], 1)

                    if even and front:
                        statistics(bb + 1)
                    if runs(t, 2):
                        judge()
                    evac(0)
                    evac(1)
                    if runs(t, 3):
                        n1 = m1_before(bb, "n0" if even else "n1")
                        wait(dve, s["m1"], n1 + 1)
                        sums = M1[:, :].rearrange("p (i h w) -> p i h w", i=HALVES, h=8)
                        own.link(V.reciprocal(rinv8[:, :, :], sums[:, :, :, HD]))
                        q = 8 * ((u + 1) % 2)
                        V.tensor_tensor(onrm[:, :, :].rearrange("p i (h d) -> p i h d", d=HD)[:, :, q:q + 8, :], sums[:, :, :, 0:HD],
                                        rinv8[:, :, :].unsqueeze(3).to_broadcast([P, HALVES, 8, HD]), ALU.mult).then_inc(s["m1c"], 1)
                        wait(dve, s["m1c"], n1 + 1)
                        dve.sem_inc(s["on"], 1)
                    if even and front:
                        normed(bb + 1)
                    if runs(t, 1):
                        wait(dve, s["signs"], signs(t - 1, "c3"))
                        own.link(V.tensor_scalar(hi_t[:, 0, :], nt[:, 1, :], -1.0, None, ALU.mult))
                        own.link(V.tensor_scalar(kk[:, 0, :], acc[:, 2, z1, :], -0.5, float(TOPK - T // 2), ALU.mult, ALU.add))
                    largest(0)
                    evac(2)
                    largest(1)
                    if even and tail:
                        wait(dve, s["m1"], m1_before(bb, "y") + 1)
                        for h in range(HALVES):
                            n = V.tensor_tensor(xrow(bb - 2, h), xrow(bb - 2, h), M1[:, h * P:(h + 1) * P], ALU.add)
                        n.then_inc(s["m1c"], 1)
                    evac(3)
                    largest(2)
                    evac(4)
                    if runs(t, 2):
                        n1 = m1_before(bb, "f0" if even else "f1")
                        wait(dve, s["m1"], n1 + 1)
                        V.tensor_copy(flags[:, 0:GT], M1[0:1, 0:GT]).then_inc(s["m1c"], 1)
                        wait(dve, s["m1c"], n1 + 1)
                        own.link(V.tensor_reduce(flags[:, GT:GT + 1], flags[:, 0:GT], AX, ALU.max))
                        redo(dve, V, z2)
                        dve.sem_inc(s["okay"], 1)
                    evac(5)
                    largest(3)
                    if runs(t):
                        move(0, "u1", nt0[:, par, 8 * (u % 2):8 * (u % 2) + 8, :].rearrange("p h i -> p (h i)"), nt[:, 0, :])
                    for h in range(8):
                        if runs(t, 2):
                            wait(dve, s["exp"], 8 * (t - 2) + h + 1)
                            wait(dve, s["pused"], 8 * (t - 2) + h - 1)
                            for i in range(HALVES):
                                c = 2 * h + i
                                n = V.scalar_tensor_tensor(prob[:, h % 2, i, :], SS[:, z2, c, :], mid[:, z2, c:c + 1], ring[:, h % 4, i, :],
                                                           ALU.is_ge, ALU.mult)
                            n.then_inc(s["p"], 1)
                        if h in (1, 3, 5):
                            largest((h - 1) // 2 + 4)
                        if h in (2, 4):
                            evac(h // 2 + 5)
                        if front and not even and h >= 1:
                            if h in (1, 2, 3):
                                (take_k, take_qr, take_g)[h - 1](m1_before(bb, ("ktok", "qtok", "gram")[h - 1]))
                            elif h == 4:
                                take_mom(bb + 1, m1_before(bb, "mom"))
                            elif h == 6:
                                guess(bb + 1, (par + 1) % 2)
                    if runs(t):
                        move(1, "u2", nt[:, 0, :], nt[:, 1, :])
                    largest(7)
                    if runs(t, 1):
                        own.need(own.n)
                        own.link(V.tensor_tensor(oh[:, :, :], iota[:, :, :], kk[:, 0, :].unsqueeze(2).to_broadcast([P, GT, 15]), ALU.is_equal))
                        own.link(V.tensor_tensor(pick[:, :, :], oh[:, :, :], L[:, :, 0:15], ALU.mult))
                        own.link(V.tensor_reduce(cur[:, :], pick[:, :, :], AX, ALU.add))
                        own.link(V.tensor_tensor(pick[:, :, :], oh[:, :, :], L[:, :, 1:16], ALU.mult))
                        own.link(V.tensor_reduce(nxt[:, :], pick[:, :, :], AX, ALU.add))
                        own.mark(V.tensor_copy(mid[:, z1, :], cur[:, :]))
                        own.mark(V.tensor_tensor(fine[:, z1, :], L[:, :, 0], hi_t[:, 0, :], ALU.is_lt))
                        own.link(V.tensor_tensor(nxt[:, :], nxt[:, :], cur[:, :], ALU.is_lt))
                        own.link(V.scalar_tensor_tensor(tmp[:, :], cur[:, :], 0.0, nxt[:, :], ALU.is_gt, ALU.mult))
                        own.link(V.tensor_tensor(fine[:, z1, :], fine[:, z1, :], tmp[:, :], ALU.mult))
                    if u == 3:
                        dve.sem_inc(s["gate"], 1)
                        own.end()

                def redo(dve, V, z):
                    slow = Own(dve, s["slow"])
                    any_failed = dve.value_load(flags[0:1, GT:GT + 1], min_val=0, max_val=P)
                    with dve.If(any_failed > 0):
                        for c in range(GT):
                            failed = dve.value_load(flags[0:1, c:c + 1], min_val=0, max_val=P)
                            with dve.If(failed > 0):
                                slow.n = 0
                                src = SS[:, z, c, :]
                                w = work[:, 0, :]
                                for r in range(TOPK // 8 + 1):
                                    slow.link(V.max(mx[:, 0, :], src if r == 0 else w))
                                    if r == TOPK // 8:
                                        slow.link(V.memset(mx[:, 0, TOPK % 8:8], GONE))
                                    slow.link(V.match_replace(w, mx[:, 0, :], src if r == 0 else w, GONE))
                                slow.link(V.tensor_scalar(w, w, GONE_BELOW, -1.0e30, ALU.is_gt, ALU.mult))
                                slow.link(V.tensor_tensor(src, src, w, ALU.add))
                                slow.link(V.memset(mid[:, z, c:c + 1], -1.0e29))
                                dve.sem_clear(s["slow"])

                schedule(dve, step)

        actx.close()

        hid = sb("hid", [P, 2, T])
        th = sb("th", [P, 2, T])
        g_s = sb("g_s", [P, 2, T])
        g_m = sb("g_m", [P, 2, T])
        sg = sb("sg", [P, HALVES, NE])
        sc_ = sb("sc_", [P, HALVES, NE])
        hi = sb("hi", [P, HALVES * NG, 2])
        lo = sb("lo", [P, HALVES * NG, 2])
        m1 = sb("m1", [P, HALVES * NG])
        m2 = sb("m2", [P, HALVES * NG])
        m3 = sb("m3", [P, HALVES * NG])
        gsc = sb("gsc", [P, HALVES, 2 * NG])
        g8 = sb("g8", [P, HALVES, 8])
        gr = sb("gr", [P, HALVES, 2 * NG])
        gm = sb("gm", [P, HALVES, NG])
        comb = sb("comb", [P, HALVES, NE])
        wsum = sb("wsum", [P, HALVES])
        combT = sb("combT", [NE, T])

        def experts(tag):
            s = sems(tag, "mv rstd xn tr cp lg th gs gate comb gu hid yused own pown gfree gate2")
            GU = bank[0:3]
            CB = [bank[3], bank[7]]
            Y = bank[4:6]
            with nc.Block() as block:
                @block.gpsimd
                def _(pool):
                    own = Own(pool, s["pown"])
                    with pool.Fori(0, BATCH) as b:
                        norm_pool(pool, own, b, s)

                @block.tensor
                def _(pe):
                    with pe.Fori(0, BATCH) as b:
                        pe.wait_ge(s["xn"], b + 1)
                        for h in range(HALVES):
                            last = nc.tensor.transpose(misc[0][:, h * P:(h + 1) * P], xn[:, h, :], ident[:, :])
                        last.then_inc(s["tr"], 1)
                        pe.wait_ge(s["cp"], 2 * b + 1)
                        for h in range(HALVES):
                            last = nc.tensor.matmul(misc[0][:, h * NE:(h + 1) * NE], xT[:, h * P:(h + 1) * P], gwT[:, :], start=True, stop=True)
                        last.then_inc(s["tr"], 1)

                        def up(e):
                            pe.wait_ge(s["gfree"], NBLK * b + e + 1)
                            g = GU[e % 3]
                            nc.tensor.matmul(g[:, 0:T], wgT[:, e, :], xT[:, :], start=True, stop=True)
                            last = nc.tensor.matmul(g[:, T:2 * T], wuT[:, e, :], xT[:, :], start=True, stop=True)
                            last.then_inc(s["gu"], 1)

                        def spread(e):
                            c = CB[e % 2][:, 0:T]
                            if e < EB:
                                nc.tensor.matmul(c, sel[:, e, :], combT[:, :], start=True, stop=True).then_inc(s["gate"], 1)

                        def down(e):
                            pe.wait_ge(s["hid"], NBLK * b + e + 1)
                            for h in range(HALVES):
                                last = nc.tensor.matmul(Y[h][:, 0:D], hid[:, e % 2, h * P:(h + 1) * P], wdT[:, e, :],
                                                        start=(e == 0), stop=(e == NBLK - 1))
                            last.then_inc(s["lg"], 1)

                        up(0)
                        up(1)
                        pe.wait_ge(s["comb"], b + 1)
                        for h in range(HALVES):
                            last = nc.tensor.transpose(misc[0][0:NE, h * P:(h + 1) * P], comb[:, h, :], ident[:, :])
                        last.then_inc(s["tr"], 1)
                        pe.wait_ge(s["cp"], 2 * b + 2)
                        pe.wait_ge(s["yused"], b + 1)
                        spread(0)
                        spread(1)
                        for e in range(NBLK):
                            if e + 2 < NBLK:
                                up(e + 2)
                            down(e)
                            if e + 2 < NBLK:
                                spread(e + 2)

                @block.scalar
                def _(act):
                    with act.Fori(0, BATCH) as b:
                        act.wait_ge(s["tr"], 3 * b + 1)
                        nc.scalar.copy(xT[:, :], misc[0][:, 0:T]).then_inc(s["cp"], 1)
                        act.wait_ge(s["tr"], 3 * b + 2)
                        nc.scalar.activation(sg[:, :, :].rearrange("p h e -> p (h e)"), misc[0][:, 0:HALVES * NE], ACT.Tanh, scale=0.5).then_inc(s["gs"], 1)

                        def tanh(e):
                            act.wait_ge(s["gu"], NBLK * b + e + 1)
                            act.wait_ge(s["gfree"], NBLK * b + e + 2)
                            nc.scalar.activation(th[:, e % 2, :], GU[e % 3][:, 0:T], ACT.Tanh, scale=0.5).then_inc(s["th"], 1)

                        tanh(0)
                        act.wait_ge(s["tr"], 3 * b + 3)
                        nc.scalar.copy(combT[:, :], misc[0][0:NE, 0:T]).then_inc(s["cp"], 1)
                        for e in range(1, NBLK):
                            tanh(e)

                @block.vector
                def _(dve):
                    own = Own(dve, s["own"])
                    dve.sem_inc(s["yused"], 1)
                    dve.sem_inc(s["gfree"], 3)
                    nc.vector.memset(gsc[:, :, :], GONE)
                    with dve.Fori(0, BATCH) as b:
                        V = nc.vector
                        norm_dve(dve, own, b, s)
                        dve.wait_ge(s["gs"], b + 1)
                        own.link(V.tensor_scalar(sg[:, :, :], sg[:, :, :], 0.5, 0.5, ALU.mult, ALU.add))
                        own.link(V.tensor_tensor(sc_[:, :, :], sg[:, :, :], gbias[:, :].unsqueeze(1).to_broadcast([P, HALVES, NE]), ALU.add))
                        q = sc_[:, :, :].rearrange("p h (g k two) -> p (h g) k two", k=2, two=2)
                        V.tensor_tensor(hi[:, :, :], q[:, :, :, 0], q[:, :, :, 1], ALU.max)
                        own.link(V.tensor_tensor(lo[:, :, :], q[:, :, :, 0], q[:, :, :, 1], ALU.min))
                        V.tensor_tensor(m1[:, :], hi[:, :, 0], hi[:, :, 1], ALU.max)
                        V.tensor_tensor(m2[:, :], hi[:, :, 0], hi[:, :, 1], ALU.min)
                        own.link(V.tensor_tensor(m3[:, :], lo[:, :, 0], lo[:, :, 1], ALU.max))
                        own.link(V.tensor_tensor(m2[:, :], m2[:, :], m3[:, :], ALU.max))
                        own.link(V.tensor_tensor(gsc[:, :, 0:NG], m1[:, :].rearrange("p (h g) -> p h g", h=HALVES),
                                                 m2[:, :].rearrange("p (h g) -> p h g", h=HALVES), ALU.add))
                        for h in range(HALVES):
                            n = own.mark(V.max(g8[:, h, :], gsc[:, h, :]))
                        own.need(n)
                        own.link(V.memset(g8[:, :, 4:8], GONE))
                        for h in range(HALVES):
                            n = own.mark(V.match_replace(gr[:, h, :], g8[:, h, :], gsc[:, h, :], GONE))
                        own.need(n)
                        own.link(V.tensor_scalar(gm[:, :, :], gr[:, :, 0:NG], GONE_BELOW, None, ALU.is_le))
                        own.link(V.tensor_tensor(sc_[:, :, :].rearrange("p h (g k) -> p h g k", k=GSZ), sc_[:, :, :].rearrange("p h (g k) -> p h g k", k=GSZ),
                                                 gm[:, :, :].unsqueeze(3).to_broadcast([P, HALVES, NG, GSZ]), ALU.mult))
                        own.link(V.tensor_scalar(sc_[:, :, :], sc_[:, :, :], 0.0, None, ALU.add))
                        for h in range(HALVES):
                            n = own.mark(V.max(g8[:, h, :], sc_[:, h, :]))
                        own.need(n)
                        for h in range(HALVES):
                            n = own.mark(V.match_replace(comb[:, h, :], g8[:, h, :], sc_[:, h, :], GONE))
                        own.need(n)
                        for h in range(HALVES):
                            n = own.mark(V.scalar_tensor_tensor(comb[:, h, :], comb[:, h, :], GONE_BELOW, sg[:, h, :], ALU.is_le, ALU.mult,
                                                                accum_out=wsum[:, h:h + 1]))
                        own.need(n)
                        own.link(V.tensor_scalar(wsum[:, :], wsum[:, :], 1e-20, None, ALU.add))
                        own.link(V.reciprocal(wsum[:, :], wsum[:, :]))
                        for h in range(HALVES):
                            n = V.tensor_scalar(comb[:, h, :], comb[:, h, :], wsum[:, h:h + 1], 0.5 * ROUTED_SCALE, ALU.mult, ALU.mult)
                        n.then_inc(s["comb"], 1)
                        for e in range(NBLK):
                            g = GU[e % 3]
                            dve.wait_ge(s["th"], NBLK * b + e + 1)
                            own.link(V.scalar_tensor_tensor(g_s[:, e % 2, :], th[:, e % 2, :], 1.0, g[:, 0:T], ALU.add, ALU.mult))
                            if e < EB:
                                V.tensor_tensor(g_m[:, e % 2, :], g_s[:, e % 2, :], g[:, T:2 * T], ALU.mult).then_inc(s["gfree"], 1)
                                dve.wait_ge(s["gfree"], NBLK * b + e + 4)
                                dve.wait_ge(s["gate"], EB * b + e + 1)
                                if e >= 2:
                                    dve.wait_ge(s["lg"], NBLK * b + e - 1)
                                V.tensor_tensor(hid[:, e % 2, :], g_m[:, e % 2, :], CB[e % 2][:, 0:T], ALU.mult).then_inc(s["hid"], 1)
                            else:
                                dve.wait_ge(s["lg"], NBLK * b + e - 1)
                                V.scalar_tensor_tensor(hid[:, e % 2, :], g_s[:, e % 2, :], 0.5, g[:, T:2 * T], ALU.mult, ALU.mult).then_inc(s["hid"], 1)
                                dve.wait_ge(s["hid"], NBLK * b + NBLK)
                                dve.sem_inc(s["gfree"], 1)
                        dve.wait_ge(s["lg"], NBLK * b + NBLK)
                        for h in range(HALVES):
                            rows = xres[:, bass.ds(b * HALVES + h, 1), :].rearrange("p a d -> p (a d)")
                            n = V.tensor_tensor(rows, rows, Y[h][:, 0:D], ALU.add)
                        n.then_inc(s["yused"], 1)
                        dve.wait_ge(s["yused"], b + 2)
                        dve.sem_inc(s["gate2"], 1)
                        own.end()

        experts("f1")

        wqrep = sb("wqrep", [P, H, P])
        vaug = sb("vaug", [P, HALVES, H, VW])
        q1 = sb("q1", [P, A, HG, J])
        q2 = sb("q2", [P, A, H, J])
        qTb = sb("qTb", [P, T])
        kTb = sb("kTb", [P, T])
        pTb = sb("pTb", [P, 2, HALVES, HG, P])
        mxb = sb("mxb", [P, 2, HALVES])
        s = sems("b", "mv rstd xn tr cp yused q1 rep q2 scores nmax sdve sact pused pt pv on y own pown gate2 vini")
        PAIRS = H
        with nc.Block() as block:
            @block.gpsimd
            def _(pool):
                own = Own(pool, s["pown"])
                with pool.Fori(0, BATCH) as b:
                    norm_pool(pool, own, b, s)

            @block.tensor
            def _(pe):
                pe.sem_inc(s["pv"], 2)
                pe.sem_inc(s["pused"], 2)
                with pe.Fori(0, BATCH) as b:
                    pe.wait_ge(s["xn"], b + 1)
                    for h in range(HALVES):
                        last = nc.tensor.transpose(misc[0][:, h * P:(h + 1) * P], xn[:, h, :], ident[:, :])
                    last.then_inc(s["tr"], 1)
                    pe.wait_ge(s["yused"], b + 1)
                    pe.wait_ge(s["cp"], 4 * b + 1)
                    nc.tensor.matmul(misc[1][:, 0:T], wqT[:, :], xT[:, :], start=True, stop=True)
                    nc.tensor.matmul(misc[1][:, T:2 * T], wkT[:, :], xT[:, :], start=True, stop=True).then_inc(s["tr"], 1)
                    for h in range(HALVES):
                        last = nc.tensor.matmul(misc[0][:, h * P:(h + 1) * P], xT[:, h * P:(h + 1) * P], wvbT[:, :], start=True, stop=True)
                    last.then_inc(s["tr"], 1)
                    for r in range(H // 2):
                        if r >= 2:
                            pe.wait_ge(s["q2"], H // 2 * b + r - 1)
                        for i in range(2):
                            last = nc.tensor.matmul(PT[r % 2][:, i * T:(i + 1) * T], wqrep[:, 2 * r + i, :], xT[:, :], start=True, stop=True)
                        last.then_inc(s["rep"], 1)
                    pe.wait_ge(s["q2"], H // 2 * b + H // 2)
                    pe.wait_ge(s["q1"], b + 1)
                    pe.wait_ge(s["cp"], 4 * b + 3)

                    def scores(u):
                        pe.wait_ge(s["sdve"], PAIRS * b + u + 1)
                        pe.wait_ge(s["sact"], PAIRS * b + u + 1)
                        hg = u // 8
                        for i in range(2):
                            a = 8 * ((u // 4) % 2) + 2 * (u % 4) + i
                            o = S[u % 3][:, i * T:(i + 1) * T]
                            r = slice(64 * hg, 64 * hg + 64)
                            nc.tensor.matmul(o, q1[r, a, :, :], kTb[r, :], start=True, stop=False)
                            last = nc.tensor.matmul(o, q2[:, a, hg * HG:(hg + 1) * HG, :], px[:, (A - 1 - a) * J:(A - 1 - a) * J + T],
                                                    start=False, stop=True)
                        last.then_inc(s["scores"], 1)

                    def weigh(g):
                        pe.wait_ge(s["pt"], PAIRS * b + 4 * g + 4)
                        hg, i = g // 2, g % 2
                        for h in range(HG):
                            for t in range(HALVES):
                                o = (i * H + hg * HG + h) * VW
                                last = nc.tensor.matmul(O[:, o:o + VW], pTb[:, g % 2, t, h, :], vaug[:, t, hg * HG + h, :],
                                                        start=(t == 0), stop=(t == HALVES - 1))
                        last.then_inc(s["pv"], 1)

                    for u in range(3):
                        scores(u)
                    for u in range(PAIRS):
                        pe.wait_ge(s["sact"], PAIRS * b + u + 4)
                        if u >= 2:
                            pe.wait_ge(s["pt"], PAIRS * b + u - 1)
                        for t in range(HALVES):
                            for i in range(2):
                                o = PT[u % 2][:, t * T:(t + 1) * T].rearrange("p (h i j) -> p h i j", h=HG, i=2)[:, :, i, :]
                                last = nc.tensor.transpose(o,
                                                           prob[:, u % 2, i, t * P:(t + 1) * P], ident[:, :])
                        last.then_inc(s["pused"], 1)
                        if u + 3 < PAIRS:
                            scores(u + 3)
                        if u % 4 == 1 and u > 4:
                            weigh(u // 4 - 1)
                    weigh(3)
                    pe.wait_ge(s["on"], b + 1)
                    for i in range(HALVES):
                        last = nc.tensor.transpose(misc[0][:, i * P:(i + 1) * P], onrm[:, i, :], ident[:, :])
                    last.then_inc(s["tr"], 1)
                    pe.wait_ge(s["cp"], 4 * b + 4)
                    for i in range(HALVES):
                        last = nc.tensor.matmul(misc[1][:, i * P:(i + 1) * P], oT[:, i * P:(i + 1) * P], wpT[:, :], start=True, stop=True)
                    last.then_inc(s["y"], 1)

            @block.scalar
            def _(act):
                act.sem_inc(s["sact"], 3)
                act.wait_ge(s["vini"], 1)
                with act.Fori(0, BATCH) as b:
                    act.wait_ge(s["tr"], 4 * b + 1)
                    nc.scalar.copy(xT[:, :], misc[0][:, 0:T]).then_inc(s["cp"], 1)
                    act.wait_ge(s["tr"], 4 * b + 2)
                    nc.scalar.copy(qTb[:, :], misc[1][:, 0:T])
                    nc.scalar.copy(kTb[:, :], misc[1][:, T:2 * T]).then_inc(s["cp"], 1)
                    act.wait_ge(s["tr"], 4 * b + 3)
                    nc.scalar.copy(vaug[:, :, :, 0:HD].rearrange("p t h d -> p (t h) d"),
                                   misc[0][:, 0:T].rearrange("p (n d) -> p n d", d=HD)).then_inc(s["cp"], 1)
                    for u in range(PAIRS):
                        act.wait_ge(s["nmax"], PAIRS * b + u + 1)
                        act.wait_ge(s["pused"], PAIRS * b + u + 1)
                        for i in range(2):
                            last = nc.scalar.activation(prob[:, u % 2, i, :], S[u % 3][:, i * T:(i + 1) * T], ACT.Exp,
                                                        bias=nb[:, u % 2, i:i + 1], scale=SCALE_B)
                        last.then_inc(s["sact"], 1)
                    act.wait_ge(s["tr"], 4 * b + 4)
                    nc.scalar.copy(oT[:, :], misc[0][:, 0:T]).then_inc(s["cp"], 1)

            @block.vector
            def _(dve):
                own = Own(dve, s["own"])
                V = nc.vector
                V.memset(vaug[:, :, :, :], 1.0).then_inc(s["vini"], 1)
                V.tensor_copy(wqrep[:, :, :].rearrange("p h (j d) -> p h j d", d=HD),
                              wqT[:, :].rearrange("p (h d) -> p h d", d=HD).unsqueeze(2).to_broadcast([P, H, J, HD])).then_inc(s["yused"], 1)
                dve.sem_inc(s["sdve"], 3)
                with dve.Fori(0, BATCH) as b:
                    norm_dve(dve, own, b, s)
                    for r in range(H // 2):
                        dve.wait_ge(s["rep"], H // 2 * b + r + 1)
                        V.tensor_tensor(q2[:, :, 2 * r:2 * r + 2, :].rearrange("p a h j -> p h a j"),
                                        PT[r % 2][:, :].rearrange("p (h a j) -> p h a j", h=2, a=A),
                                        mask_h16[:, :].unsqueeze(1).unsqueeze(1).to_broadcast([P, 2, A, J]), ALU.mult).then_inc(s["q2"], 1)
                    dve.wait_ge(s["cp"], 4 * b + 2)
                    V.tensor_tensor(q1[:, :, :, :], qTb[:, :].rearrange("p (a j) -> p a j", j=J).unsqueeze(2).to_broadcast([P, A, HG, J]),
                                    mask_h8[:, :].unsqueeze(1).unsqueeze(3).to_broadcast([P, A, HG, J]), ALU.mult).then_inc(s["q1"], 1)

                    def copy_pt(u):
                        dve.wait_ge(s["pused"], PAIRS * b + u + 3)
                        if u % 4 == 0:
                            dve.wait_ge(s["pv"], 4 * b + u // 4 + 1)
                        V.tensor_copy(pTb[:, (u // 4) % 2, :, :, 2 * J * (u % 4):2 * J * (u % 4 + 1)],
                                      PT[u % 2][:, :].rearrange("p (t h r) -> p t h r", t=2, h=HG)).then_inc(s["pt"], 1)

                    for u in range(PAIRS):
                        dve.wait_ge(s["scores"], PAIRS * b + u + 1)
                        V.tensor_reduce(mxb[:, u % 2, :], S[u % 3][:, :].rearrange("p (i t) -> p i t", i=2), AX, ALU.max).then_inc(s["sdve"], 1)
                        dve.wait_ge(s["sdve"], PAIRS * b + u + 4)
                        V.tensor_scalar(nb[:, u % 2, :], mxb[:, u % 2, :], -SCALE_B, None, ALU.mult).then_inc(s["nmax"], 1)
                        if u >= 1:
                            copy_pt(u - 1)
                    copy_pt(PAIRS - 1)
                    dve.wait_ge(s["pv"], 4 * b + 6)
                    own.link(V.reciprocal(rinv[:, :], o_all[:, :, HD]))
                    V.tensor_tensor(onrm[:, :, :].rearrange("p i (h d) -> p (i h) d", d=HD), o_all[:, :, 0:HD],
                                    rinv[:, :].unsqueeze(2).to_broadcast([P, HALVES * H, HD]), ALU.mult).then_inc(s["on"], 1)
                    dve.wait_ge(s["y"], b + 1)
                    rows = xres[:, bass.ds(b * HALVES, HALVES), :]
                    V.tensor_tensor(rows, rows, misc[1][:, 0:T].rearrange("p (i d) -> p i d", i=HALVES), ALU.add).then_inc(s["yused"], 1)
                    dve.wait_ge(s["yused"], b + 2)
                    dve.sem_inc(s["gate2"], 1)
                    own.end()

        experts("f2")

        s_out = sem("s_out")
        with nc.Block() as block:
            @block.sync
            def _(sp):
                for c in range(4):
                    n = BATCH * HALVES // 4
                    sp.dma_start(out_dram[:, c * n:(c + 1) * n, :], xres[:, c * n:(c + 1) * n, :]).then_inc(s_out, 16)
                sp.wait_ge(s_out, 16 * 4)


_INS = ['L0_attn_a_x', 'L0_attn_a_W_qkv', 'L0_attn_a_b_qkv', 'L0_attn_a_W_out', 'L0_attn_a_b_out',
        'L0_attn_b_Wq', 'L0_attn_b_Wk', 'L0_attn_b_Wv', 'L0_attn_b_Wp', 'L0_attn_b_pos_emb_k',
        'L0_ffn_gate_w', 'L0_ffn_gate_bias', 'L0_ffn_w_gate', 'L0_ffn_w_up', 'L0_ffn_w_down',
        'L0_ffn_sh_gate', 'L0_ffn_sh_up', 'L0_ffn_sh_down']


def kernel(**inputs):
    import numpy as _np
    import concourse.bacc as _bacc
    from concourse import mybir as _mybir
    from concourse.bass_utils import run_bass_kernel_spmd as _run

    nc = _bacc.Bacc("TRN2", target_bir_lowering=False, num_devices=1)
    arrays, args = {}, []
    for name in _INS:
        a = _np.ascontiguousarray(inputs[name])
        arrays[f"in_{name}_dram"] = a
        args.append(nc.dram_tensor(f"in_{name}_dram", a.shape, _mybir.dt.from_np(a.dtype), kind="ExternalInput").ap())
    args.append(nc.dram_tensor("out_0_dram", (BATCH, T, D), _mybir.dt.float32, kind="ExternalOutput").ap())
    build(nc, *args)
    r = _run(nc, [arrays], core_ids=[0])
    return r.results[0]["out_0_dram"]
```

```python
import concourse.bass as bass
from concourse import mybir
from contextlib import ExitStack

BATCH, T, D = 32, 256, 128
P = 128
HALVES = T // P
H = 16
HD = D // H
TOPK = int(T * 0.3)
NE, NI = 32, 64
EB = NE * NI // P
NBLK = EB + 1
NG, GSZ = 8, NE // 8
REL = 128
PAD32 = 32
CH = H // 4
J = 16
A = T // J
HG = 8
VW = HD + 1
EPS = 1e-5
SCALE_A = float(D) ** -0.5
SCALE_B = float(HD) ** -0.5
ROUTED_SCALE = 2.5
GONE = -3.0e38
GONE_BELOW = -2.9e38


class Own:

    def __init__(self, eng, sem):
        self.eng, self.sem, self.n = eng, sem, 0

    def mark(self, ins):
        ins.then_inc(self.sem, 1)
        self.n += 1
        return self.n

    def need(self, n):
        self.eng.wait_ge(self.sem, n)

    def link(self, ins):
        self.need(self.mark(ins))

    def end(self):
        if self.n == 0:
            return
        self.need(self.n)
        self.eng.sem_clear(self.sem)
        self.n = 0


def build(nc, x, W_qkv, b_qkv, W_out, b_out, Wq, Wk, Wv, Wp, pos, gate_w, gate_bias,
          w_gate, w_up, w_down, sh_gate, sh_up, sh_down, out):
    f32 = mybir.dt.float32
    bf16 = mybir.dt.bfloat16
    ALU = mybir.AluOpType
    ACT = mybir.ActivationFunctionType
    AX = mybir.AxisListType.X
    ctx = ExitStack()
    with ctx:
        def sb(name, shape, dt=f32):
            return ctx.enter_context(nc.sbuf_tensor(name, shape, dt))

        def sem(name):
            return ctx.enter_context(nc.semaphore(name))

        bank = [ctx.enter_context(nc.psum_tensor(f"bank{i}", [P, 512], f32)) for i in range(8)]
        misc = bank[6:8]

        xres = sb("xres", [P, BATCH * HALVES, D])
        ident = sb("ident", [P, P])
        ones1 = sb("ones1", [1, P])
        wqkT = sb("wqkT", [P, 2, CH, P])
        bqk = sb("bqk", [P, 2, CH])
        wvT = sb("wvT", [P, D])
        bv = sb("bv", [1, D])
        woT = sb("woT", [P, D])
        bo = sb("bo", [1, D])
        wqT = sb("wqT", [P, D])
        wqT_a = sb("wqT_a", [P, D])
        wkT_a = sb("wkT_a", [P, D])
        wkT = sb("wkT", [P, D])
        wvbT = sb("wvbT", [P, D])
        wpT = sb("wpT", [P, D])
        px = sb("px", [P, T + (A - 1) * J])
        mask_h16 = sb("mask_h16", [P, H])
        mask_h8 = sb("mask_h8", [P, HG])
        gwT = sb("gwT", [P, NE])
        gbias = sb("gbias", [P, NE])
        wgT = sb("wgT", [P, NBLK, P])
        wuT = sb("wuT", [P, NBLK, P])
        wdT = sb("wdT", [P, NBLK, P])
        sel = sb("sel", [3 * NE, EB, P], bf16)
        ident16 = sb("ident16", [P, P], bf16)
        half_pow = sb("half_pow", [P, HALVES])
        eps_t = sb("eps_t", [P, HALVES])

        stats = sb("stats", [P, HALVES, 6])
        mv = sb("mv", [P, HALVES, 2])
        vareps = sb("vareps", [P, HALVES])
        rstd = sb("rstd", [P, HALVES])
        xn = sb("xn", [P, HALVES, D])
        xT = sb("xT", [P, T])
        mx = sb("mx", [P, HALVES, 8])
        nb = sb("nb", [P, 2, HALVES])
        work = sb("work", [P, HALVES, T])
        prob = sb("prob", [P, 2, HALVES, T])
        pT = sb("pT", [P, 2, HALVES, T])
        rinv = sb("rinv", [P, HALVES * H])
        onrm = sb("onrm", [P, HALVES, D])
        oT = sb("oT", [P, T])
        sctx = ctx.enter_context(ExitStack())

        def sb_setup(name, shape):
            return sctx.enter_context(nc.sbuf_tensor(name, shape, f32))

        stage = sb_setup("stage", [P, 3, EB, P])

        nat = sb_setup("nat", [P, 11, P])
        gnat = sb_setup("gnat", [NE, D])
        pnat = sb_setup("pnat", [P, 2, HD])
        pext = sb_setup("pext", [HD, 2 * T + J])

        s_ones = sem("s_ones")
        s_const = sem("s_const")
        s_w = sem("s_w")
        s_x = sem("s_x")
        s_tr = sem("s_tr")
        s_trc = sem("s_trc")
        s_rep = sem("s_rep")
        s_pext = sem("s_pext")
        s_px = sem("s_px")
        s_setv = sem("s_setv")

        b_cgd = b_qkv.rearrange("(w c g d) -> w g d c", w=3, c=CH, g=4)
        x_dram = x.rearrange("b (h p) d -> p (b h) d", p=P)
        out_dram = out.rearrange("b (h p) d -> p (b h) d", p=P)

        with nc.Block() as block:
            @block.sync
            def _(sp):
                sp.wait_ge(s_setv, 1)
                for i, w in enumerate((W_qkv[0:P, :], W_qkv[P:2 * P, :], W_qkv[2 * P:3 * P, :], W_out,
                                       Wq, Wk, Wv, Wp, sh_gate, sh_up, sh_down)):
                    sp.dma_start(nat[:, i, :], w).then_inc(s_w, 16)
                sp.dma_start(gnat[:, :], gate_w).then_inc(s_w, 16)
                sp.dma_start(pnat[:, :, :], pos.rearrange("(k p) d -> p k d", p=P)).then_inc(s_w, 16)
                sp.dma_start(bv[:, :], b_qkv[2 * D:3 * D].rearrange("(a n) -> a n", a=1)).then_inc(s_w, 16)
                sp.dma_start(bo[:, :], b_out.rearrange("(a n) -> a n", a=1)).then_inc(s_w, 16)
                sp.dma_start(gbias[:, :], gate_bias.rearrange("(a n) -> a n", a=1).to_broadcast([P, NE])).then_inc(s_w, 16)
                for w in range(2):
                    for g in range(4):
                        sp.dma_start(bqk[PAD32 * g:PAD32 * g + HD, w, :], b_cgd[w, g],
                                     allow_slow_non_contiguous=True).then_inc(s_w, 16)
                sp.dma_start(stage[:, 0], w_gate.rearrange("e i h -> (e i) h").rearrange("(k p) h -> p k h", p=P)).then_inc(s_w, 16)
                sp.dma_start(stage[:, 1], w_up.rearrange("e i h -> (e i) h").rearrange("(k p) h -> p k h", p=P)).then_inc(s_w, 16)
                sp.dma_start(stage[:, 2].rearrange("h k (e i) -> h (k e) i", e=2), w_down.rearrange("e h i -> h e i")).then_inc(s_w, 16)
                for c in range(4):
                    n = BATCH * HALVES // 4
                    sp.dma_start(xres[:, c * n:(c + 1) * n, :], x_dram[:, c * n:(c + 1) * n, :]).then_inc(s_x, 16)
                sp.wait_ge(s_pext, 1)
                for j in range(J):
                    sp.dma_start(px[HD * j:HD * j + HD, :], pext[:, J - 1 - j:J - 1 - j + T + (A - 1) * J]).then_inc(s_px, 16)
                sp.wait_ge(s_px, 16 * J)
                sp.wait_ge(s_x, 16 * 4)

            @block.gpsimd
            def _(pool):
                one = [
                    pool.memset(ident[:, :], 0.0), pool.memset(mask_h16[:, :], 1.0),
                    pool.memset(sel[:, :, :], 0.0), pool.memset(half_pow[:, :], -0.5), pool.memset(eps_t[:, :], EPS),
                    pool.memset(ones1[:, :], 1.0),
                ]
                one[-1].then_inc(s_ones, 1)
                pool.wait_ge(s_ones, 1)
                pool.affine_select(out=ident[:, :], in_=ident[:, :], compare_op=ALU.not_equal, fill=1.0, base=0,
                                   pattern=[[-1, P]], channel_multiplier=1)
                pool.affine_select(out=mask_h16[:, :], in_=mask_h16[:, :], compare_op=ALU.is_ge, fill=0.0, base=0,
                                   pattern=[[-HD, H]], channel_multiplier=1)
                for k in range(3):
                    pool.affine_select(out=sel[:, :, :], in_=sel[:, :, :], compare_op=ALU.not_equal, fill=1.0, base=-k * NE,
                                       pattern=[[-2, EB], [-1, 2], [0, NI]], channel_multiplier=1).then_inc(s_ones, 1)
                    pool.wait_ge(s_ones, k + 2)
                pool.tensor_copy(ident16[:, :], ident[:, :])
                pool.affine_select(out=mask_h16[:, :], in_=mask_h16[:, :], compare_op=ALU.is_ge, fill=0.0, base=HD - 1,
                                   pattern=[[HD, H]], channel_multiplier=-1).then_inc(s_const, 1)

            @block.tensor
            def _(pe):
                pe.wait_ge(s_const, 1)
                pe.wait_ge(s_w, 16 * 27)
                jobs = ([nat[:, i, :] for i in range(11)]
                        + [stage[:, w, k, :] for w in range(3) for k in range(EB)])
                for n, src in enumerate(jobs):
                    if n % 4 == 0 and n >= 16:
                        pe.wait_ge(s_trc, n // 4 - 3)
                    last = nc.tensor.transpose(bank[(n // 4) % 4][:, (n % 4) * P:(n % 4 + 1) * P], src, ident[:, :])
                    if n % 4 == 3 or n == len(jobs) - 1:
                        last.then_inc(s_tr, 1)
                nc.tensor.transpose(bank[4][:, 0:NE], gnat[:, :], ident[0:NE, 0:NE])
                for k in range(2):
                    last = nc.tensor.transpose(bank[4][0:HD, 64 + k * P:64 + (k + 1) * P], pnat[:, k, :], ident[:, :])
                last.then_inc(s_tr, 1)

            @block.vector
            def _(dve):
                own = Own(dve, sem("set_own"))
                nc.vector.memset(bqk[:, :, :], 0.0).then_inc(s_setv, 1)
                own.link(nc.vector.memset(wqkT[:, :, :, :], 0.0))
                NJ = 11 + 3 * EB
                flat = [wgT, wuT, wdT]

                def put(n, src):
                    if n < 2:
                        nc.vector.tensor_copy((wqT_a, wkT_a)[n][:, :], src)
                        o = wqkT[:, n, :, :].rearrange("p c (g e) -> p (c g) e", g=4)[:, :, 0:HD]
                        return nc.vector.tensor_copy(o, src.rearrange("p (h d) -> p h d", d=HD))
                    o = {2: wvT[:, :], 3: woT[:, :], 4: wqT[:, :], 5: wkT[:, :], 6: wvbT[:, :], 7: wpT[:, :],
                         8: wgT[:, EB, :], 9: wuT[:, EB, :], 10: wdT[:, EB, :]}.get(n)
                    if n == 10:
                        return nc.vector.tensor_scalar(o, src, 0.5, None, ALU.mult)
                    if o is None:
                        o = flat[(n - 11) // EB][:, (n - 11) % EB, :]
                    return nc.vector.tensor_copy(o, src)

                for n in range(NJ):
                    if n % 4 == 0:
                        dve.wait_ge(s_tr, n // 4 + 1)
                    last = put(n, bank[(n // 4) % 4][:, (n % 4) * P:(n % 4 + 1) * P])
                    if n % 4 == 3 or n == NJ - 1:
                        last.then_inc(s_trc, 1)
                dve.wait_ge(s_tr, (NJ + 3) // 4 + 1)
                nc.vector.tensor_copy(gwT[:, :], bank[4][:, 0:NE])
                mid = T - J + (J - 1) - REL
                own.mark(nc.vector.tensor_scalar(pext[:, mid:mid + REL], bank[4][0:HD, 64 + P:64 + 2 * P], 2.0, None, ALU.mult))
                own.link(nc.vector.tensor_scalar(pext[:, mid + REL:mid + 2 * REL], bank[4][0:HD, 64:64 + P], 2.0, None, ALU.mult))
                nc.vector.tensor_copy(pext[:, 0:mid], pext[:, mid:mid + 1].to_broadcast([HD, mid]))
                tail = 2 * T + J - mid - 2 * REL
                nc.vector.tensor_copy(pext[:, mid + 2 * REL:], pext[:, mid + 2 * REL - 1:mid + 2 * REL].to_broadcast([HD, tail])).then_inc(s_pext, 1)
                dve.wait_ge(s_const, 1)
                nc.vector.tensor_tensor(mask_h8[:, :], mask_h16[:, 0:HG], mask_h16[:, HG:H], ALU.add)
                dve.wait_ge(s_trc, (NJ + 3) // 4)

        def sems(tag, names):
            return {n: sem(f"{tag}_{n}") for n in names.split()}

        sctx.close()

        GT = 16
        GROUPS = BATCH * 2
        NB4 = 4
        TARGET = TOPK - 8
        Z0, DENS = 0.626, 0.328
        GAIN = (0.7, 0.5)
        actx = ctx.enter_context(ExitStack())

        def sb_a(name, shape, dt=f32):
            return actx.enter_context(nc.sbuf_tensor(name, shape, dt))

        q4 = sb_a("q4", [P, 2, CH, T])
        k4 = sb_a("k4", [P, 2, CH, T])
        vaug4 = sb_a("vaug4", [P, 2, HALVES, H, PAD32])
        kept = sb_a("kept", [P, NB4, GT, T])
        xTc = sb_a("xTc", [P, T])
        xsum = sb_a("xsum", [P, 2])
        ktok = sb_a("ktok", [P, HALVES, D])
        qtok = sb_a("qtok", [P, HALVES, D])
        qnat = sb_a("qnat", [P, T])
        gram = sb_a("gram", [P, D])
        prod = sb_a("prod", [P, HALVES * H, HD])
        sig = sb_a("sig", [P, 2, H, HALVES])
        var = sb_a("var", [P, HALVES * H])
        per_rank = sb_a("per_rank", [P, 2, H, HALVES])
        neg_first = sb_a("neg_first", [P, 2, H, HALVES])
        row_max = sb_a("row_max", [P, NB4, GT])
        exp_bias = sb_a("exp_bias", [P, NB4, GT])
        acc = sb_a("acc", [P, 3, NB4, GT])
        neg_thr = sb_a("neg_thr", [P, 2, GT])
        tmp = sb_a("tmp", [P, GT])
        shift = sb_a("shift", [P, GT])
        upper_t = sb_a("upper_t", [P, 2, GT])
        rank = sb_a("rank", [P, 2, GT])
        osum = sb_a("osum", [P, 2, T])
        rinv8 = sb_a("rinv8", [P, HALVES, 8])
        below = sb_a("below", [P, 2, T])
        sixteen = sb_a("sixteen", [P, GT, 16])
        iota = sb_a("iota", [P, GT, 15])
        oh = sb_a("oh", [P, GT, 15])
        pick = sb_a("pick", [P, GT, 15])
        nxt = sb_a("nxt", [P, GT])
        mid = sb_a("mid", [P, NB4, GT])
        fine = sb_a("fine", [P, NB4, GT])
        fail = sb_a("fail", [P, GT])
        flags = sb_a("flags", [1, GT + 1], mybir.dt.int32)
        junk = sb_a("junk", [P, 2, T], mybir.dt.bfloat16)
        ring = sb_a("ring", [P, 4, HALVES, T])
        bnat = sb_a("bnat", [P, 1])
        bq = sb_a("bq", [1, D])
        ones128 = sb_a("ones128", [P, 1])
        half_p = sb_a("half_p", [P, HALVES * H])
        mask_bd = sb_a("mask_bd", [P, H, HD])

        s = sems("a", "mv rstd xn m0 m0c m1 m1c var sig scores evac signs u0 u1 u2 failed okay "
                      "exp p pused pt pv on own aown pown slow oc gate pgate upper ini inid")
        S = bank[0:3]
        PT = bank[3:5]
        O = bank[5]
        o_all = O[:, 0:HALVES * H * VW].rearrange("p (n w) -> p n w", w=VW)

        def runs(t, lag=0, n=GROUPS):
            return not isinstance(t, int) or 0 <= t - lag < n

        def wait(eng, sm, v):
            if not (isinstance(v, int) and v <= 0):
                eng.wait_ge(sm, v)

        M0, M1 = misc
        USES = ({"v": 0, "xT": -1, "oT": 2, "q0": -1, "q1": -1, "k0": -1, "k1": -1, "qn": -1},
                {"f0": 1, "n0": 2, "y": 2, "f1": 1, "n1": 1, "ktok": -1, "qtok": -1, "gram": -1, "mom": -1})

        def before(m, b, what):
            order = USES[m]
            first = sum(lag == -1 for lag in order.values())
            if not isinstance(b, int):
                return b * len(order) + first - sum(max(lag, 0) for lag in order.values()) + list(order).index(what)
            n = first
            for c in range(b + 1):
                for o, lag in order.items():
                    if c == b and o == what:
                        return n
                    n += 0 <= c - lag < BATCH

        SIGNS = {"c1": 0, "c2": 0, "c3": 0}

        def signs(t, what, tiles=GT):
            if not isinstance(t, int):
                return (t * len(SIGNS) + list(SIGNS).index(what)) * GT + tiles
            n = 0
            for c in range(t + 1):
                for o, lag in SIGNS.items():
                    if c == t and o == what:
                        return n + tiles
                    n += GT * (0 <= c - lag < GROUPS)

        def m0_before(b, what):
            return before(0, b, what)

        def m1_before(b, what):
            return before(1, b, what)

        BODY = (1, BATCH // 2 - 1)

        def schedule(eng, step):
            step(-1, -1, 3)
            for u in range(4):
                step(u, 0, u)
            with eng.Fori(*BODY) as i:
                for u in range(4):
                    step(i * 4 + u, i * 2 + u // 2, u)
            for i in (BODY[1], BODY[1] + 1):
                for u in range(4):
                    if 4 * i + u <= GROUPS + 2:
                        step(4 * i + u, 2 * i + u // 2, u)

        with nc.Block() as block:
            @block.gpsimd
            def _(pool):
                own = Own(pool, s["pown"])
                pool.memset(half_p[:, :], 0.5)
                pool.memset(ones128[:, :], 1.0)
                pool.memset(mask_bd[:, :, :], 1.0).then_inc(s["ini"], 1)
                pool.wait_ge(s["ini"], 1)
                pool.affine_select(out=mask_bd[:, :, :], in_=mask_bd[:, :, :], compare_op=ALU.is_ge, fill=0.0, base=0,
                                   pattern=[[-HD, H], [0, HD]], channel_multiplier=1).then_inc(s["ini"], 1)
                pool.iota(iota[:, :, :], [[0, GT], [1, 15]], base=1, channel_multiplier=0,
                          allow_small_or_imprecise_dtypes=True)
                pool.wait_ge(s["ini"], 2)
                pool.affine_select(out=mask_bd[:, :, :], in_=mask_bd[:, :, :], compare_op=ALU.is_ge, fill=0.0, base=HD - 1,
                                   pattern=[[HD, H], [0, HD]], channel_multiplier=-1).then_inc(s["ini"], 1)

                def front(b):
                    pool.wait_ge(s["mv"], b + 1)
                    own.link(pool.tensor_tensor(vareps[:, :], mv[:, :, 1], eps_t[:, :], ALU.add))
                    pool.tensor_tensor(rstd[:, :], vareps[:, :], half_pow[:, :], ALU.pow).then_inc(s["rstd"], 1)

                def guess(b, par):
                    pool.wait_ge(s["var"], b + 1)
                    own.link(pool.tensor_tensor(sig[:, par, :, :].rearrange("p h i -> p i h"), var[:, :].rearrange("p (i h) -> p i h", i=HALVES),
                                                half_p[:, :].rearrange("p (i h) -> p i h", i=HALVES), ALU.pow))
                    pool.tensor_scalar(per_rank[:, par, :, :], sig[:, par, :, :], 1.0 / (T ** 0.5 * T * DENS), None, ALU.mult)
                    own.link(pool.tensor_scalar(neg_first[:, par, :, :], sig[:, par, :, :], -Z0 / T ** 0.5, None, ALU.mult))
                    pool.sem_inc(s["u0"], 2)

                front(0)
                guess(0, 0)
                own.end()

                def step(t, b, u):
                    par, even = u // 2 % 2, u % 2 == 0
                    bb = t // 2 if isinstance(t, int) else b
                    ahead = not isinstance(bb, int) or 0 <= bb < BATCH - 1

                    def move(k, done, prev, out):
                        wait(pool, s["signs"], signs(t, ("c1", "c2")[k]))
                        kp = per_rank[:, par, 8 * (u % 2):8 * (u % 2) + 8, :].rearrange("p h i -> p (h i)")
                        pool.sem_inc(s["pgate"], 1)
                        own.link(pool.tensor_scalar(shift[:, :], acc[:, k, u, :], float(T - 2 * TARGET), -0.5 * GAIN[k], ALU.add, ALU.mult))
                        own.link(pool.tensor_tensor(shift[:, :], shift[:, :], kp, ALU.mult))
                        pool.tensor_tensor(out, prev, shift[:, :], ALU.add).then_inc(s[done], 1)
                        pool.wait_ge(s[done], t + 1)

                    if runs(t, 1):
                        wait(pool, s["signs"], signs(t - 1, "c3"))
                        pool.sem_inc(s["pgate"], 1)
                        own.mark(pool.tensor_scalar(upper_t[:, u % 2, :], neg_thr[:, 1, :], -1.0, None, ALU.mult))
                        own.link(pool.tensor_scalar(rank[:, u % 2, :], acc[:, 2, (u + 3) % 4, :], -0.5, float(TOPK - T // 2), ALU.mult, ALU.add))
                        pool.sem_inc(s["upper"], 1)
                    if even and ahead:
                        front(bb + 1)
                    if runs(t):
                        move(0, "u1", neg_first[:, par, 8 * (u % 2):8 * (u % 2) + 8, :].rearrange("p h i -> p (h i)"), neg_thr[:, 0, :])
                        move(1, "u2", neg_thr[:, 0, :], neg_thr[:, 1, :])
                    if not even and ahead:
                        guess(bb + 1, (par + 1) % 2)
                    if u == 3:
                        own.end()

                schedule(pool, step)

            @block.sync
            def _(sp):
                sp.dma_start(bnat[:, :], b_qkv[0:D].rearrange("(n a) -> n a", a=1), allow_slow_non_contiguous=True).then_inc(s["inid"], 16)
                sp.dma_start(bq[:, :], b_qkv[0:D].rearrange("(a n) -> a n", a=1)).then_inc(s["inid"], 16)
                sp.wait_ge(s["inid"], 32)

            @block.tensor
            def _(pe):
                pe.wait_ge(s["ini"], 3)
                pe.wait_ge(s["inid"], 32)

                def use0(n):
                    wait(pe, s["m0c"], n)

                def use1(n):
                    wait(pe, s["m1c"], n)

                def turn_x(b, n):
                    pe.wait_ge(s["xn"], b + 1)
                    use0(n)
                    for h in range(HALVES):
                        last = nc.tensor.transpose(M0[:, h * P:(h + 1) * P], xn[:, h, :], ident[:, :])
                    last.then_inc(s["m0"], 1)

                def project(m, n):
                    use0(n)
                    for j in range(2):
                        last = nc.tensor.matmul(M0[:, j * T:(j + 1) * T], wqkT[:, m // 2, 2 * (m % 2) + j, :],
                                                (xT if m < 2 else xTc)[:, :], start=True, stop=True)
                    last.then_inc(s["m0"], 1)

                def values(n):
                    use0(n)
                    for h in range(HALVES):
                        nc.tensor.matmul(M0[:, h * P:(h + 1) * P], xT[:, h * P:(h + 1) * P], wvT[:, :], start=True, stop=False)
                        last = nc.tensor.matmul(M0[:, h * P:(h + 1) * P], ones1[:, :], bv[:, :], start=False, stop=True)
                    last.then_inc(s["m0"], 1)

                def queries(n):
                    use0(n)
                    nc.tensor.matmul(M0[:, 0:T], wqT_a[:, :], xT[:, :], start=True, stop=True).then_inc(s["m0"], 1)

                def k_rows(n):
                    use1(n)
                    for h in range(HALVES):
                        last = nc.tensor.matmul(M1[:, h * P:(h + 1) * P], xTc[:, h * P:(h + 1) * P], wkT_a[:, :], start=True, stop=True)
                    last.then_inc(s["m1"], 1)

                def q_rows(n):
                    use1(n)
                    for h in range(HALVES):
                        nc.tensor.matmul(M1[:, h * P:(h + 1) * P], xT[:, h * P:(h + 1) * P], wqT_a[:, :], start=True, stop=False)
                        last = nc.tensor.matmul(M1[:, h * P:(h + 1) * P], ones1[:, :], bq[:, :], start=False, stop=True)
                    last.then_inc(s["m1"], 1)

                def moments(n):
                    use1(n)
                    for h in range(HALVES):
                        last = nc.tensor.matmul(M1[:, 0:P], ktok[:, h, :], ktok[:, h, :], start=(h == 0), stop=(h == HALVES - 1))
                    last.then_inc(s["m1"], 1)

                def spreads(n):
                    use1(n)
                    for h in range(HALVES):
                        last = nc.tensor.matmul(M1[:, h * P:(h + 1) * P], qnat[:, h * P:(h + 1) * P], gram[:, :], start=True, stop=True)
                    last.then_inc(s["m1"], 1)

                turn_x(0, 0)
                for m in range(4):
                    project(m, m + 1)
                queries(5)
                wait(pe, s["m0c"], 6)
                for n, f in enumerate((k_rows, q_rows, moments, spreads)):
                    f(n)

                def scores(t, h, u):
                    g = 8 * (u % 2) + h
                    par = u // 2 % 2
                    wait(pe, s["evac"], GT * t + (-2, 0)[h] if h < 2 else GT * t + 2 * h - 4)
                    r = slice(PAD32 * (g % 4), PAD32 * (g % 4) + HD)
                    for i in range(HALVES):
                        last = nc.tensor.matmul(S[h % 3][:, i * T:(i + 1) * T], q4[r, par, g // 4, i * P:(i + 1) * P],
                                                k4[r, par, g // 4, :], start=True, stop=True)
                    last.then_inc(s["scores"], 1)

                scores(0, 0, 0)
                scores(0, 1, 0)

                def step(t, b, u):
                    even = u % 2 == 0
                    bb = t // 2 if isinstance(t, int) else b
                    front = not isinstance(bb, int) or 0 <= bb < BATCH - 1

                    if runs(t, 2):
                        wait(pe, s["failed"], t - 1)
                        use1(m1_before(bb, "f0" if even else "f1"))
                        nc.tensor.matmul(M1[0:1, 0:GT], ones128[:, :], fail[:, :], start=True, stop=True).then_inc(s["m1"], 1)

                    def turn(h):
                        wait(pe, s["p"], 8 * (t - 2) + h + 1)
                        for i in range(HALVES):
                            for k in range(HALVES):
                                last = nc.tensor.transpose(PT[h % 2][:, k * T + i * P:k * T + (i + 1) * P],
                                                           prob[:, h % 2, i, k * P:(k + 1) * P], ident[:, :])
                        last.then_inc(s["pused"], 1)

                    def weigh(h):
                        g = 8 * (u % 2) + h
                        wait(pe, s["pt"], 8 * (t - 2) + h + 1)
                        if h == 0:
                            wait(pe, s["oc"], t - 2)
                        for k in range(HALVES):
                            last = nc.tensor.matmul(O[PAD32 * (h % 4):PAD32 * (h % 4 + 1), (h // 4) * T:(h // 4 + 1) * T],
                                                    vaug4[:, (u // 2 + 1) % 2, k, g, :], pT[:, h % 2, k, :],
                                                    start=(k == 0), stop=(k == HALVES - 1), tile_position=(0, PAD32 * (h % 4)))
                        last.then_inc(s["pv"], 1)

                    def turn_sums():
                        wait(pe, s["oc"], t - 2)
                        use1(m1_before(bb, "n0" if even else "n1"))
                        for i in range(HALVES):
                            for c in range(2):
                                last = nc.tensor.transpose(M1[:, (i * 2 + c) * P:(i * 2 + c + 1) * P], osum[:, c, i * P:(i + 1) * P], ident[:, :])
                        last.then_inc(s["m1"], 1)

                    def turn_o():
                        pe.wait_ge(s["on"], t - 2)
                        use0(m0_before(bb, "oT"))
                        for i in range(HALVES):
                            last = nc.tensor.transpose(M0[:, i * P:(i + 1) * P], onrm[:, i, :], ident[:, :])
                        last.then_inc(s["m0"], 1)

                    def project_o():
                        wait(pe, s["m0c"], m0_before(bb, "oT") + 1)
                        use1(m1_before(bb, "y"))
                        for i in range(HALVES):
                            nc.tensor.matmul(M1[:, i * P:(i + 1) * P], oT[:, i * P:(i + 1) * P], woT[:, :], start=True, stop=False)
                            last = nc.tensor.matmul(M1[:, i * P:(i + 1) * P], ones1[:, :], bo[:, :], start=False, stop=True)
                        last.then_inc(s["m1"], 1)

                    tail = runs(bb, 2, BATCH)
                    for h in range(8):
                        if h + 2 < 8 and runs(t, -1):
                            scores(t + 1, h + 2, u + 1)
                        if runs(t, 2) and h >= 1:
                            turn(h - 1)
                        if even:
                            if h == 0 and runs(bb, 0, BATCH):
                                values(m0_before(bb, "v"))
                            if h == 2 and front:
                                turn_x(bb + 1, m0_before(bb, "xT"))
                            if h == 3 and tail:
                                turn_o()
                            if h == 5 and tail:
                                project_o()
                            if front:
                                for m in ({4: (0, 1), 5: (2,), 6: (3,)}.get(h, ())):
                                    project(m, m0_before(bb, ("q0", "q1", "k0", "k1")[m]))
                                if h == 7:
                                    queries(m0_before(bb, "qn"))
                        elif front and 2 <= h <= 5:
                            if h == 2:
                                wait(pe, s["m0c"], m0_before(bb, "qn") + 1)
                            (k_rows, q_rows, moments, spreads)[h - 2](m1_before(bb, ("ktok", "qtok", "gram", "mom")[h - 2]))
                        if h == 1 and runs(t, 3):
                            turn_sums()
                        if runs(t, 2) and h >= 2:
                            weigh(h - 2)
                    if even and front:
                        wait(pe, s["m0c"], m0_before(bb, "k1") + 1)
                    if runs(t, 2):
                        turn(7)
                    if runs(t, -2):
                        scores(t + 2, 0, u + 2)
                    if runs(t, 2):
                        weigh(6)
                    if runs(t, -2):
                        scores(t + 2, 1, u + 2)
                    if runs(t, 2):
                        weigh(7)

                schedule(pe, step)

            @block.scalar
            def _(act):
                own = Own(act, s["aown"])
                act.wait_ge(s["inid"], 32)

                def take_x(n):
                    wait(act, s["m0"], n + 1)
                    own.link(nc.scalar.activation(xT[:, :], M0[:, 0:T], ACT.Copy, accum_out=xsum[:, 0:1]))
                    own.link(nc.scalar.mul(xsum[:, 1:2], xsum[:, 0:1], -1.0 / T))
                    nc.scalar.activation(xTc[:, :], xT[:, :], ACT.Identity, bias=xsum[:, 1:2]).then_inc(s["m0c"], 1)

                def take_q(m, par, n):
                    wait(act, s["m0"], n + 1)
                    for j in range(2):
                        c = 2 * (m % 2) + j
                        if m < 2:
                            last = nc.scalar.activation(q4[:, par, c, :], M0[:, j * T:(j + 1) * T], ACT.Identity, bias=bqk[:, 0, c:c + 1])
                    if m >= 2:
                        last = nc.scalar.copy(k4[:, par, 2 * (m % 2):2 * (m % 2) + 2, :].rearrange("p c t -> p (c t)"), M0[:, :])
                    last.then_inc(s["m0c"], 1)

                def take_v(slot, n):
                    wait(act, s["m0"], n + 1)
                    nc.scalar.copy(vaug4[:, slot, :, :, 0:HD].rearrange("p t h d -> p (t h) d"),
                                   M0[:, 0:T].rearrange("p (n d) -> p n d", d=HD)).then_inc(s["m0c"], 1)

                def take_qn(n):
                    wait(act, s["m0"], n + 1)
                    nc.scalar.activation(qnat[:, :], M0[:, 0:T], ACT.Identity, bias=bnat[:, 0:1]).then_inc(s["m0c"], 1)

                take_x(0)
                for m in range(4):
                    take_q(m, 0, m + 1)
                take_qn(5)
                own.end()

                def exponentials(t, h, u):
                    wait(act, s["p"], 8 * (t - 2) + h - 3)
                    for i in range(HALVES):
                        c = 2 * h + i
                        last = nc.scalar.activation(ring[:, h % 4, i, :], kept[:, (u + 2) % 4, c, :], ACT.Exp,
                                                    bias=exp_bias[:, (u + 2) % 4, c:c + 1], scale=SCALE_A)
                    last.then_inc(s["exp"], 1)

                def step(t, b, u):
                    par, even = u // 2 % 2, u % 2 == 0
                    bb = t // 2 if isinstance(t, int) else b
                    front = not isinstance(bb, int) or 0 <= bb < BATCH - 1

                    def count(tt, k, uu, bias, ready, done, part=range(GT)):
                        if part[0] == 0:
                            wait(act, s[ready], tt + 1)
                        for c in part:
                            wait(act, s["signs"], signs(t, done, c) - 1)
                            nc.scalar.activation(junk[:, c % 2, :], kept[:, uu % 4, c, :], ACT.Sign, bias=bias(c),
                                                 accum_out=acc[:, k, uu % 4, c:c + 1]).then_inc(s["signs"], 1)

                    if runs(t, 3):
                        wait(act, s["pv"], 8 * (t - 2))
                        nc.scalar.copy(osum[:, :, :].rearrange("p c i -> p (c i)"), O[:, :]).then_inc(s["oc"], 1)

                    def copy_pt(h):
                        wait(act, s["pused"], 8 * (t - 2) + h + 1)
                        wait(act, s["pv"], 8 * (t - 2) + h - 1)
                        nc.scalar.copy(pT[:, h % 2, :, :].rearrange("p t i -> p (t i)"), PT[h % 2][:, :]).then_inc(s["pt"], 1)

                    PASS = (("u0", "c1", lambda c: neg_first[:, par, 8 * (u % 2) + c // 2, c % 2:c % 2 + 1]),
                            ("u1", "c2", lambda c: neg_thr[:, 0, c:c + 1]),
                            ("u2", "c3", lambda c: neg_thr[:, 1, c:c + 1]))
                    CUTS = ((0, 6, 11, 16), (0, 5, 11, 16), (0, 5, 10, 16))
                    for h in range(9):
                        if h < 8 and h > 0 and runs(t, 2):
                            exponentials(t, h, u)
                        if runs(t):
                            k, j = h // 3, h % 3
                            ready, done, bias = PASS[k]
                            if h == 0:
                                wait(act, s["evac"], GT * t + GT)
                            count(t, k, u, bias, ready, done, range(CUTS[k][j], CUTS[k][j + 1]))
                        if h == 0 and runs(t, 2):
                            wait(act, s["okay"], t - 1)
                            exponentials(t, 0, u)
                        if h == 0 and even and runs(bb, 0, BATCH):
                            take_v(par, m0_before(bb, "v"))
                        if h >= 1 and runs(t, 2):
                            copy_pt(h - 1)
                        if even and front:
                            if h == 2:
                                take_x(m0_before(bb, "xT"))
                        if even and h == 3 and runs(bb, 2, BATCH):
                            wait(act, s["m0"], m0_before(bb, "oT") + 1)
                            nc.scalar.copy(oT[:, :], M0[:, 0:T]).then_inc(s["m0c"], 1)
                        if even and front:
                            for m in ({4: (0, 1), 5: (2,), 6: (3,)}.get(h, ())):
                                take_q(m, (par + 1) % 2, m0_before(bb, ("q0", "q1", "k0", "k1")[m]))
                            if h == 7:
                                take_qn(m0_before(bb, "qn"))
                    if u == 3:
                        own.end()

                schedule(act, step)

            @block.vector
            def _(dve):
                own = Own(dve, s["own"])
                V = nc.vector
                va = vaug4[:, :, :, :, :].rearrange("p a t h w -> p (a t h) w")
                own.link(V.memset(va, 0.0))
                own.link(V.memset(va[:, :, HD:VW], 1.0))
                dve.wait_ge(s["ini"], 3)

                def statistics(b):
                    for h in range(HALVES):
                        n = own.mark(V.bn_stats(stats[:, h, :], xrow(b, h)))
                    own.need(n)
                    for h in range(HALVES):
                        n = V.bn_aggr(mv[:, h, :], stats[:, h, :])
                    n.then_inc(s["mv"], 1)

                def xrow(b, h):
                    if isinstance(b, int):
                        return xres[:, b * HALVES + h, :]
                    return xres[:, bass.ds(b * HALVES + h, 1), :].rearrange("p a d -> p (a d)")

                def normed(b):
                    dve.wait_ge(s["rstd"], b + 1)
                    for h in range(HALVES):
                        n = V.tensor_scalar(xn[:, h, :], xrow(b, h), mv[:, h, 0:1], rstd[:, h:h + 1], ALU.subtract, ALU.mult)
                    n.then_inc(s["xn"], 1)

                def take_k(n):
                    wait(dve, s["m1"], n + 1)
                    V.tensor_copy(ktok[:, :, :].rearrange("p i d -> p (i d)"), M1[:, 0:T]).then_inc(s["m1c"], 1)

                def take_qr(n):
                    wait(dve, s["m1"], n + 1)
                    V.tensor_copy(qtok[:, :, :].rearrange("p i d -> p (i d)"), M1[:, 0:T]).then_inc(s["m1c"], 1)

                def take_g(n):
                    wait(dve, s["m1"], n + 1)
                    V.tensor_tensor(gram[:, :], M1[:, 0:P], mask_bd[:, :, :].rearrange("p h d -> p (h d)"), ALU.mult).then_inc(s["m1c"], 1)

                def take_mom(b, n):
                    wait(dve, s["m1"], n + 1)
                    wait(dve, s["m1c"], n - 1)
                    V.tensor_tensor(prod[:, :, :].rearrange("p n d -> p (n d)"), M1[:, 0:T], qtok[:, :, :].rearrange("p i d -> p (i d)"),
                                    ALU.mult).then_inc(s["m1c"], 1)
                    wait(dve, s["m1c"], n + 1)
                    own.link(V.tensor_reduce(var[:, :], prod[:, :, :], AX, ALU.add))
                    V.tensor_scalar(var[:, :], var[:, :], 0.0, None, ALU.max).then_inc(s["var"], 1)

                statistics(0)
                normed(0)
                for n, f in enumerate((take_k, take_qr, take_g)):
                    f(n)
                take_mom(0, 3)
                own.end()

                def step(t, b, u):
                    par, even = u // 2 % 2, u % 2 == 0
                    bb = t // 2 if isinstance(t, int) else b
                    front = not isinstance(bb, int) or 0 <= bb < BATCH - 1
                    tail = runs(bb, 2, BATCH)
                    z1 = (u + 3) % 4
                    z2 = (u + 2) % 4

                    def evac(h):
                        if not runs(t, -1):
                            return
                        wait(dve, s["scores"], 8 * (t + 1) + h + 1)
                        for i in range(HALVES):
                            c = 2 * h + i
                            V.tensor_scalar(kept[:, (u + 1) % 4, c, :], S[h % 3][:, i * T:(i + 1) * T], 1.0, -3.0e38, ALU.mult, ALU.max,
                                            accum_out=row_max[:, (u + 1) % 4, c:c + 1]).then_inc(s["evac"], 1)
                        if h == 7:
                            wait(dve, s["evac"], GT * (t + 1) + GT)
                            own.mark(V.tensor_scalar(exp_bias[:, (u + 1) % 4, :], row_max[:, (u + 1) % 4, :], -SCALE_A, None, ALU.mult))

                    def judge():
                        V.tensor_scalar(fail[:, :], fine[:, z2, :], -1.0, 1.0, ALU.mult, ALU.add).then_inc(s["failed"], 1)

                    taken = [0]

                    def largest(p):
                        if not runs(t, 1):
                            return
                        if p > 0:
                            own.need(taken[0])
                        for i in range(2):
                            c = 2 * p + i
                            n = own.mark(V.scalar_tensor_tensor(below[:, i, :], kept[:, z1, c, :], upper_t[:, u % 2, c:c + 1], kept[:, z1, c, :],
                                                                ALU.is_le, ALU.mult))
                        for i in range(2):
                            own.need(n - 1 + i)
                            m = own.mark(V.max(sixteen[:, 2 * p + i, 0:8], below[:, i, :]))
                        for i in range(2):
                            own.need(m - 1 + i)
                            n = own.mark(V.match_replace(below[:, i, :], sixteen[:, 2 * p + i, 0:8], below[:, i, :], GONE))
                        for i in range(2):
                            own.need(n - 1 + i)
                            m = own.mark(V.max(sixteen[:, 2 * p + i, 8:16], below[:, i, :]))
                        taken[0] = m

                    def normalise():
                        n1 = m1_before(bb, "n0" if even else "n1")
                        wait(dve, s["m1"], n1 + 1)
                        sums = M1[:, :].rearrange("p (i h w) -> p i h w", i=HALVES, h=8)
                        own.link(V.reciprocal(rinv8[:, :, :], sums[:, :, :, HD]))
                        q = 8 * ((u + 1) % 2)
                        V.tensor_tensor(onrm[:, :, :].rearrange("p i (h d) -> p i h d", d=HD)[:, :, q:q + 8, :], sums[:, :, :, 0:HD],
                                        rinv8[:, :, :].unsqueeze(3).to_broadcast([P, HALVES, 8, HD]), ALU.mult).then_inc(s["m1c"], 1)
                        wait(dve, s["m1c"], n1 + 1)
                        dve.sem_inc(s["on"], 1)

                    def check_flags():
                        n1 = m1_before(bb, "f0" if even else "f1")
                        wait(dve, s["m1"], n1 + 1)
                        V.tensor_copy(flags[:, 0:GT], M1[0:1, 0:GT]).then_inc(s["m1c"], 1)
                        wait(dve, s["m1c"], n1 + 1)
                        own.link(V.tensor_reduce(flags[:, GT:GT + 1], flags[:, 0:GT], AX, ALU.max))
                        redo(dve, V, z2)
                        dve.sem_inc(s["okay"], 1)

                    def probabilities(h):
                        if not runs(t, 2):
                            return
                        wait(dve, s["exp"], 8 * (t - 2) + h + 1)
                        wait(dve, s["pused"], 8 * (t - 2) + h - 1)
                        for i in range(HALVES):
                            c = 2 * h + i
                            n = V.scalar_tensor_tensor(prob[:, h % 2, i, :], kept[:, z2, c, :], mid[:, z2, c:c + 1], ring[:, h % 4, i, :],
                                                       ALU.is_ge, ALU.mult)
                        n.then_inc(s["p"], 1)

                    if even and front:
                        statistics(bb + 1)
                    if runs(t, 2):
                        judge()
                    for h in range(8):
                        evac(h)
                        if h == 0 and runs(t, 1):
                            wait(dve, s["upper"], t)
                        if h == 0 and runs(t, 1):
                            dve.sem_inc(s["gate"], 1)
                            largest(0)
                        if h == 0 and runs(t, 2):
                            check_flags()
                        if h == 1 and even and front:
                            normed(bb + 1)
                        if h >= 1:
                            probabilities(h - 1)
                            largest(h)
                        if h == 1 and runs(t, 3):
                            normalise()
                        if front and not even:
                            if h in (2, 3, 4):
                                (take_k, take_qr, take_g)[h - 2](m1_before(bb, ("ktok", "qtok", "gram")[h - 2]))
                            elif h == 5:
                                take_mom(bb + 1, m1_before(bb, "mom"))
                        if h == 6 and even and tail:
                            wait(dve, s["m1"], m1_before(bb, "y") + 1)
                            for i in range(HALVES):
                                n = V.tensor_tensor(xrow(bb - 2, i), xrow(bb - 2, i), M1[:, i * P:(i + 1) * P], ALU.add)
                            n.then_inc(s["m1c"], 1)
                    if runs(t, 1):
                        own.need(own.n)
                        n = own.mark(V.tensor_tensor(oh[:, :, :], iota[:, :, :], rank[:, u % 2, :].unsqueeze(2).to_broadcast([P, GT, 15]), ALU.is_equal))
                        probabilities(7)
                        own.need(n)
                        own.link(V.tensor_tensor(pick[:, :, :], oh[:, :, :], sixteen[:, :, 0:15], ALU.mult))
                        n = own.mark(V.tensor_reduce(mid[:, z1, :], pick[:, :, :], AX, ALU.add))
                        own.mark(V.tensor_tensor(fine[:, z1, :], sixteen[:, :, 0], upper_t[:, u % 2, :], ALU.is_lt))
                        own.need(n)
                        own.link(V.tensor_tensor(pick[:, :, :], oh[:, :, :], sixteen[:, :, 1:16], ALU.mult))
                        own.link(V.tensor_reduce(nxt[:, :], pick[:, :, :], AX, ALU.add))
                        own.link(V.tensor_tensor(nxt[:, :], nxt[:, :], mid[:, z1, :], ALU.is_lt))
                        own.link(V.scalar_tensor_tensor(tmp[:, :], mid[:, z1, :], 0.0, nxt[:, :], ALU.is_gt, ALU.mult))
                        own.link(V.tensor_tensor(fine[:, z1, :], fine[:, z1, :], tmp[:, :], ALU.mult))
                    else:
                        probabilities(7)
                    if u == 3:
                        dve.sem_inc(s["gate"], 1)
                        own.end()

                def redo(dve, V, z):
                    slow = Own(dve, s["slow"])
                    any_failed = dve.value_load(flags[0:1, GT:GT + 1], min_val=0, max_val=P)
                    with dve.If(any_failed > 0):
                        for c in range(GT):
                            failed = dve.value_load(flags[0:1, c:c + 1], min_val=0, max_val=P)
                            with dve.If(failed > 0):
                                slow.n = 0
                                src = kept[:, z, c, :]
                                w = work[:, 0, :]
                                for r in range(TOPK // 8 + 1):
                                    slow.link(V.max(mx[:, 0, :], src if r == 0 else w))
                                    if r == TOPK // 8:
                                        slow.link(V.memset(mx[:, 0, TOPK % 8:8], GONE))
                                    slow.link(V.match_replace(w, mx[:, 0, :], src if r == 0 else w, GONE))
                                slow.link(V.tensor_scalar(w, w, GONE_BELOW, -1.0e30, ALU.is_gt, ALU.mult))
                                slow.link(V.tensor_tensor(src, src, w, ALU.add))
                                slow.link(V.memset(mid[:, z, c:c + 1], -1.0e29))
                                dve.sem_clear(s["slow"])

                schedule(dve, step)

        actx.close()

        NBUF = 4
        th = sb("th", [P, 3, T])
        g_s = sb("g_s", [P, 3, T])
        g_m = sb("g_m", [P, NBUF + 1, T])
        hid = sb("hid", [P, NBUF, T])
        cbs = sb("cbs", [P, NBUF, 2 * T])
        xTf = sb("xTf", [P, 2, T])
        combT = sb("combT", [3 * NE, 2, T], bf16)
        pieces = sb("pieces", [P, HALVES, 3, NE], bf16)
        remains = sb("remains", [P, HALVES, NE])
        sg = sb("sg", [P, HALVES, NE])
        sc_ = sb("sc_", [P, HALVES, NE])
        hi = sb("hi", [P, HALVES * NG, 2])
        lo = sb("lo", [P, HALVES * NG, 2])
        m1 = sb("m1", [P, HALVES * NG])
        m2 = sb("m2", [P, HALVES * NG])
        m3 = sb("m3", [P, HALVES * NG])
        gsc = sb("gsc", [P, HALVES, 2 * NG])
        g8 = sb("g8", [P, HALVES, 8])
        gr = sb("gr", [P, HALVES, 2 * NG])
        gm = sb("gm", [P, HALVES, NG])
        comb = sb("comb", [P, HALVES, NE])
        wsum = sb("wsum", [P, HALVES])

        def xrow(b, h):
            if isinstance(b, int):
                return xres[:, b * HALVES + h, :]
            return xres[:, bass.ds(b * HALVES + h, 1), :].rearrange("p a d -> p (a d)")

        def wait(eng, sm, v):
            if not (isinstance(v, int) and v <= 0):
                eng.wait_ge(sm, v)

        def experts(tag):
            s = sems(tag, "mv rstd xn m mc gu th gm hid lg comb yused own pown gate")
            GU = bank[0:3]
            M = bank[3]
            Y = (bank[4:6], bank[6:8])
            SLOT = {"p1": 0, "p2": 1, "p3": 3, "xT": 4, "p4": 5, "rt": 6, "p5": 7, "p6": 9, "p7": 11, "cT": 15, "p0": 16}
            AHEAD = ("xT", "rt", "cT", "p0")

            def use(b, what):
                order = [w for w in SLOT if not (isinstance(b, int) and b == BATCH - 1 and w in AHEAD)]
                return 4 + len(SLOT) * b + order.index(what)

            def uses(b, e, more):
                return [w for w, at in SLOT.items() if at == e and (more or w not in AHEAD)]

            def all_batches(eng, batch, end):
                batch(0, 0, True)
                end()
                with eng.Fori(0, BATCH // 2 - 1) as i:
                    for v in range(2):
                        batch(i * 2 + (1 + v), (1 + v) % 2, True)
                        end()
                batch(BATCH - 1, 1, False)
                end()

            def products(b, e):
                return NBLK * b + e

            with nc.Block() as block:
                @block.gpsimd
                def _(pool):
                    own = Own(pool, s["pown"])

                    def deviation(b):
                        pool.wait_ge(s["mv"], b + 1)
                        own.link(pool.tensor_tensor(vareps[:, :], mv[:, :, 1], eps_t[:, :], ALU.add))
                        pool.tensor_tensor(rstd[:, :], vareps[:, :], half_pow[:, :], ALU.pow).then_inc(s["rstd"], 1)

                    deviation(0)
                    own.end()

                    def batch(b, par, more):
                        for e in range(EB):
                            pool.wait_ge(s["mc"], 4 + len(SLOT) * b if e < 2 else use(b, f"p{e // 2}") + 1)
                            wait(pool, s["lg"], NBLK * b + e - 3 if e >= NBUF else NBLK * b + e - 4)
                            pool.wait_ge(s["gm"], products(b, e) + 1)
                            pool.tensor_tensor(hid[:, e % NBUF, :], g_m[:, e % NBUF, :],
                                               cbs[:, e // 2 % NBUF, e % 2 * T:(e % 2 + 1) * T], ALU.mult).then_inc(s["hid"], 1)
                            if e == 1 and more:
                                deviation(b + 1)

                    all_batches(pool, batch, own.end)

                @block.tensor
                def _(pe):
                    def up(b, e, par):
                        wait(pe, s["gm"], products(b, e) - 2 if e >= 2 else products(b, e) - 1)
                        g = GU[e % 3]
                        nc.tensor.matmul(g[:, 0:T], wgT[:, e, :], xTf[:, par, :], start=True, stop=True)
                        nc.tensor.matmul(g[:, T:2 * T], wuT[:, e, :], xTf[:, par, :], start=True, stop=True).then_inc(s["gu"], 1)

                    def turn_x(b, n):
                        pe.wait_ge(s["xn"], b + 1)
                        wait(pe, s["mc"], n)
                        for h in range(HALVES):
                            last = nc.tensor.transpose(M[:, h * P:(h + 1) * P], xn[:, h, :], ident[:, :])
                        last.then_inc(s["m"], 1)

                    def router(par, n):
                        pe.wait_ge(s["mc"], n)
                        for h in range(HALVES):
                            last = nc.tensor.matmul(M[:, h * NE:(h + 1) * NE], xTf[:, par, h * P:(h + 1) * P], gwT[:, :], start=True, stop=True)
                        last.then_inc(s["m"], 1)

                    def turn_shares(b, n):
                        pe.wait_ge(s["comb"], b + 1)
                        pe.wait_ge(s["mc"], n)
                        for h in range(HALVES):
                            last = nc.tensor.matmul(M[0:3 * NE, h * P:(h + 1) * P], pieces[:, h, :, :].rearrange("p k e -> p (k e)"), ident16[:, :],
                                                    start=True, stop=True)
                        last.then_inc(s["m"], 1)

                    def spread(par, k, n):
                        pe.wait_ge(s["mc"], n)
                        for i in range(2):
                            last = nc.tensor.matmul(M[:, i * T:(i + 1) * T], sel[:, 2 * k + i, :], combT[:, par, :], start=True, stop=True)
                        last.then_inc(s["m"], 1)

                    def down(b, e, par):
                        if e == 0:
                            wait(pe, s["yused"], b - 1)
                        if e < EB:
                            pe.wait_ge(s["hid"], EB * b + e + 1)
                        else:
                            pe.wait_ge(s["gm"], products(b, e) + 1)
                        src = hid[:, e % NBUF, :] if e < EB else g_m[:, NBUF, :]
                        for h in range(HALVES):
                            last = nc.tensor.matmul(Y[par][h][:, 0:D], src[:, h * P:(h + 1) * P], wdT[:, e, :],
                                                    start=(e == 0), stop=(e == NBLK - 1))
                        last.then_inc(s["lg"], 1)

                    turn_x(0, 0)
                    router(0, 1)
                    up(0, 0, 0)
                    up(0, 1, 0)
                    turn_shares(0, 2)
                    spread(0, 0, 3)

                    def batch(b, par, more):
                        nxt = 1 - par
                        for e in range(NBLK):
                            if e == SLOT["cT"] and more:
                                turn_shares(b + 1, use(b, "cT"))
                            if e + 2 < NBLK:
                                up(b, e + 2, par)
                            elif more:
                                up(b + 1, e + 2 - NBLK, nxt)
                            for w in uses(b, e, more):
                                n = use(b, w)
                                if w == "xT":
                                    turn_x(b + 1, n)
                                elif w == "rt":
                                    router(nxt, n)
                                elif w == "p0":
                                    spread(nxt, 0, n)
                                elif w != "cT":
                                    spread(par, int(w[1]), n)
                            if e >= 1:
                                down(b, e - 1, par)
                            elif not (isinstance(b, int) and b == 0):
                                down(b - 1, NBLK - 1, nxt)
                        if not more:
                            down(b, NBLK - 1, par)

                    all_batches(pe, batch, lambda: None)

                @block.scalar
                def _(act):
                    def tanh(b, e):
                        act.wait_ge(s["gu"], products(b, e) + 1)
                        nc.scalar.activation(th[:, e % 3, :], GU[e % 3][:, 0:T], ACT.Tanh, scale=0.5).then_inc(s["th"], 1)

                    def take(b, par, w, n):
                        act.wait_ge(s["m"], n + 1)
                        if w == "xT":
                            i = nc.scalar.copy(xTf[:, par, :], M[:, 0:T])
                        elif w == "rt":
                            i = nc.scalar.activation(sg[:, :, :].rearrange("p h e -> p (h e)"), M[:, 0:HALVES * NE], ACT.Tanh, scale=0.5)
                        elif w == "cT":
                            i = nc.scalar.copy(combT[:, par, :], M[0:3 * NE, 0:T])
                        else:
                            k = int(w[1])
                            wait(act, s["hid"], EB * b + 2 * k - 6)
                            i = nc.scalar.copy(cbs[:, k % NBUF, :], M[:, :])
                        i.then_inc(s["mc"], 1)

                    take(0, 0, "xT", 0)
                    take(0, 0, "rt", 1)
                    tanh(0, 0)
                    tanh(0, 1)
                    take(0, 0, "cT", 2)
                    take(0, 0, "p0", 3)

                    def batch(b, par, more):
                        for e in range(NBLK):
                            if e == SLOT["cT"] and more:
                                take(b + 1, 1 - par, "cT", use(b, "cT"))
                            if e + 2 < NBLK:
                                tanh(b, e + 2)
                            elif more:
                                tanh(b + 1, e + 2 - NBLK)
                            for w in uses(b, e, more):
                                if w in AHEAD:
                                    if w != "cT":
                                        take(b + 1, 1 - par, w, use(b, w))
                                else:
                                    take(b, par, w, use(b, w))

                    all_batches(act, batch, lambda: None)

                @block.vector
                def _(dve):
                    own = Own(dve, s["own"])
                    V = nc.vector
                    V.memset(gsc[:, :, :], GONE)

                    def statistics(b):
                        dve.sem_inc(s["gate"], 1)
                        for h in range(HALVES):
                            n = own.mark(V.bn_stats(stats[:, h, :], xrow(b, h)))
                        own.need(n)
                        for h in range(HALVES):
                            n = V.bn_aggr(mv[:, h, :], stats[:, h, :])
                        n.then_inc(s["mv"], 1)

                    def normed(b):
                        dve.wait_ge(s["rstd"], b + 1)
                        for h in range(HALVES):
                            n = V.tensor_scalar(xn[:, h, :], xrow(b, h), mv[:, h, 0:1], rstd[:, h:h + 1], ALU.subtract, ALU.mult)
                        n.then_inc(s["xn"], 1)

                    def router(b, n_rt):
                        q = sc_[:, :, :].rearrange("p h (g k two) -> p (h g) k two", k=2, two=2)
                        by_group = sc_[:, :, :].rearrange("p h (g k) -> p h g k", k=GSZ)

                        def sigmoid():
                            dve.wait_ge(s["mc"], n_rt + 1)
                            return [V.tensor_scalar(sg[:, :, :], sg[:, :, :], 0.5, 0.5, ALU.mult, ALU.add)]

                        def share(h):
                            return V.scalar_tensor_tensor(comb[:, h, :], comb[:, h, :], GONE_BELOW, sg[:, h, :], ALU.is_le, ALU.mult,
                                                          accum_out=wsum[:, h:h + 1])

                        H2 = range(HALVES)
                        return [
                            sigmoid,
                            lambda: [V.tensor_tensor(sc_[:, :, :], sg[:, :, :], gbias[:, :].unsqueeze(1).to_broadcast([P, HALVES, NE]), ALU.add)],
                            lambda: [V.tensor_tensor(hi[:, :, :], q[:, :, :, 0], q[:, :, :, 1], ALU.max),
                                     V.tensor_tensor(lo[:, :, :], q[:, :, :, 0], q[:, :, :, 1], ALU.min)],
                            lambda: [V.tensor_tensor(m1[:, :], hi[:, :, 0], hi[:, :, 1], ALU.max),
                                     V.tensor_tensor(m2[:, :], hi[:, :, 0], hi[:, :, 1], ALU.min),
                                     V.tensor_tensor(m3[:, :], lo[:, :, 0], lo[:, :, 1], ALU.max)],
                            lambda: [V.tensor_tensor(m2[:, :], m2[:, :], m3[:, :], ALU.max)],
                            lambda: [V.tensor_tensor(gsc[:, :, 0:NG], m1[:, :].rearrange("p (h g) -> p h g", h=HALVES),
                                                     m2[:, :].rearrange("p (h g) -> p h g", h=HALVES), ALU.add)],
                            lambda: [V.max(g8[:, h, :], gsc[:, h, :]) for h in H2],
                            lambda: [V.memset(g8[:, :, 4:8], GONE)],
                            lambda: [V.match_replace(gr[:, h, :], g8[:, h, :], gsc[:, h, :], GONE) for h in H2],
                            lambda: [V.tensor_scalar(gm[:, :, :], gr[:, :, 0:NG], GONE_BELOW, None, ALU.is_le)],
                            lambda: [V.tensor_tensor(by_group, by_group, gm[:, :, :].unsqueeze(3).to_broadcast([P, HALVES, NG, GSZ]), ALU.mult)],
                            lambda: [V.tensor_scalar(sc_[:, :, :], sc_[:, :, :], 0.0, None, ALU.add)],
                            lambda: [V.max(g8[:, h, :], sc_[:, h, :]) for h in H2],
                            lambda: [V.match_replace(comb[:, h, :], g8[:, h, :], sc_[:, h, :], GONE) for h in H2],
                            lambda: [share(h) for h in H2],
                            lambda: [V.tensor_scalar(wsum[:, :], wsum[:, :], 1e-20, None, ALU.add)],
                            lambda: [V.reciprocal(wsum[:, :], wsum[:, :])],
                            lambda: [V.tensor_scalar(comb[:, h, :], comb[:, h, :], wsum[:, h:h + 1], 0.5 * ROUTED_SCALE, ALU.mult, ALU.mult) for h in H2],
                            lambda: [V.tensor_copy(pieces[:, :, 0, :], comb[:, :, :])],
                            lambda: [V.tensor_tensor(remains[:, :, :], comb[:, :, :], pieces[:, :, 0, :], ALU.subtract)],
                            lambda: [V.tensor_copy(pieces[:, :, 1, :], remains[:, :, :])],
                            lambda: [V.tensor_tensor(pieces[:, :, 2, :], remains[:, :, :], pieces[:, :, 1, :], ALU.subtract)],
                        ]

                    def run(f):
                        if own.n:
                            own.need(own.n)
                        for i in f():
                            own.mark(i)

                    def done():
                        own.need(own.n)
                        dve.sem_inc(s["comb"], 1)

                    statistics(0)
                    normed(0)
                    for f in router(0, 1):
                        run(f)
                    done()
                    own.end()
                    FIRST, EACH = 8, 4

                    def add_y(b, par):
                        dve.wait_ge(s["lg"], NBLK * (b + 1))
                        for h in range(HALVES):
                            n = V.tensor_tensor(xrow(b, h), xrow(b, h), Y[par][h][:, 0:D], ALU.add)
                        n.then_inc(s["yused"], 1)

                    def batch(b, par, more):
                        steps = router(b + 1, use(b, "rt")) if more else []
                        at = 0
                        for e in range(NBLK):
                            def some(k):
                                nonlocal at
                                if e >= FIRST:
                                    for _ in range(k):
                                        if at < len(steps):
                                            run(steps[at])
                                            at += 1
                            some(1)
                            g = GU[e % 3]
                            dve.wait_ge(s["th"], products(b, e) + 1)
                            wait(dve, s["gm"], products(b, e) - 1)
                            n = own.mark(V.scalar_tensor_tensor(g_s[:, e % 3, :], th[:, e % 3, :], 1.0, g[:, 0:T], ALU.add, ALU.mult))
                            some(1)
                            own.need(n)
                            if e < EB:
                                wait(dve, s["hid"], EB * b + e - 3)
                            else:
                                wait(dve, s["lg"], NBLK * b)
                            V.tensor_tensor(g_m[:, e % NBUF if e < EB else NBUF, :], g_s[:, e % 3, :], g[:, T:2 * T], ALU.mult).then_inc(s["gm"], 1)
                            some(EACH - 2)
                            if more and e == 0:
                                statistics(b + 1)
                            if more and e == 3:
                                normed(b + 1)
                            if at == len(steps) and at:
                                done()
                                steps, at = [], 0
                            if e == 2 and not (isinstance(b, int) and b == 0):
                                add_y(b - 1, 1 - par)

                    all_batches(dve, batch, own.end)
                    add_y(BATCH - 1, 1)
                    dve.wait_ge(s["yused"], BATCH)

        experts("f1")

        bctx = ctx.enter_context(ExitStack())

        def sb_b(name, shape):
            return bctx.enter_context(nc.sbuf_tensor(name, shape, f32))

        wqrep = sb_b("wqrep", [P, H, P])
        vaug = sb_b("vaug", [P, 2, HALVES, H, VW])
        q1 = sb_b("q1", [P, 2, A, HG, J])
        q2 = sb_b("q2", [P, A, H, J])
        xTb = sb_b("xTb", [P, T])
        qTb = sb_b("qTb", [P, T])
        kTb = sb_b("kTb", [P, 2, T])
        pTb = sb_b("pTb", [P, 2, HALVES, HG, P])
        mxb = sb_b("mxb", [P, 2, HALVES])
        s = sems("b", "mv rstd xn m0 m0c m1 m1c q1 scores smax nmax exp pused pt pv on yused ini own pown gate")
        PAIRS = H
        S = bank[0:2]
        PT = bank[2:4]
        O = bank[4]
        M0, M1 = bank[5], bank[6]
        o_all = O[:, 0:HALVES * H * VW].rearrange("p (n w) -> p n w", w=VW)
        SLOT0 = {"xT'": 5, "qk'": 6, "oT": 6, "v'": 7}
        SLOT1 = {"r5": 0, "r6": 2, "r7": 4, "y": 7, "r0'": 8, "r1'": 9, "r2'": 10, "r3'": 12, "r4'": 14}
        FIRST0, FIRST1 = 3, 5

        def use(slots, first, b, what):
            static = isinstance(b, int)
            order = [w for w in slots if not (static and (b == 0 and w in ("oT", "y") or b == BATCH - 1 and w[-1] == "'"))]
            return first + len(slots) * b - (0 if static and b == 0 else 1) + order.index(what)

        def batches(eng, batch, end):
            batch(0, 0, False, True)
            end()
            with eng.Fori(0, BATCH // 2 - 1) as i:
                for v in range(2):
                    batch(i * 2 + (1 + v), (1 + v) % 2, True, True)
                    end()
            batch(BATCH - 1, 1, True, False)
            end()

        LAST0 = use(SLOT0, FIRST0, BATCH - 1, "oT") + 1
        LAST1 = use(SLOT1, FIRST1, BATCH - 1, "y") + 1

        with nc.Block() as block:
            @block.gpsimd
            def _(pool):
                own = Own(pool, s["pown"])

                def deviation(b):
                    pool.wait_ge(s["mv"], b + 1)
                    own.link(pool.tensor_tensor(vareps[:, :], mv[:, :, 1], eps_t[:, :], ALU.add))
                    pool.tensor_tensor(rstd[:, :], vareps[:, :], half_pow[:, :], ALU.pow).then_inc(s["rstd"], 1)
                    own.end()

                deviation(0)
                with pool.Fori(0, BATCH - 1) as b:
                    deviation(b + 1)

            @block.tensor
            def _(pe):
                def turn_x(b, n):
                    pe.wait_ge(s["xn"], b + 1)
                    wait(pe, s["m0c"], n)
                    for h in range(HALVES):
                        last = nc.tensor.transpose(M0[:, h * P:(h + 1) * P], xn[:, h, :], ident[:, :])
                    last.then_inc(s["m0"], 1)

                def project(n):
                    wait(pe, s["m0c"], n)
                    nc.tensor.matmul(M0[:, 0:T], wqT[:, :], xTb[:, :], start=True, stop=True)
                    nc.tensor.matmul(M0[:, T:2 * T], wkT[:, :], xTb[:, :], start=True, stop=True).then_inc(s["m0"], 1)

                def values(n):
                    wait(pe, s["m0c"], n)
                    for h in range(HALVES):
                        last = nc.tensor.matmul(M0[:, h * P:(h + 1) * P], xTb[:, h * P:(h + 1) * P], wvbT[:, :], start=True, stop=True)
                    last.then_inc(s["m0"], 1)

                def repeat(r, n):
                    wait(pe, s["m1c"], n)
                    for i in range(2):
                        last = nc.tensor.matmul(M1[:, i * T:(i + 1) * T], wqrep[:, 2 * r + i, :], xTb[:, :], start=True, stop=True)
                    last.then_inc(s["m1"], 1)

                def scores(b, u, par):
                    wait(pe, s["exp"], PAIRS * b + u - 1)
                    hg = u // 8
                    for i in range(2):
                        a = 8 * ((u // 4) % 2) + 2 * (u % 4) + i
                        o = S[u % 2][:, i * T:(i + 1) * T]
                        r = slice(64 * hg, 64 * hg + 64)
                        nc.tensor.matmul(o, q1[r, par, a, :, :], kTb[r, par, :], start=True, stop=False)
                        last = nc.tensor.matmul(o, q2[:, a, hg * HG:(hg + 1) * HG, :], px[:, (A - 1 - a) * J:(A - 1 - a) * J + T],
                                                start=False, stop=True)
                    last.then_inc(s["scores"], 1)

                def turn(b, u):
                    pe.wait_ge(s["exp"], PAIRS * b + u + 1)
                    wait(pe, s["pt"], PAIRS * b + u - 1)
                    for t in range(HALVES):
                        for i in range(2):
                            o = PT[u % 2][:, t * T:(t + 1) * T].rearrange("p (h i j) -> p h i j", h=HG, i=2)[:, :, i, :]
                            last = nc.tensor.transpose(o, prob[:, u % 2, i, t * P:(t + 1) * P], ident[:, :])
                    last.then_inc(s["pused"], 1)

                def weigh(b, par, g, j):
                    if j == 0:
                        pe.wait_ge(s["pt"], PAIRS * b + 4 * g + 4)
                    if g == 0 and j == 0:
                        wait(pe, s["on"], b)
                    hg, i = g // 2, g % 2
                    for h in (2 * j, 2 * j + 1):
                        for t in range(HALVES):
                            o = (i * H + hg * HG + h) * VW
                            last = nc.tensor.matmul(O[:, o:o + VW], pTb[:, g % 2, t, h, :], vaug[:, par, t, hg * HG + h, :],
                                                    start=(t == 0), stop=(t == HALVES - 1))
                    if j == 3:
                        last.then_inc(s["pv"], 1)

                def turn_o(b, n):
                    pe.wait_ge(s["on"], b + 1)
                    wait(pe, s["m0c"], n)
                    for i in range(HALVES):
                        last = nc.tensor.transpose(M0[:, i * P:(i + 1) * P], onrm[:, i, :], ident[:, :])
                    last.then_inc(s["m0"], 1)

                def project_o(n0, n1):
                    pe.wait_ge(s["m0c"], n0)
                    wait(pe, s["m1c"], n1)
                    for i in range(HALVES):
                        last = nc.tensor.matmul(M1[:, i * P:(i + 1) * P], oT[:, i * P:(i + 1) * P], wpT[:, :], start=True, stop=True)
                    last.then_inc(s["m1"], 1)

                turn_x(0, 0)
                project(1)
                values(2)
                pe.wait_ge(s["ini"], 2)
                for r in range(5):
                    repeat(r, r)
                pe.wait_ge(s["m1c"], 4)
                pe.wait_ge(s["q1"], 1)
                pe.wait_ge(s["m0c"], 3)
                scores(0, 0, 0)
                scores(0, 1, 0)

                def batch(b, par, prev, more):
                    for u in range(PAIRS):
                        g, j = (u - 5) // 4, (u - 5) % 4
                        if u >= 5:
                            weigh(b, par, g, j)
                        elif prev:
                            weigh(b - 1, 1 - par, *((2, 3) if u == 0 else (3, u - 1)))
                        for w in [w for w, at in SLOT0.items() if at == u]:
                            if w == "oT" and prev:
                                turn_o(b - 1, use(SLOT0, FIRST0, b, w))
                            elif w[-1] == "'" and more:
                                n = use(SLOT0, FIRST0, b, w)
                                {"xT'": lambda: turn_x(b + 1, n), "qk'": lambda: project(n), "v'": lambda: values(n)}[w]()
                        for w in [w for w, at in SLOT1.items() if at == u]:
                            if w == "y":
                                if prev:
                                    project_o(use(SLOT0, FIRST0, b, "oT") + 1, use(SLOT1, FIRST1, b, w))
                            elif more or w[-1] != "'":
                                repeat(int(w[1]), use(SLOT1, FIRST1, b, w))
                        turn(b, u)
                        if u == PAIRS // 2 - 2:
                            pe.wait_ge(s["m1c"], use(SLOT1, FIRST1, b, "r7") + 1)
                        if u == PAIRS - 2 and more:
                            pe.wait_ge(s["m1c"], use(SLOT1, FIRST1, b, "r3'") + 1)
                            pe.wait_ge(s["q1"], b + 2)
                            pe.wait_ge(s["m0c"], use(SLOT0, FIRST0, b, "v'") + 1)
                        if u + 2 < PAIRS:
                            scores(b, u + 2, par)
                        elif more:
                            scores(b + 1, u + 2 - PAIRS, 1 - par)

                batches(pe, batch, lambda: None)
                for g, j in ((2, 3), (3, 0), (3, 1), (3, 2), (3, 3)):
                    weigh(BATCH - 1, 1, g, j)
                turn_o(BATCH - 1, LAST0)
                project_o(LAST0 + 1, LAST1)

            @block.scalar
            def _(act):
                def take(par, w, n):
                    act.wait_ge(s["m0"], n + 1)
                    if w == "xT'":
                        i = nc.scalar.copy(xTb[:, :], M0[:, 0:T])
                    elif w == "qk'":
                        nc.scalar.copy(kTb[:, par, :], M0[:, T:2 * T])
                        i = nc.scalar.copy(qTb[:, :], M0[:, 0:T])
                    elif w == "v'":
                        i = nc.scalar.copy(vaug[:, par, :, :, 0:HD].rearrange("p t h d -> p (t h) d"),
                                           M0[:, 0:T].rearrange("p (n d) -> p n d", d=HD))
                    else:
                        i = nc.scalar.copy(oT[:, :], M0[:, 0:T])
                    i.then_inc(s["m0c"], 1)

                act.wait_ge(s["ini"], 1)
                take(0, "xT'", 0)
                take(0, "qk'", 1)
                take(0, "v'", 2)

                def batch(b, par, prev, more):
                    for u in range(PAIRS):
                        act.wait_ge(s["nmax"], PAIRS * b + u + 1)
                        wait(act, s["pused"], PAIRS * b + u - 1)
                        for i in range(2):
                            last = nc.scalar.activation(prob[:, u % 2, i, :], S[u % 2][:, i * T:(i + 1) * T], ACT.Exp,
                                                        bias=nb[:, u % 2, i:i + 1], scale=SCALE_B)
                        last.then_inc(s["exp"], 1)
                        for w in [w for w, at in SLOT0.items() if at == u]:
                            if prev if w == "oT" else more:
                                take(1 - par, w, use(SLOT0, FIRST0, b, w))

                batches(act, batch, lambda: None)
                take(0, "oT", LAST0)

            @block.vector
            def _(dve):
                own = Own(dve, s["own"])
                V = nc.vector
                V.memset(vaug[:, :, :, :, :], 1.0).then_inc(s["ini"], 1)
                V.tensor_copy(wqrep[:, :, :].rearrange("p h (j d) -> p h j d", d=HD),
                              wqT[:, :].rearrange("p (h d) -> p h d", d=HD).unsqueeze(2).to_broadcast([P, H, J, HD])).then_inc(s["ini"], 1)

                def statistics(b):
                    dve.sem_inc(s["gate"], 1)
                    for h in range(HALVES):
                        n = own.mark(V.bn_stats(stats[:, h, :], xrow(b, h)))
                    own.need(n)
                    for h in range(HALVES):
                        n = V.bn_aggr(mv[:, h, :], stats[:, h, :])
                    n.then_inc(s["mv"], 1)

                def normed(b):
                    dve.wait_ge(s["rstd"], b + 1)
                    for h in range(HALVES):
                        n = V.tensor_scalar(xn[:, h, :], xrow(b, h), mv[:, h, 0:1], rstd[:, h:h + 1], ALU.subtract, ALU.mult)
                    n.then_inc(s["xn"], 1)

                def mask(r, n):
                    dve.wait_ge(s["m1"], n + 1)
                    V.tensor_tensor(q2[:, :, 2 * r:2 * r + 2, :].rearrange("p a h j -> p h a j"),
                                    M1[:, :].rearrange("p (h a j) -> p h a j", h=2, a=A),
                                    mask_h16[:, :].unsqueeze(1).unsqueeze(1).to_broadcast([P, 2, A, J]), ALU.mult).then_inc(s["m1c"], 1)

                def by_head(par, n):
                    dve.wait_ge(s["m0c"], n + 1)
                    V.tensor_tensor(q1[:, par, :, :, :], qTb[:, :].rearrange("p (a j) -> p a j", j=J).unsqueeze(2).to_broadcast([P, A, HG, J]),
                                    mask_h8[:, :].unsqueeze(1).unsqueeze(3).to_broadcast([P, A, HG, J]), ALU.mult).then_inc(s["q1"], 1)

                def copy_pt(b, u, g, v):
                    dve.wait_ge(s["pused"], PAIRS * b + u + 1)
                    if v == 0:
                        wait(dve, s["pv"], 4 * b + g - 1)
                    V.tensor_copy(pTb[:, g % 2, :, :, 2 * J * v:2 * J * (v + 1)],
                                  PT[u % 2][:, :].rearrange("p (t h r) -> p t h r", t=2, h=HG)).then_inc(s["pt"], 1)

                def normalise(b):
                    dve.wait_ge(s["pv"], 4 * b + 4)
                    own.link(V.reciprocal(rinv[:, :], o_all[:, :, HD]))
                    V.tensor_tensor(onrm[:, :, :].rearrange("p i (h d) -> p (i h) d", d=HD), o_all[:, :, 0:HD],
                                    rinv[:, :].unsqueeze(2).to_broadcast([P, HALVES * H, HD]), ALU.mult).then_inc(s["on"], 1)

                def add_y(b, n):
                    dve.wait_ge(s["m1"], n + 1)
                    for h in range(HALVES):
                        i = V.tensor_tensor(xrow(b, h), xrow(b, h), M1[:, h * P:(h + 1) * P], ALU.add)
                    i.then_inc(s["m1c"], 1)

                statistics(0)
                normed(0)
                by_head(0, 1)
                for r in range(5):
                    mask(r, r)
                own.end()

                def batch(b, par, prev, more):
                    for u in range(PAIRS):
                        dve.wait_ge(s["scores"], PAIRS * b + u + 1)
                        V.tensor_reduce(mxb[:, u % 2, :], S[u % 2][:, :].rearrange("p (i t) -> p i t", i=2), AX, ALU.max).then_inc(s["smax"], 1)
                        dve.wait_ge(s["smax"], PAIRS * b + u + 1)
                        V.tensor_scalar(nb[:, u % 2, :], mxb[:, u % 2, :], -SCALE_B, None, ALU.mult).then_inc(s["nmax"], 1)
                        if u >= 1:
                            copy_pt(b, u - 1, (u - 1) // 4, (u - 1) % 4)
                        elif prev:
                            copy_pt(b - 1, PAIRS - 1, 3, 3)
                        if u == 0 and more:
                            statistics(b + 1)
                        if u == 2 and more:
                            normed(b + 1)
                        if u == 5 and prev:
                            normalise(b - 1)
                        if u == 7 and more:
                            by_head(1 - par, use(SLOT0, FIRST0, b, "qk'"))
                        for w in [w for w, at in SLOT1.items() if at == u]:
                            if w == "y":
                                if prev:
                                    add_y(b - 1, use(SLOT1, FIRST1, b, w))
                            elif more or w[-1] != "'":
                                mask(int(w[1]), use(SLOT1, FIRST1, b, w))

                batches(dve, batch, own.end)
                copy_pt(BATCH - 1, PAIRS - 1, 3, 3)
                normalise(BATCH - 1)
                add_y(BATCH - 1, LAST1)
                dve.wait_ge(s["m1c"], LAST1 + 1)
                own.end()

        bctx.close()

        experts("f2")

        s_out = sem("s_out")
        with nc.Block() as block:
            @block.sync
            def _(sp):
                for c in range(4):
                    n = BATCH * HALVES // 4
                    sp.dma_start(out_dram[:, c * n:(c + 1) * n, :], xres[:, c * n:(c + 1) * n, :]).then_inc(s_out, 16)
                sp.wait_ge(s_out, 16 * 4)


_INS = ['L0_attn_a_x', 'L0_attn_a_W_qkv', 'L0_attn_a_b_qkv', 'L0_attn_a_W_out', 'L0_attn_a_b_out',
        'L0_attn_b_Wq', 'L0_attn_b_Wk', 'L0_attn_b_Wv', 'L0_attn_b_Wp', 'L0_attn_b_pos_emb_k',
        'L0_ffn_gate_w', 'L0_ffn_gate_bias', 'L0_ffn_w_gate', 'L0_ffn_w_up', 'L0_ffn_w_down',
        'L0_ffn_sh_gate', 'L0_ffn_sh_up', 'L0_ffn_sh_down']


def kernel(**inputs):
    import numpy as _np
    import concourse.bacc as _bacc
    from concourse import mybir as _mybir
    from concourse.bass_utils import run_bass_kernel_spmd as _run

    nc = _bacc.Bacc("TRN2", target_bir_lowering=False, num_devices=1)
    arrays, args = {}, []
    for name in _INS:
        a = _np.ascontiguousarray(inputs[name])
        arrays[f"in_{name}_dram"] = a
        args.append(nc.dram_tensor(f"in_{name}_dram", a.shape, _mybir.dt.from_np(a.dtype), kind="ExternalInput").ap())
    args.append(nc.dram_tensor("out_0_dram", (BATCH, T, D), _mybir.dt.float32, kind="ExternalOutput").ap())
    build(nc, *args)
    r = _run(nc, [arrays], core_ids=[0])
    return r.results[0]["out_0_dram"]
```
